# Optimizing a Trainium2 kernel written in Bass

```python
import numpy as np
import jax
import jax.numpy as jnp

def _softmax(x, axis=-1):
    return jax.nn.softmax(x, axis=axis)

def _gelu(x):
    return jax.nn.gelu(x, approximate=True)

def _silu(x):
    return jax.nn.silu(x)

def _sigmoid(x):
    return jax.nn.sigmoid(x)

def _layernorm(x, axis=-1, eps=1e-05):
    m = jnp.mean(x, axis=axis, keepdims=True)
    v = jnp.var(x, axis=axis, keepdims=True)
    return (x - m) / jnp.sqrt(v + eps)

def _scatter_add(tgt, idx, src, axis=0):
    return tgt.at[idx].add(src)

def _segment_sum(src, seg, n):
    return jax.ops.segment_sum(src, seg, n)
kernel_name = 'mk_recurrent_d1_jaxref_r4_8e75fa'

def setup_inputs(seed: int=0):
    np.random.seed(seed)
    _w = jnp.asarray

    def _L0_attn_setup():
        import jax, jax.numpy as jnp
        import numpy as np
        from math import log, sqrt
        B, S, D, H = (2, 512, 256, 16)
        HD = D // H
        NUM_BUCKETS = 32
        MAX_DISTANCE = 128
        ROPE_BASE = 10000.0

        def _rope_cos_sin(seq_len, dim, base):
            inv_freq = 1.0 / base ** (jnp.arange(0, dim, 2, dtype=jnp.float32) / dim)
            t = jnp.arange(seq_len, dtype=jnp.float32)
            freqs = jnp.outer(t, inv_freq)
            emb = jnp.concatenate([freqs, freqs], axis=-1)
            return (jnp.cos(emb), jnp.sin(emb))

        def _rotate_half(t):
            d = t.shape[-1] // 2
            return jnp.concatenate([-t[..., d:], t[..., :d]], axis=-1)

        def _rel_pos_bucket(relative_position, num_buckets, max_distance):
            rp = -jnp.minimum(relative_position, 0)
            max_exact = num_buckets // 2
            is_small = rp < max_exact
            rp_f = jnp.maximum(rp.astype(jnp.float32), 1.0)
            large = max_exact + (jnp.log(rp_f / max_exact) / log(max_distance / max_exact) * (num_buckets - max_exact)).astype(jnp.int32)
            large = jnp.minimum(large, num_buckets - 1)
            return jnp.where(is_small, rp, large)
        key = jax.random.key(seed)
        kx, kq, kk, kv, ko, kr = jax.random.split(key, 6)
        scale = 0.02
        return {'x': jax.random.normal(kx, (B, S, D), dtype=jnp.float32), 'Wq': jax.random.normal(kq, (D, D), dtype=jnp.float32) * scale, 'Wk': jax.random.normal(kk, (D, D), dtype=jnp.float32) * scale, 'Wv': jax.random.normal(kv, (D, D), dtype=jnp.float32) * scale, 'Wo': jax.random.normal(ko, (D, D), dtype=jnp.float32) * scale, 'rel_emb': jax.random.normal(kr, (NUM_BUCKETS, H), dtype=jnp.float32) * scale}
    _L0_attn_in = _L0_attn_setup()

    def _L0_ffn_setup():
        import jax, jax.numpy as jnp
        import numpy as np
        E = 8
        H = 256
        F = 256
        K = 2
        B, T = (2, 256)
        key = jax.random.key(seed)
        k1, k2, k3, k4 = jax.random.split(key, 4)
        return {'hidden_states': jax.random.normal(k1, (B, T, H), dtype=jnp.float32), 'router_weight': jax.random.normal(k2, (E, H), dtype=jnp.float32), 'gate_up_proj': jax.random.normal(k3, (E, 2 * F, H), dtype=jnp.float32), 'down_proj': jax.random.normal(k4, (E, H, F), dtype=jnp.float32)}
    _L0_ffn_in = _L0_ffn_setup()
    _d = {'L0_attn_x': _L0_attn_in['x'], 'L0_attn_Wq': _L0_attn_in['Wq'], 'L0_attn_Wk': _L0_attn_in['Wk'], 'L0_attn_Wv': _L0_attn_in['Wv'], 'L0_attn_Wo': _L0_attn_in['Wo'], 'L0_attn_rel_emb': _L0_attn_in['rel_emb'], 'L0_ffn_router_weight': _L0_ffn_in['router_weight'], 'L0_ffn_gate_up_proj': _L0_ffn_in['gate_up_proj'], 'L0_ffn_down_proj': _L0_ffn_in['down_proj']}
    _x0 = _d['L0_attn_x']
    _d['L0_attn_x'] = jax.random.normal(jax.random.fold_in(jax.random.key(seed), 1), (8, 1024, 256), dtype=_x0.dtype)
    del _x0
    return _d

def reference(L0_attn_x, L0_attn_Wq, L0_attn_Wk, L0_attn_Wv, L0_attn_Wo, L0_attn_rel_emb, L0_ffn_router_weight, L0_ffn_gate_up_proj, L0_ffn_down_proj):

    def _L0_attn_ref(x, Wq, Wk, Wv, Wo, rel_emb):
        import jax, jax.numpy as jnp
        import numpy as np
        from math import log, sqrt
        B, S, D, H = (2, 512, 256, 16)
        HD = D // H
        NUM_BUCKETS = 32
        MAX_DISTANCE = 128
        ROPE_BASE = 10000.0

        def _rope_cos_sin(seq_len, dim, base):
            inv_freq = 1.0 / base ** (jnp.arange(0, dim, 2, dtype=jnp.float32) / dim)
            t = jnp.arange(seq_len, dtype=jnp.float32)
            freqs = jnp.outer(t, inv_freq)
            emb = jnp.concatenate([freqs, freqs], axis=-1)
            return (jnp.cos(emb), jnp.sin(emb))

        def _rotate_half(t):
            d = t.shape[-1] // 2
            return jnp.concatenate([-t[..., d:], t[..., :d]], axis=-1)

        def _rel_pos_bucket(relative_position, num_buckets, max_distance):
            rp = -jnp.minimum(relative_position, 0)
            max_exact = num_buckets // 2
            is_small = rp < max_exact
            rp_f = jnp.maximum(rp.astype(jnp.float32), 1.0)
            large = max_exact + (jnp.log(rp_f / max_exact) / log(max_distance / max_exact) * (num_buckets - max_exact)).astype(jnp.int32)
            large = jnp.minimum(large, num_buckets - 1)
            return jnp.where(is_small, rp, large)
        b, s, d = x.shape

        def heads_split(t):
            return t.reshape(b, s, H, HD).transpose(0, 2, 1, 3)
        q = heads_split(x @ Wq)
        k = heads_split(x @ Wk)
        v = heads_split(x @ Wv)
        cos, sin = _rope_cos_sin(s, HD, ROPE_BASE)
        q = q * cos + _rotate_half(q) * sin
        k = k * cos + _rotate_half(k) * sin
        pos = jnp.arange(s, dtype=jnp.int32)
        rel = pos[None, :] - pos[:, None]
        buckets = _rel_pos_bucket(rel, NUM_BUCKETS, MAX_DISTANCE)
        bias = rel_emb[buckets].transpose(2, 0, 1)[None]
        scores = jnp.einsum('bhqd,bhkd->bhqk', q, k) / sqrt(HD) + bias
        causal = jnp.tril(jnp.ones((s, s), dtype=bool))
        scores = jnp.where(causal, scores, jnp.float32(-1000000000.0))
        attn = jax.nn.softmax(scores, axis=-1)
        ctx = jnp.einsum('bhqk,bhkd->bhqd', attn, v)
        ctx = ctx.transpose(0, 2, 1, 3).reshape(b, s, d)
        return ctx @ Wo

    def _L0_ffn_ref(hidden_states, router_weight, gate_up_proj, down_proj):
        import jax, jax.numpy as jnp
        import numpy as np
        E = 8
        H = 256
        F = 256
        K = 2
        B, T = (2, 256)
        b, t, h_dim = hidden_states.shape
        h = hidden_states.reshape(-1, h_dim)
        logits = h @ router_weight.T
        probs = jax.nn.softmax(logits, axis=-1)
        top_v, top_i = jax.lax.top_k(probs, K)
        top_v = top_v / top_v.sum(axis=-1, keepdims=True)
        combine = (jax.nn.one_hot(top_i, E, dtype=top_v.dtype) * top_v[..., None]).sum(axis=1)
        combine = combine.T

        def body(acc, xs):
            gu, dp, w = xs
            gate, up = jnp.split(h @ gu.T, 2, axis=-1)
            out = jax.nn.silu(gate) * up @ dp.T
            return (acc + w[:, None] * out, None)
        acc0 = jnp.zeros_like(h)
        final, _ = jax.lax.scan(body, acc0, (gate_up_proj, down_proj, combine))
        return final.reshape(b, t, h_dim)
    x = L0_attn_x
    xn = _layernorm(x, axis=-1)
    s = _L0_attn_ref(xn, L0_attn_Wq, L0_attn_Wk, L0_attn_Wv, L0_attn_Wo, L0_attn_rel_emb)
    g = _silu(_L0_ffn_ref(xn, L0_ffn_router_weight, L0_ffn_gate_up_proj, L0_ffn_down_proj))
    x = x + s * g
    return x

_drawn_inputs = setup_inputs


def setup_inputs(seed=0):
    import zlib

    import numpy as np

    out = dict(_drawn_inputs(seed))
    spreads = {}
    factors = {'L0_attn_rel_emb': 3.414}
    for name, (base, spread) in spreads.items():
        noise = np.random.default_rng([zlib.crc32(name.encode()), seed]).standard_normal(out[name].shape)
        drawn = base * np.exp(spread * noise) if base else spread * noise
        out[name] = jnp.asarray(drawn.astype(out[name].dtype))
    for name, factor in factors.items():
        out[name] = (out[name] * factor).astype(out[name].dtype)
    return out
```

```python
from contextlib import ExitStack

import concourse.bass as bass
from concourse import mybir

F32 = mybir.dt.float32
BF16 = mybir.dt.bfloat16
I32 = mybir.dt.int32
U32 = mybir.dt.uint32
ALU = mybir.AluOpType
ACT = mybir.ActivationFunctionType
AX = mybir.AxisListType

P = 128
B, S, D = 8, 1024, 256
H, HD = 16, 16
G = 4
NG = H // G
T = S // P
NT = B * T
KD = D // P
E, F = 8, 256
NU = B * NG
EPS = 1e-5
BIG = 1.0e30
LOWEST = -3.0e38
NBUCKET = 32
NREL = 2 * P + P

QCAP = B * S
NX = 2 * B * S // P + E
DUMMY = E * QCAP
NROW = DUMMY + E * P

QTERM = (0, 0, 0, 1, 1, 2)
KTERM = (0, 1, 2, 0, 1, 0)
NTERM = len(QTERM)
KROWS = NTERM * HD
MROWS = 3


def phase_a(nc, x, cst, xs, xT_dram, slots_dram, dl_dram, fvec_dram, frow_dram, tab, unused):
    with ExitStack() as ctx:
        def sb(name, shape, dt=F32):
            return ctx.enter_context(nc.sbuf_tensor("a_" + name, shape, dt))

        def sem(name):
            return ctx.enter_context(nc.semaphore("a_" + name))

        ps = ctx.enter_context(nc.psum_tensor("a_ps", [P, 8, 512], F32))
        xb = sb("xb", [P, 2, T, D])
        xn = sb("xn", [P, 2, T, D])
        xT = sb("xT", [P, 2, KD, S])
        wr = sb("wr", [P, KD, E])
        ident = sb("ident", [P, P])
        lowerf = sb("lowerf", [P, P])
        lower = sb("lower", [P, P], BF16)
        ones = sb("ones", [P, P], BF16)
        rev = sb("rev", [P, T, E])
        eoff = sb("eoff", [P, T, E])
        rel = sb("rel", [NBUCKET + 1, H])
        fone = sb("fone", [NBUCKET + 1, 2, NREL])
        fsb = sb("fsb", [H, 2, NREL])
        stats = sb("stats", [P, T, 6])
        mv = sb("mv", [P, T, 2])
        var = sb("var", [P, T])
        sd = sb("sd", [P, T])
        r0 = sb("r0", [P, T])
        r1 = sb("r1", [P, T])
        r2 = sb("r2", [P, T])
        r3 = sb("r3", [P, T])
        rstd = sb("rstd", [P, T])
        lg = sb("lg", [P, T, E])
        lg2 = sb("lg2", [P, T, E])
        top = sb("top", [P, 2, T])
        eq = sb("eq", [P, T, E])
        code = sb("code", [P, T])
        hot = sb("hot", [P, 2, T, E])
        both = sb("both", [P, T, E], BF16)
        acum = sb("acum", [P, T + 1, E], BF16)
        pos = sb("pos", [P, T, E])
        slotf = sb("slotf", [P, 2, T])
        slot = sb("slot", [P, 2, 2 * T], U32)
        dl = sb("dl", [P, 2, T])
        zero = sb("zero", [P, D])
        cnt = sb("cnt", [P, E])
        cnti = sb("cnti", [P, E], I32)
        pcol = sb("pcol", [P, 1])
        padend = sb("padend", [P, E])
        padf = sb("padf", [P, E])
        padg = sb("padg", [P, E])
        padi = sb("padi", [P, E], U32)
        tiles = sb("tiles", [1, E])
        tend = sb("tend", [1, E + 1])
        tnum = sb("tnum", [1, NX])
        tge = sb("tge", [1, NX])
        trow = sb("trow", [1, NX])
        texp = sb("texp", [1, NX])

        x_loaded = [sem(f"x_loaded{n}") for n in range(2)]
        cst_loaded = sem("cst_loaded")
        dve = sem("dve")
        passed = sem("passed")
        ppassed = sem("ppassed")
        var_ready = sem("var_ready")
        sd_ready = sem("sd_ready")
        xn_ready = sem("xn_ready")
        xnT_psum = sem("xnT_psum")
        xT_ready = sem("xT_ready")
        xT_stored = [sem(f"xT_stored{n}") for n in range(2)]
        lg_psum = sem("lg_psum")
        lg_read = sem("lg_read")
        acum_ready = sem("acum_ready")
        pos_psum = sem("pos_psum")
        pos_read = sem("pos_read")
        slot_ready = sem("slot_ready")
        slot_stored = [sem(f"slot_stored{n}") for n in range(2)]
        scattered = [sem(f"scattered{n}") for n in range(2)]
        zero_ready = sem("zero_ready")
        iota_ready = sem("iota_ready")
        cnt_psum = sem("cnt_psum")
        pad_ready = sem("pad_ready")
        pad_done = sem("pad_done")
        f_psum = sem("f_psum")
        f_ready = sem("f_ready")
        f_stored = sem("f_stored")
        dummy_done = sem("dummy_done")

        CST = 16 * 7
        block = ctx.enter_context(nc.Block())

        @block.sync
        def _(sp):
            for dst, name in ((wr, "wr"), (ident, "ident"), (lowerf, "lower"),
                              (rev, "rev"), (eoff, "eoff"), (fone, "fone")):
                sp.dma_start(dst[:], cst[name]).then_inc(cst_loaded, 16)
            sp.dma_start(rel[0:NBUCKET, :], cst["rel"]).then_inc(cst_loaded, 16)

            def load(blk, j):
                sp.dma_start(xb[:, j], x[bass.ds(blk * S, S), :].rearrange("(t p) d -> p t d", p=P)
                             ).then_inc(x_loaded[j], 16)

            def store(blk, j):
                sp.wait_ge(xT_ready, blk * 4 + 4)
                sp.dma_start(xT_dram[bass.ds(blk, 1)].rearrange("o p k s -> (o p) k s"),
                             xT[:, j]).then_inc(xT_stored[j], 16)
                sp.wait_ge(slot_ready, blk + 1)
                sp.dma_start(slots_dram[bass.ds(blk, 1)].rearrange("o p s -> (o p) s"),
                             slot[:, j]).then_inc(slot_stored[j], 16)
                sp.dma_start(dl_dram[bass.ds(blk, 1)].rearrange("o p s -> (o p) s"),
                             dl[:, j]).then_inc(slot_stored[j], 16)

            load(0, 0)
            load(1, 1)
            sp.wait_ge(f_ready, 1)
            sp.dma_start(fvec_dram, fsb[:]).then_inc(f_stored, 16)
            sp.wait_ge(f_stored, 16)
            sp.dma_start(frow_dram, fvec_dram.unsqueeze(1).to_broadcast([H, P, 2, NREL])).then_inc(f_stored, 16)
            sp.wait_ge(zero_ready, 1)
            for e in range(E):
                sp.dma_start(xs[DUMMY + e * P:DUMMY + (e + 1) * P, :], zero[:]).then_inc(dummy_done, 16)
            with sp.Fori(0, B // 2 - 1) as i:
                for j in range(2):
                    blk = i * 2 + j
                    store(blk, j)
                    sp.wait_ge(xn_ready, blk * T + T)
                    load(blk + 2, j)
            for j in range(2):
                store(B - 2 + j, j)
            for j in range(2):
                sp.wait_ge(xT_stored[j], 16 * (B // 2))
                sp.wait_ge(slot_stored[j], 32 * (B // 2))
            sp.wait_ge(f_stored, 32)
            sp.wait_ge(dummy_done, 16 * E)

        @block.gpsimd
        def _(pool):
            nc.gpsimd.memset(zero[:], 0.0).then_inc(zero_ready, 1)
            nc.gpsimd.iota(pcol[:], [[0, 1]], channel_multiplier=1,
                           allow_small_or_imprecise_dtypes=True).then_inc(iota_ready, 1)
            nc.gpsimd.iota(tnum[:], [[1, NX]], channel_multiplier=0,
                           allow_small_or_imprecise_dtypes=True).then_inc(iota_ready, 1)

            def scatter(blk, j):
                pool.wait_ge(xn_ready, blk * T + T)
                pool.wait_ge(slot_ready, blk + 1)
                pool.sem_inc(ppassed, 1)
                for c in range(2):
                    for t in range(T):
                        nc.gpsimd.indirect_dma_start(
                            xs[:, :], bass.IndirectOffsetOnAxis(ap=slot[:, j, c * T + t:c * T + t + 1], axis=0),
                            xn[:, j, t, :], None).then_inc(scattered[j], 16)

            with pool.Fori(0, B // 2) as i:
                for j in range(2):
                    scatter(i * 2 + j, j)
            pool.wait_ge(zero_ready, 1)
            pool.wait_ge(pad_ready, 1)
            for e in range(E):
                nc.gpsimd.indirect_dma_start(
                    xs[:, :], bass.IndirectOffsetOnAxis(ap=padi[:, e:e + 1], axis=0),
                    zero[:], None, bounds_check=NROW - 1, oob_is_err=False).then_inc(pad_done, 16)
            for j in range(2):
                pool.wait_ge(scattered[j], 16 * NT)
            pool.wait_ge(pad_done, 16 * E)

        @block.scalar
        def _(act):
            def block_(i, j):
                blk = i * 2 + j
                act.wait_ge(var_ready, blk + 1)
                nc.scalar.activation(sd[:], var[:], ACT.Sqrt).then_inc(sd_ready, 1)
                if not isinstance(i, int):
                    act.wait_ge(xT_stored[j], i * 16)
                for c in range(4):
                    act.wait_ge(xnT_psum, blk * 4 + c + 1)
                    nc.scalar.copy(xT[:, j, :, c * 256:(c + 1) * 256],
                                   ps[:, c % 2, :].rearrange("p (k s) -> p k s", k=KD)
                                   ).then_inc(xT_ready, 1)

            for j in range(2):
                block_(0, j)
            with act.Fori(1, B // 2) as i:
                for j in range(2):
                    block_(i, j)

        @block.vector
        def _(v):
            n = [0]
            V = nc.vector

            def seq(ins):
                ins.then_inc(dve, 1)
                n[0] += 1
                v.wait_ge(dve, base[0] + n[0])
                return ins

            base = [0]
            seq(V.memset(acum[:], 0.0))
            seq(V.memset(rel[NBUCKET:NBUCKET + 1, :], 1.0))
            v.wait_ge(cst_loaded, CST)
            seq(V.tensor_copy(lower[:], lowerf[:]))
            seq(V.memset(ones[:], 1.0))
            v.wait_ge(f_psum, 1)
            V.tensor_copy(fsb[:], ps[0:H, 4:6, 0:NREL]).then_inc(f_ready, 1)

            def block_(i, j):
                blk = i * 2 + j
                v.wait_ge(x_loaded[j], i * 16 + 16)
                for t in range(T):
                    V.bn_stats(stats[:, t, :], xb[:, j, t, :]).then_inc(dve, 1)
                    n[0] += 1
                v.wait_ge(dve, base[0] + n[0])
                v.sem_inc(passed, 1)
                for t in range(T):
                    V.bn_aggr(mv[:, t, :], stats[:, t, :]).then_inc(dve, 1)
                    n[0] += 1
                v.wait_ge(dve, base[0] + n[0])
                V.tensor_scalar(var[:], mv[:, :, 1], EPS, None, ALU.add).then_inc(var_ready, 1)
                v.wait_ge(var_ready, blk + 1)
                v.wait_ge(sd_ready, blk + 1)
                seq(V.reciprocal(r0[:], sd[:]))
                seq(V.tensor_tensor(r1[:], r0[:], r0[:], ALU.mult))
                seq(V.tensor_tensor(r2[:], r1[:], var[:], ALU.mult))
                seq(V.tensor_scalar(r3[:], r2[:], -0.5, 1.5, ALU.mult, ALU.add))
                seq(V.tensor_tensor(rstd[:], r0[:], r3[:], ALU.mult))
                if not isinstance(i, int):
                    v.wait_ge(scattered[j], i * (16 * 2 * T))
                    v.wait_ge(xnT_psum, blk * 4 - 4)
                for t in range(T):
                    V.tensor_scalar(xn[:, j, t, :], xb[:, j, t, :], mv[:, t, 0:1], rstd[:, t:t + 1],
                                    ALU.subtract, ALU.mult).then_inc(xn_ready, 1)
                v.wait_ge(lg_psum, blk + 1)
                seq(V.tensor_copy(lg[:], ps[:, 2, 0:T * E].rearrange("p (t e) -> p t e", t=T)))
                V.tensor_copy(lg2[:], lg[:]).then_inc(lg_read, 1)
                v.wait_ge(lg_read, blk + 1)
                for c, src in ((0, lg), (1, lg2)):
                    if c == 1:
                        seq(V.scalar_tensor_tensor(out=lg2[:], in0=hot[:, 0], scalar=LOWEST,
                                                   in1=lg[:], op0=ALU.mult, op1=ALU.add))
                    seq(V.tensor_reduce(top[:, c, :], src[:], AX.X, ALU.max))
                    seq(V.tensor_tensor(eq[:], src[:], top[:, c, :].unsqueeze(2).to_broadcast([P, T, E]),
                                        ALU.is_equal))
                    seq(V.tensor_tensor(eq[:], eq[:], rev[:], ALU.mult))
                    seq(V.tensor_reduce(code[:], eq[:], AX.X, ALU.max))
                    seq(V.tensor_tensor(hot[:, c], rev[:], code[:].unsqueeze(2).to_broadcast([P, T, E]),
                                        ALU.is_equal))
                seq(V.tensor_tensor(both[:], hot[:, 0], hot[:, 1], ALU.add))
                for t in range(T):
                    ins = V.tensor_tensor(acum[:, t + 1, :], acum[:, t, :], both[:, t, :], ALU.add)
                    if t < T - 1:
                        seq(ins)
                    else:
                        ins.then_inc(acum_ready, 1)
                v.wait_ge(pos_psum, blk + 1)
                V.tensor_tensor(pos[:], ps[:, 3, 0:T * E].rearrange("p (t e) -> p t e", t=T), eoff[:],
                                ALU.add).then_inc(pos_read, 1)
                v.wait_ge(pos_read, blk + 1)
                v.wait_ge(acum_ready, blk + 1)
                seq(V.tensor_copy(acum[:, 0, :], acum[:, T, :]))
                if not isinstance(i, int):
                    v.wait_ge(slot_stored[j], i * 32)
                for c in range(2):
                    seq(V.tensor_tensor(eq[:], hot[:, c], pos[:], ALU.mult))
                    seq(V.tensor_reduce(slotf[:, c, :], eq[:], AX.X, ALU.add))
                seq(V.tensor_tensor(dl[:, j, :], top[:, 1, :], top[:, 0, :], ALU.subtract))
                V.tensor_copy(slot[:, j, :], slotf[:].rearrange("p c t -> p (c t)")).then_inc(slot_ready, 1)

            for j in range(2):
                block_(0, j)
            first = n[0]
            start = 4
            per = first - start
            with v.Fori(1, B // 2) as i:
                n[0] = 0
                base[0] = i * per + start
                for j in range(2):
                    block_(i, j)
            assert n[0] == per
            n[0] = 0
            base[0] = start + per * (B // 2)

            v.wait_ge(cnt_psum, 1)
            v.wait_ge(iota_ready, 2)
            seq(V.tensor_copy(cnt[:], ps[:, 3, 0:E]))
            seq(V.tensor_scalar(padf[:], cnt[:], float(P - 1), None, ALU.add))
            seq(V.tensor_copy(cnti[:], padf[:]))
            seq(V.tensor_scalar(cnti[:], cnti[:], 7, 7, ALU.logical_shift_right, ALU.logical_shift_left))
            seq(V.tensor_copy(padend[:], cnti[:]))
            seq(V.tensor_scalar(padf[:], cnt[:], pcol[:, 0:1], None, ALU.add))
            seq(V.tensor_tensor(padg[:], padf[:], padend[:], ALU.is_ge))
            seq(V.tensor_tensor(padf[:], padf[:], eoff[:, 0, :], ALU.add))
            seq(V.scalar_tensor_tensor(out=padf[:], in0=padg[:], scalar=float(1 << 20), in1=padf[:],
                                       op0=ALU.mult, op1=ALU.add))
            V.tensor_copy(padi[:], padf[:]).then_inc(pad_ready, 1)
            seq(V.tensor_scalar(tiles[:], padend[0:1, :], 1.0 / P, None, ALU.mult))
            seq(V.tensor_scalar(unused[:], padend[:], -1.0, float(QCAP), ALU.mult, ALU.add))
            seq(V.memset(tend[:], 0.0))
            for e in range(E):
                seq(V.tensor_tensor(tend[:, e + 1:e + 2], tend[:, e:e + 1], tiles[:, e:e + 1], ALU.add))
            seq(V.tensor_scalar(trow[:], tnum[:], float(P), None, ALU.mult))
            seq(V.memset(texp[:], 0.0))
            for e in range(1, E + 1):
                seq(V.tensor_scalar(tge[:], tnum[:], tend[:, e:e + 1], None, ALU.is_ge))
                seq(V.scalar_tensor_tensor(out=trow[:], in0=tge[:], scalar=unused[0:1, e - 1:e], in1=trow[:],
                                           op0=ALU.mult, op1=ALU.add))
                if e < E:
                    seq(V.tensor_tensor(texp[:], texp[:], tge[:], ALU.add))
            seq(V.tensor_copy(tab[:, 0, :], trow[:]))
            seq(V.tensor_copy(tab[:, 1, :], texp[:]))

        @block.tensor
        def _(pe):
            M = nc.tensor
            pe.wait_ge(cst_loaded, CST)
            pe.wait_ge(dve, 4)
            M.matmul(ps[0:H, 4, 0:NREL], rel[:], fone[:, 0, :], start=True, stop=True)
            M.matmul(ps[0:H, 5, 0:NREL], rel[:], fone[:, 1, :], start=True, stop=True).then_inc(f_psum, 1)

            def block_(i, j):
                blk = i * 2 + j
                past = not isinstance(blk, int) or blk >= 1
                for c in range(4):
                    pe.wait_ge(xn_ready, blk * T + 2 * c + 2)
                    if past or c >= 2:
                        pe.wait_ge(xT_ready, blk * 4 + c - 1)
                    for k in range(KD):
                        for h in range(2):
                            ins = M.transpose(ps[:, c % 2, k * 256 + h * P:k * 256 + (h + 1) * P],
                                              xn[:, j, 2 * c + h, k * P:(k + 1) * P], ident[:])
                    ins.then_inc(xnT_psum, 1)
                if past:
                    pe.wait_ge(lg_read, blk)
                for t in range(T):
                    if t % 2 == 0:
                        pe.wait_ge(xT_ready, blk * 4 + t // 2 + 1)
                    for k in range(KD):
                        ins = M.matmul(ps[:, 2, t * E:(t + 1) * E], xT[:, j, k, t * P:(t + 1) * P],
                                       wr[:, k, :], start=(k == 0), stop=(k == KD - 1))
                ins.then_inc(lg_psum, 1)
                pe.wait_ge(acum_ready, blk + 1)
                if past:
                    pe.wait_ge(pos_read, blk)
                M.matmul(ps[:, 3, 0:T * E], lower[:], both[:].rearrange("p t e -> p (t e)"),
                         start=True, stop=False)
                M.matmul(ps[:, 3, 0:T * E], ones[:], acum[:, 0:T, :].rearrange("p t e -> p (t e)"),
                         start=False, stop=True).then_inc(pos_psum, 1)

            for j in range(2):
                block_(0, j)
            with pe.Fori(1, B // 2) as i:
                for j in range(2):
                    block_(i, j)
            pe.wait_ge(pos_read, B)
            M.matmul(ps[:, 3, 0:E], ones[:], acum[:, T, :], start=True, stop=True).then_inc(cnt_psum, 1)


def phase_b(nc, cst, xs, ys, tab):
    U = 4
    with ExitStack() as ctx:
        def sb(name, shape, dt=F32):
            return ctx.enter_context(nc.sbuf_tensor("b_" + name, shape, dt))

        def sem(name):
            return ctx.enter_context(nc.semaphore("b_" + name))

        ps = ctx.enter_context(nc.psum_tensor("b_ps", [P, 8, 512], F32))
        xt_ps, gu_ps, ht_ps, y_ps = (ps[:, 2 * n:2 * n + 2] for n in range(4))
        wgu = sb("wgu", [P, E, KD, 2 * F])
        wd = sb("wd", [P, E, KD, D])
        ident = sb("ident", [P, P])
        xt = sb("xt", [P, U, D])
        xT = sb("xT", [P, 2, KD, P])
        th = sb("th", [P, 2, F])
        ga = sb("ga", [P, 2, F])
        h = sb("h", [P, 2, F])
        hT = sb("hT", [P, 2, KD, P])
        y = sb("y", [P, 2, D])

        w_loaded = sem("w_loaded")
        x_loaded = [sem(f"x_loaded{n}") for n in range(U)]
        xT_psum = sem("xT_psum")
        xT_ready = sem("xT_ready")
        gu_psum = sem("gu_psum")
        th_ready = sem("th_ready")
        ga_ready = sem("ga_ready")
        h_ready = sem("h_ready")
        hT_psum = sem("hT_psum")
        hT_ready = sem("hT_ready")
        y_psum = sem("y_psum")
        y_ready = sem("y_ready")
        y_stored = [sem(f"y_stored{n}") for n in range(2)]

        def fixed(t):
            return isinstance(t, int)

        def loop(eng, body):
            for j in range(U):
                body(0, j)
            with eng.Fori(1, NX // U - 1) as i:
                for j in range(U):
                    body(i, j)
            for j in range(U):
                body(NX // U - 1, j)

        block = ctx.enter_context(nc.Block())

        @block.sync
        def _(sp):
            sp.dma_start(ident[:], cst["ident"]).then_inc(w_loaded, 16)
            sp.dma_start(wgu[:], cst["wgu"]).then_inc(w_loaded, 16)
            sp.dma_start(wd[:], cst["wd"]).then_inc(w_loaded, 16)

            def body(i, j):
                t = i * U + j
                if not fixed(t) or t >= U:
                    sp.wait_ge(xT_psum, t - U + 1)
                row = nc.sync.value_load(tab[0:1, 0, bass.ds(t, 1)], min_val=0, max_val=NROW - P)
                sp.dma_start(xt[:, j, :], xs[bass.ds(row, P), :]).then_inc(x_loaded[j], 16)

            loop(sp, body)

        @block.gpsimd
        def _(pool):
            def body(i, j):
                t = i * U + j
                pool.wait_ge(y_ready, t + 1)
                pool.dma_start(ys[bass.ds(t * P, P), :], y[:, j % 2, :]).then_inc(y_stored[j % 2], 16)

            loop(pool, body)
            for n in range(2):
                pool.wait_ge(y_stored[n], 16 * (NX // 2))

        @block.tensor
        def _(pe):
            M = nc.tensor
            pe.wait_ge(w_loaded, 48)

            def transpose_x(i, jj):
                t, j = i * U + jj, jj % U
                pe.wait_ge(x_loaded[j], (i + jj // U) * 16 + 16)
                if not fixed(t) or t >= 2:
                    pe.wait_ge(xT_ready, t - 1)
                for k in range(KD):
                    ins = M.transpose(xt_ps[:, j % 2, k * P:(k + 1) * P], xt[:, j, k * P:(k + 1) * P], ident[:])
                ins.then_inc(xT_psum, 1)

            def gate_up(t, j, e):
                pe.wait_ge(xT_ready, t + 1)
                if not fixed(t) or t >= 2:
                    pe.wait_ge(h_ready, t - 1)
                for k in range(KD):
                    ins = M.matmul(gu_ps[:, j % 2, :], xT[:, j % 2, k, :],
                                   wgu[:, bass.ds(e, 1), k, :].rearrange("p o n -> p (o n)"),
                                   start=(k == 0), stop=(k == KD - 1))
                ins.then_inc(gu_psum, 1)

            def transpose_h(t, j):
                pe.wait_ge(h_ready, t + 1)
                if not fixed(t) or t >= 2:
                    pe.wait_ge(hT_ready, t - 1)
                for k in range(KD):
                    ins = M.transpose(ht_ps[:, j % 2, k * P:(k + 1) * P], h[:, j % 2, k * P:(k + 1) * P], ident[:])
                ins.then_inc(hT_psum, 1)

            def down(t, j, e):
                pe.wait_ge(hT_ready, t + 1)
                if not fixed(t) or t >= 2:
                    pe.wait_ge(y_ready, t - 1)
                for k in range(KD):
                    ins = M.matmul(y_ps[:, j % 2, 0:D], hT[:, j % 2, k, :],
                                   wd[:, bass.ds(e, 1), k, :].rearrange("p o n -> p (o n)"),
                                   start=(k == 0), stop=(k == KD - 1))
                ins.then_inc(y_psum, 1)

            def expert(t):
                return nc.tensor.value_load(tab[0:1, 1, bass.ds(t, 1)], min_val=0, max_val=E - 1)

            def body(i, j):
                t = i * U + j
                if not fixed(t) or t < NX - 1:
                    transpose_x(i, j + 1)
                gate_up(t, j, expert(t))
                if not fixed(t) or t >= 1:
                    transpose_h(t - 1, (j - 1) % U)
                if not fixed(t) or t >= 2:
                    down(t - 2, (j - 2) % U, expert(t - 2))

            transpose_x(0, 0)
            loop(pe, body)
            down(NX - 2, (NX - 2) % U, expert(NX - 2))
            transpose_h(NX - 1, (NX - 1) % U)
            down(NX - 1, (NX - 1) % U, expert(NX - 1))

        @block.scalar
        def _(act):
            def copy_x(t, j):
                act.wait_ge(xT_psum, t + 1)
                if not fixed(t) or t >= 2:
                    act.wait_ge(gu_psum, t - 1)
                nc.scalar.copy(xT[:, j % 2].rearrange("p k s -> p (k s)"),
                               xt_ps[:, j % 2, 0:D]).then_inc(xT_ready, 1)

            def tanh(t, j):
                act.wait_ge(gu_psum, t + 1)
                if not fixed(t) or t >= 2:
                    act.wait_ge(ga_ready, t - 1)
                nc.scalar.activation(th[:, j % 2, :], gu_ps[:, j % 2, 0:F], ACT.Tanh,
                                     scale=0.5).then_inc(th_ready, 1)

            def copy_h(t, j):
                act.wait_ge(hT_psum, t + 1)
                if not fixed(t) or t >= 2:
                    act.wait_ge(y_psum, t - 1)
                nc.scalar.copy(hT[:, j % 2].rearrange("p k s -> p (k s)"),
                               ht_ps[:, j % 2, 0:F]).then_inc(hT_ready, 1)

            def body(i, j):
                t = i * U + j
                if not fixed(t) or t < NX - 1:
                    copy_x(t + 1, (j + 1) % U)
                tanh(t, j)
                if not fixed(t) or t >= 1:
                    copy_h(t - 1, (j - 1) % U)

            copy_x(0, 0)
            loop(act, body)
            copy_h(NX - 1, (NX - 1) % U)

        @block.vector
        def _(v):
            V = nc.vector

            def swiglu(t, j):
                v.wait_ge(th_ready, t + 1)
                V.scalar_tensor_tensor(out=ga[:, j % 2, :], in0=th[:, j % 2, :], scalar=1.0,
                                       in1=gu_ps[:, j % 2, 0:F], op0=ALU.add, op1=ALU.mult).then_inc(ga_ready, 1)
                v.wait_ge(ga_ready, t + 1)
                if not fixed(t) or t >= 2:
                    v.wait_ge(hT_psum, t - 1)
                V.tensor_tensor(h[:, j % 2, :], gu_ps[:, j % 2, F:2 * F], ga[:, j % 2, :],
                                ALU.mult).then_inc(h_ready, 1)

            def copy_y(i, jj):
                t, j = i * U + jj, jj % U
                v.wait_ge(y_psum, t + 1)
                if not fixed(t) or t >= 2:
                    v.wait_ge(y_stored[j % 2], (i * (U // 2) + jj // 2) * 16)
                V.tensor_copy(y[:, j % 2, :], y_ps[:, j % 2, 0:D]).then_inc(y_ready, 1)

            def body(i, j):
                t = i * U + j
                swiglu(t, j)
                if not fixed(t) or t >= 2:
                    copy_y(i, j - 2)

            loop(v, body)
            copy_y(NX // U, -2)
            copy_y(NX // U, -1)


def phase_c(nc, cst, xT_dram, frow_dram, part_dram, ctx_dram):
    NS = T * G
    with ExitStack() as ctx:
        def sb(name, shape, dt=F32):
            return ctx.enter_context(nc.sbuf_tensor("c_" + name, shape, dt))

        def sem(name):
            return ctx.enter_context(nc.semaphore("c_" + name))

        ps = ctx.enter_context(nc.psum_tensor("c_ps", [P, 8, 512], F32))
        st_ps = [ps[:, 2 * n:2 * n + 2].rearrange("p b n -> p (b n)") for n in range(2)]
        o_ps = ps[:, 4:6].rearrange("p b n -> p (b n)")
        ring = [ps[:, 6, :], ps[:, 7, :]]
        PS = 8

        ident = sb("ident", [P, P])
        wqkv = sb("wqkv", [P, KD, NG, 3 * G * HD])
        cos = sb("cos", [P, T, 2 * G * HD])
        sin = sb("sin", [P, T, 2 * G * HD])
        bias = sb("bias", [P, H, 2 * P])
        biasT = sb("biasT", [P, H, 2 * P])
        xT = sb("xT", [P, KD, S])
        qst = sb("qst", [P, 2, G, S], BF16)
        kst = sb("kst", [P, 2, G, S], BF16)
        vst = sb("vst", [P, NG, T, G, 2 * HD])
        ra = sb("ra", [P, T, 2 * G * HD])
        rb = sb("rb", [P, T, 2 * G * HD])
        qk = sb("qk", [P, T, 2 * G * HD])
        part = [sb(f"part{n}", [P, S], BF16) for n in range(3)]
        rest = sb("rest", [P, S])
        mp = sb("mp", [P, G * T, 3])
        mx = sb("mx", [P, G * T])
        mpart = [sb(f"mpart{n}", [G * T, P], BF16) for n in range(3)]
        mr = sb("mr", [G * T, P])
        mr2 = sb("mr2", [G * T, P])
        prob = sb("prob", [P, PS, S])
        oT = sb("oT", [P, S])
        rs = sb("rs", [P, T * G])
        cn = sb("cn", [P, 2, T, G * HD])

        cst_loaded = sem("cst_loaded")
        kones = sem("kones")
        vones = sem("vones")
        mp_set = sem("mp_set")
        passed = sem("passed")
        x_loaded = sem("x_loaded")
        ring_full = sem("ring_full")
        ring_free = sem("ring_free")
        rope_ready = sem("rope_ready")
        v_ready = sem("v_ready")
        qk_ready = sem("qk_ready")
        qkT_done = sem("qkT_done")
        p0_ready = sem("p0_ready")
        rest_ready = sem("rest_ready")
        p1_ready = sem("p1_ready")
        p2_ready = sem("p2_ready")
        part_stored = sem("part_stored")
        stack_loaded = [sem(f"stack_loaded{n}") for n in range(2)]
        mp_done = sem("mp_done")
        mx_ready = sem("mx_ready")
        mp_step = sem("mp_step")
        m_ready = sem("m_ready")
        m_loaded = sem("m_loaded")
        st_full = sem("st_full")
        biased = sem("biased")
        exped = sem("exped")
        pv_done = sem("pv_done")
        oT_ready = sem("oT_ready")
        o_ready = sem("o_ready")
        rs_ready = sem("rs_ready")
        cn_ready = sem("cn_ready")
        cn_stored = [sem(f"cn_stored{n}") for n in range(2)]

        NCST = 6
        NSTACK = 6

        def max_items():
            items = []
            for qt in range(T):
                last = (qt + 1) * P
                near = min(last, 512)
                per = 512 // near
                for h0 in range(0, G, per):
                    items.append(("near", qt, h0, per, last - near, near))
                far = last - near
                if far:
                    per = 512 // far if far <= 256 else 1
                    for h0 in range(0, G, per):
                        items.append(("far", qt, h0, per, 0, far))
            return items

        MAXI = max_items()
        PROJ = [("proj", p) for p in range(T // 2)]
        QKT = [("qkT", c) for c in range(2)]
        NI = len(MAXI) + 1 + len(PROJ) + len(QKT)
        assert (NI * NG) % 2 == 0

        LEAD, TAIL = 6, 4
        items = MAXI + [("mT",)] + PROJ + QKT

        def plan(with_max, with_proj):
            todo = (MAXI + [("mT",)] if with_max else []) + (PROJ + QKT if with_proj else [])
            strips = [("strip", kt, h) for kt in range(T) for h in range(G)]
            out = strips[:LEAD]
            rest_, at, n = strips[LEAD:], 0, 0
            for i, it in enumerate(todo):
                out.append(it)
                while n < len(rest_) and (n + 1) * len(todo) <= (i + 1) * len(rest_):
                    out.append(rest_[n])
                    n += 1
            return out + rest_[n:]

        RING_AT = {it: r for r, it in enumerate(items)}

        PRO = PROJ + QKT + MAXI + [("mT",)] + PROJ + QKT
        R0 = len(PRO)

        def passes(eng, body):
            with eng.Fori(0, B - 1) as i:
                for j in range(NG):
                    body(i * NG + j, j, True, True)
            for j in range(NG):
                u = NU - NG + j
                body(u, j, u < NU - 1, u < NU - 2)

        def ring_index(u, r):
            return u * NI + (R0 + r)

        block = ctx.enter_context(nc.Block())

        @block.sync
        def _(sp):
            for dst, name in ((ident, "ident"), (wqkv, "wqkv"), (cos, "cos"), (sin, "sin")):
                sp.dma_start(dst[:], cst[name]).then_inc(cst_loaded, 16)
            fh = frow_dram
            for h in range(H):
                sp.dma_start(bias[:, h, :], bass.AP(tensor=fh.tensor, offset=h * P * 2 * NREL + P - 1,
                                                    ap=[[2 * NREL - 1, P], [1, 2 * P]])).then_inc(cst_loaded, 16)
                sp.dma_start(biasT[:, h, :], bass.AP(tensor=fh.tensor, offset=(h * P * 2 + 1) * NREL + P - 1,
                                                     ap=[[2 * NREL - 1, P], [1, 2 * P]])).then_inc(cst_loaded, 16)

            def load_x(b):
                if not isinstance(b, int) or b >= 1:
                    sp.wait_ge(v_ready, b * NG * 4)
                sp.dma_start(xT[:], xT_dram[bass.ds(b, 1)].rearrange("o p k s -> (o p) k s")
                             ).then_inc(x_loaded, 16)

            def load_stacks(u, j):
                for n, ready in enumerate((p0_ready, p1_ready, p2_ready)):
                    sp.wait_ge(ready, u * 2 + 2)
                    sp.dma_start(part_dram[n], part[n][:]).then_inc(part_stored, 16)
                sp.wait_ge(part_stored, u * 48 + 48)
                if not isinstance(u, int) or u >= 2:
                    sp.wait_ge(st_full, u * NS - NS)
                half = G * HD * S
                for stack, terms, at in ((qst, QTERM, 0), (kst, KTERM, half)):
                    t = 0
                    while t < NTERM:
                        step = terms[t + 1] - terms[t] if t + 1 < NTERM else 0
                        n = 1
                        while step >= 0 and t + n < NTERM and terms[t + n] - terms[t + n - 1] == step:
                            n += 1
                        src = bass.AP(tensor=part_dram.tensor, offset=terms[t] * 2 * half + at,
                                      ap=[[step * 2 * half, n], [G * S, HD], [1, G * S]])
                        sp.dma_start(stack[t * HD:(t + n) * HD, j % 2].rearrange("p h s -> p (h s)"), src).then_inc(stack_loaded[j % 2], 16)
                        t += n

            def load_m(u, j):
                sp.wait_ge(m_ready, u * 3 + 3)
                for n in range(3):
                    sp.dma_start(qst[KROWS + n:KROWS + n + 1, j % 2, :, :].rearrange("o h (q i) -> o (h q) i", i=P),
                                 mpart[n][:]).then_inc(m_loaded, 16)

            def store(u, j, b, g):
                sp.wait_ge(cn_ready, u + 1)
                sp.dma_start(ctx_dram[bass.ds(b * S, S), g * G * HD:(g + 1) * G * HD]
                             .rearrange("(t p) d -> p t d", p=P), cn[:, j % 2]).then_inc(cn_stored[j % 2], 16)

            load_x(0)
            load_stacks(0, 0)
            load_m(0, 0)
            load_stacks(1, 1)

            def body(u, j, b, with_max, with_proj):
                if with_max:
                    load_m(u + 1, (j + 1) % NG)
                if with_proj and (j + 2) % NG == 0:
                    load_x(b + 1)
                if with_proj:
                    load_stacks(u + 2, (j + 2) % NG)
                if not (isinstance(u, int) and u == 0):
                    store(u - 1, (j - 1) % NG, b if j else b - 1, (j - 1) % NG)

            for j in range(NG):
                body(j, j, 0, True, True)
            with sp.Fori(1, B - 1) as i:
                for j in range(NG):
                    body(i * NG + j, j, i, True, True)
            for j in range(NG):
                u = NU - NG + j
                body(u, j, B - 1, u < NU - 1, u < NU - 2)
            store(NU - 1, NG - 1, B - 1, NG - 1)
            for n in range(2):
                sp.wait_ge(cn_stored[n], 16 * (NU // 2))

        @block.tensor
        def _(pe):
            M = nc.tensor
            pe.wait_ge(cst_loaded, 16 * (4 + 2 * H))
            pe.wait_ge(kones, 1)
            pe.wait_ge(vones, 2)

            def take(n):
                if not isinstance(n, int) or n >= 2:
                    pe.wait_ge(ring_free, n - 1)

            def proj(u, g, p, n, par, b1):
                take(n)
                if p == 0 and g == 0:
                    pe.wait_ge(x_loaded, b1 * 16)
                for t in range(2):
                    for k in range(KD):
                        ins = M.matmul(ring[par][:, t * 256:t * 256 + 3 * G * HD],
                                       xT[:, k, (2 * p + t) * P:(2 * p + t + 1) * P],
                                       wqkv[:, k, g, :], start=(k == 0), stop=(k == KD - 1))
                ins.then_inc(ring_full, 1)

            def qkT(u, c, n, par):
                take(n)
                pe.wait_ge(qk_ready, u * 4 + 2 * c + 2)
                for t in range(4):
                    ins = M.transpose(ring[par][:, t * P:(t + 1) * P], qk[:, 4 * c + t, :], ident[:])
                ins.then_inc(ring_full, 1)

            def maxi(u, j, it, n, par):
                kind, qt, h0, per, k0, keys = it
                take(n)
                for h in range(h0, h0 + per):
                    c = (h - h0) * keys
                    ins = M.matmul(ring[par][:, c:c + keys], qst[0:KROWS, j % 2, h, qt * P:(qt + 1) * P],
                                   kst[0:KROWS, j % 2, h, k0:k0 + keys], start=True, stop=True)
                ins.then_inc(ring_full, 1)

            def mT(u, n, par):
                take(n)
                pe.wait_ge(mx_ready, u + 1)
                M.transpose(ring[par][0:G * T, 0:P], mx[:], ident[:]).then_inc(ring_full, 1)

            def item(u, i, jj, it, n, par, b1=None):
                if it[0] == "proj":
                    proj(u, jj % NG, it[1], n, par, b1)
                elif it[0] == "qkT":
                    qkT(u, it[1], n, par)
                elif it[0] == "mT":
                    mT(u, n, par)
                else:
                    if it == MAXI[0]:
                        pe.wait_ge(stack_loaded[jj % 2], (i * 2 + jj // 2 + 1) * (16 * NSTACK))
                    maxi(u, jj, it, n, par)

            def strip(u, j, kt, h):
                s = kt * G + h
                if not isinstance(u, int) or u or s >= 2:
                    pe.wait_ge(exped, u * NS + s - 1)
                w = S - kt * P
                for c in range(0, w, 512):
                    e = min(w, c + 512)
                    ins = M.matmul(st_ps[s % 2][:, c:e], kst[0:KROWS + MROWS, j % 2, h, kt * P:(kt + 1) * P],
                                   qst[0:KROWS + MROWS, j % 2, h, kt * P + c:kt * P + e],
                                   start=True, stop=True)
                ins.then_inc(st_full, 1)

            def pv(u, g, kt):
                pe.wait_ge(exped, u * NS + (kt + 1) * G)
                if kt == 0 and (not isinstance(u, int) or u):
                    pe.wait_ge(cn_ready, u)
                if kt == 0:
                    pe.wait_ge(v_ready, u * 4 + 4)
                q0 = kt * P
                for c0, c1 in ((q0, 512), (max(q0, 512), S)):
                    if c0 >= c1:
                        continue
                    for h in range(G):
                        ins = M.matmul(o_ps[32 * h:32 * h + 32, c0:c1], vst[:, g, kt, h, :],
                                       prob[:, (kt * G + h) % PS, c0 - q0:c1 - q0],
                                       start=(kt == 0), stop=(kt == (3 if c1 == 512 else T - 1)))
                ins.then_inc(pv_done, 1)

            def back(u):
                pe.wait_ge(oT_ready, u + 1)
                for t in range(T):
                    ins = M.transpose(o_ps[:, t * P:(t + 1) * P], oT[:, t * P:(t + 1) * P], ident[:])
                ins.then_inc(o_ready, 1)

            r = 0
            for it in PROJ + QKT:
                item(0, 0, 0, it, r, r % 2, 1)
                r += 1
            for it in MAXI + [("mT",)]:
                item(0, 0, 0, it, r, r % 2)
                r += 1
            for it in PROJ + QKT:
                item(1, 0, 1, it, r, r % 2, 1)
                r += 1

            def body(u, j, b, with_max, with_proj):
                first = isinstance(u, int) and u == 0
                pe.wait_ge(m_loaded, u * 48 + 48)
                r = 0
                for st in plan(with_max, with_proj):
                    if st[0] == "strip":
                        _, kt, h = st
                        strip(u, j, kt, h)
                        if h == G - 1 and kt:
                            pv(u, j, kt - 1)
                        elif h == G - 1 and not first:
                            pv(u - 1, (j - 1) % NG, T - 1)
                        if (kt, h) == (1, 1) and not first:
                            back(u - 1)
                    else:
                        n = u * NI + (R0 + r)
                        par = (R0 + j * NI + r) % 2
                        ahead = 2 if st[0] in ("proj", "qkT") else 1
                        item(u + ahead, b, j + ahead, st, n, par, b + 1 + (j + 2) // NG)
                        r += 1

            for j in range(NG):
                body(j, j, 0, True, True)
            with pe.Fori(1, B - 1) as i:
                for j in range(NG):
                    body(i * NG + j, j, i, True, True)
            for j in range(NG):
                u = NU - NG + j
                body(u, j, B - 1, u < NU - 1, u < NU - 2)
            pv(NU - 1, NG - 1, T - 1)
            back(NU - 1)

        @block.vector
        def _(v):
            V = nc.vector
            V.memset(mp[:], LOWEST).then_inc(mp_set, 1)
            v.wait_ge(mp_set, 1)
            V.memset(kst[KROWS:KROWS + MROWS].rearrange("p a h s -> p (a h s)"), 1.0).then_inc(kones, 1)
            v.wait_ge(cst_loaded, 16 * (4 + 2 * H))

            def item(u, i, jj, it, n, par):
                j = jj % NG
                v.wait_ge(ring_full, n + 1)
                if it[0] == "proj":
                    p = it[1]
                    src = ring[par].rearrange("p (t c) -> p t c", t=2)
                    w = 2 * G * HD
                    at = slice(2 * p, 2 * p + 2)
                    if not isinstance(u, int) or u >= 1:
                        v.wait_ge(qk_ready, u * 4 + p - 3)
                    V.tensor_tensor(ra[:, at, :], src[:, :, 0:w], cos[:, at, :], ALU.mult).then_inc(rope_ready, 1)
                    wh = G * HD // 2
                    for o in range(2):
                        to, of = slice(o * wh, (o + 1) * wh), slice((1 - o) * wh, (2 - o) * wh)
                        V.tensor_tensor(rb[:, at, :].rearrange("p t (a z) -> p t a z", a=2)[:, :, :, to],
                                        src[:, :, 0:w].rearrange("p t (a z) -> p t a z", a=2)[:, :, :, of],
                                        sin[:, at, :].rearrange("p t (a z) -> p t a z", a=2)[:, :, :, to],
                                        ALU.mult).then_inc(rope_ready, 1)
                    V.tensor_copy(vst[:, j % NG, at, :, 0:HD],
                                  src[:, :, w:w + G * HD].rearrange("p t (h z) -> p t h z", z=HD)).then_inc(v_ready, 1)
                    v.wait_ge(v_ready, u * 4 + p + 1)
                    v.sem_inc(ring_free, 1)
                elif it[0] == "qkT":
                    c = it[1]
                    at = slice(c * 512, (c + 1) * 512)
                    if not isinstance(u, int) or u >= 1:
                        v.wait_ge(part_stored, u * 48)
                        v.wait_ge(p2_ready, u * 2)
                    V.tensor_copy(part[0][:, at], ring[par]).then_inc(p0_ready, 1)
                    v.wait_ge(p0_ready, u * 2 + c + 1)
                    V.tensor_tensor(rest[:, at], ring[par], part[0][:, at], ALU.subtract).then_inc(rest_ready, 1)
                    v.wait_ge(rest_ready, u * 2 + c + 1)
                    v.sem_inc(ring_free, 1)
                elif it[0] == "mT":
                    if not isinstance(u, int) or u >= 1:
                        v.wait_ge(m_loaded, u * 48)
                    src = ring[par][0:G * T, 0:P]
                    V.tensor_scalar(mpart[0][:], src, -1.0, None, ALU.mult).then_inc(m_ready, 1)
                    v.wait_ge(m_ready, u * 3 + 1)
                    V.scalar_tensor_tensor(out=mr[:], in0=src, scalar=-1.0, in1=mpart[0][:], op0=ALU.mult,
                                           op1=ALU.subtract).then_inc(ring_free, 1)
                    v.wait_ge(ring_free, n + 1)
                    V.tensor_copy(mpart[1][:], mr[:]).then_inc(m_ready, 1)
                    v.wait_ge(m_ready, u * 3 + 2)
                    V.tensor_tensor(mpart[2][:], mr[:], mpart[1][:], ALU.subtract).then_inc(m_ready, 1)
                else:
                    kind, qt, h0, per, k0, keys = it
                    bank = ring[par][:, 0:per * keys].rearrange("p (h k) -> p h k", h=per)
                    out = mp[:].rearrange("p (h q) n -> p h q n", h=G)[:, h0:h0 + per, qt, :]
                    if kind == "near":
                        wn = min(2 * P, keys)
                        if keys > wn:
                            V.tensor_reduce(out[:, :, 1], bank[:, :, 0:keys - wn], AX.X, ALU.max)
                        else:
                            v.sem_inc(passed, 1)
                        for h in range(per):
                            ins = V.tensor_tensor_reduce(
                                out=bank[:, h, keys - wn:keys], in0=bank[:, h, keys - wn:keys],
                                in1=biasT[:, (j % NG) * G + h0 + h, 2 * P - wn:2 * P],
                                scale=1.0, scalar=LOWEST, op0=ALU.add, op1=ALU.max,
                                accum_out=out[:, h, 0:1])
                    else:
                        ins = V.tensor_reduce(out[:, :, 2], bank, AX.X, ALU.max)
                    ins.then_inc(ring_free, 1)
                    if it == MAXI[-1]:
                        v.wait_ge(ring_free, n + 1)
                        if not isinstance(u, int) or u >= 1:
                            v.wait_ge(ring_full, n)
                        V.tensor_reduce(mx[:], mp[:], AX.X, ALU.max).then_inc(mx_ready, 1)

            def strip(u, j, kt, h):
                s = kt * G + h
                v.wait_ge(st_full, u * NS + s + 1)
                w = min(2 * P, S - kt * P)
                V.tensor_tensor(st_ps[s % 2][:, 0:w], st_ps[s % 2][:, 0:w],
                                bias[:, j * G + h, 0:w], ALU.add).then_inc(biased, 1)

            def norm(u, i, jj):
                j = jj % NG
                v.wait_ge(o_ready, u + 1)
                heads = o_ps.rearrange("p (h z) -> p h z", z=2 * HD)
                if not isinstance(u, int) or u >= 2:
                    v.wait_ge(cn_stored[j % 2], (i * 2 + jj // 2) * 16)
                V.reciprocal(rs[:], heads[:, :, HD]).then_inc(rs_ready, 1)
                v.wait_ge(rs_ready, u + 1)
                V.tensor_tensor(cn[:, j % 2].rearrange("p t (h z) -> p (t h) z", z=HD), heads[:, :, 0:HD],
                                rs[:].unsqueeze(2).to_broadcast([P, T * G, HD]), ALU.mult).then_inc(cn_ready, 1)

            r = 0
            for it in PROJ + QKT:
                item(0, 0, 0, it, r, r % 2)
                r += 1
            for it in MAXI + [("mT",)]:
                item(0, 0, 0, it, r, r % 2)
                r += 1
            for it in PROJ + QKT:
                item(1, 0, 1, it, r, r % 2)
                r += 1

            def body(u, j, b, with_max, with_proj):
                first = isinstance(u, int) and u == 0
                r = 0
                for st in plan(with_max, with_proj):
                    if st[0] == "strip":
                        strip(u, j, st[1], st[2])
                        if (st[1], st[2]) == (1, 2) and not first:
                            norm(u - 1, b, j - 1)
                    else:
                        ahead = 2 if st[0] in ("proj", "qkT") else 1
                        item(u + ahead, b, j + ahead, st, u * NI + (R0 + r), (R0 + j * NI + r) % 2)
                        r += 1

            for j in range(NG):
                body(j, j, 0, True, True)
            with v.Fori(1, B - 1) as i:
                for j in range(NG):
                    body(i * NG + j, j, i, True, True)
            for j in range(NG):
                u = NU - NG + j
                body(u, j, B - 1, u < NU - 1, u < NU - 2)
            norm(NU - 1, B - 1, NG - 1)

        @block.scalar
        def _(act):
            def second(u):
                for c in range(2):
                    act.wait_ge(rest_ready, u * 2 + c + 1)
                    nc.scalar.copy(part[1][:, c * 512:(c + 1) * 512],
                                   rest[:, c * 512:(c + 1) * 512]).then_inc(p1_ready, 1)

            def strip(u, kt, h):
                s = kt * G + h
                act.wait_ge(biased, u * NS + s + 1)
                if s >= PS:
                    act.wait_ge(pv_done, u * T + (kt - 1))
                elif not isinstance(u, int) or u:
                    act.wait_ge(pv_done, u * T + (kt - 1))
                w = S - kt * P
                nc.scalar.activation(prob[:, s % PS, 0:w], st_ps[s % 2][:, 0:w], ACT.Exp).then_inc(exped, 1)

            def copy_o(u):
                act.wait_ge(pv_done, u * T + T)
                if not isinstance(u, int) or u >= 1:
                    act.wait_ge(o_ready, u)
                nc.scalar.copy(oT[:], o_ps).then_inc(oT_ready, 1)

            second(0)
            second(1)

            def body(u, j, b, with_max, with_proj):
                first = isinstance(u, int) and u == 0
                for kt in range(T):
                    for h in range(G):
                        strip(u, kt, h)
                        if (kt, h) == (0, G - 1) and not first:
                            copy_o(u - 1)
                if with_proj:
                    second(u + 2)

            for j in range(NG):
                body(j, j, 0, True, True)
            with act.Fori(1, B - 1) as i:
                for j in range(NG):
                    body(i * NG + j, j, i, True, True)
            for j in range(NG):
                u = NU - NG + j
                body(u, j, B - 1, u < NU - 1, u < NU - 2)
            copy_o(NU - 1)

        @block.gpsimd
        def _(pool):
            nc.gpsimd.memset(vst[:], 0.0).then_inc(vones, 1)
            pool.wait_ge(vones, 1)
            nc.gpsimd.memset(vst[:, :, :, :, HD:HD + 1], 1.0).then_inc(vones, 1)

            def unit(u):
                for p in range(T // 2):
                    at = slice(2 * p, 2 * p + 2)
                    pool.wait_ge(rope_ready, u * 12 + 3 * p + 3)
                    if not isinstance(u, int) or u:
                        pool.wait_ge(rest_ready, u * 2)
                    nc.gpsimd.tensor_tensor(qk[:, at, :].rearrange("p t c -> p (t c)"),
                                            ra[:, at, :].rearrange("p t c -> p (t c)"),
                                            rb[:, at, :].rearrange("p t c -> p (t c)"), ALU.add).then_inc(qk_ready, 1)
                for c in range(2):
                    pool.wait_ge(p1_ready, u * 2 + c + 1)
                    nc.gpsimd.tensor_tensor(part[2][:, c * 512:(c + 1) * 512], rest[:, c * 512:(c + 1) * 512],
                                            part[1][:, c * 512:(c + 1) * 512], ALU.subtract).then_inc(p2_ready, 1)

            unit(0)
            with pool.Fori(1, NU) as u:
                unit(u)


def phase_d(nc, x, cst, ctx_dram, ys, slots_dram, dl_dram, unused, out):
    with ExitStack() as ctx:
        def sb(name, shape, dt=F32):
            return ctx.enter_context(nc.sbuf_tensor("d_" + name, shape, dt))

        def sem(name):
            return ctx.enter_context(nc.semaphore("d_" + name))

        ps = ctx.enter_context(nc.psum_tensor("d_ps", [P, 8, 512], F32))
        ident = sb("ident", [P, P])
        wo = sb("wo", [P, KD, D])
        slot = sb("slot", [P, B, 2 * T], U32)
        yf = sb("yf", [P, B, 2 * T])
        yg = sb("yg", [P, B, 2 * T])
        yi = sb("yi", [P, B, 2 * T], U32)
        dl = sb("dl", [P, B, T])
        ex = sb("ex", [P, B, T])
        den = sb("den", [P, B, T])
        w1 = sb("w1", [P, B, T])
        w2 = sb("w2", [P, B, T])
        cx = sb("cx", [P, 2, T, D])
        xr = sb("xr", [P, 2, T, D])
        y1 = sb("y1", [P, 2, T, D])
        y2 = sb("y2", [P, 2, T, D])
        cT = sb("cT", [P, 2, D])
        fa = sb("fa", [P, 2, D])
        fb = sb("fb", [P, 2, D])
        th = sb("th", [P, 2, D])
        fc = sb("fc", [P, 2, D])
        fd = sb("fd", [P, 2, D])
        ob = sb("ob", [P, 2, T, D])

        cst_loaded = sem("cst_loaded")
        w_ready = sem("w_ready")
        w_step = sem("w_step")
        y_step = sem("y_step")
        yi_ready = sem("yi_ready")
        c_loaded = [sem(f"c_loaded{n}") for n in range(2)]
        x_loaded = [sem(f"x_loaded{n}") for n in range(2)]
        y_loaded = [sem(f"y_loaded{n}") for n in range(2)]
        cT_psum = sem("cT_psum")
        cT_ready = sem("cT_ready")
        s_psum = sem("s_psum")
        fa_ready = sem("fa_ready")
        fb_ready = sem("fb_ready")
        th_ready = sem("th_ready")
        fc_ready = sem("fc_ready")
        fd_ready = sem("fd_ready")
        o_ready = sem("o_ready")
        o_stored = [sem(f"o_stored{n}") for n in range(2)]
        block = ctx.enter_context(nc.Block())

        def old(b, n):
            return not isinstance(b, int) or b >= n

        @block.sync
        def _(sp):
            sp.dma_start(ident[:], cst["ident"]).then_inc(cst_loaded, 16)
            sp.dma_start(wo[:], cst["wo"]).then_inc(cst_loaded, 16)
            sp.dma_start(slot[:], slots_dram.rearrange("b p s -> p b s")).then_inc(cst_loaded, 16)
            sp.dma_start(dl[:], dl_dram.rearrange("b p s -> p b s")).then_inc(cst_loaded, 16)
            for b in range(B):
                j = b % 2
                if b >= 2:
                    sp.wait_ge(cT_psum, (b - 1) * T)
                    sp.wait_ge(o_ready, (b - 1) * T)
                rows = slice(b * S, (b + 1) * S)
                sp.dma_start(cx[:, j], ctx_dram[rows, :].rearrange("(t p) d -> p t d", p=P)).then_inc(c_loaded[j], 16)
                sp.dma_start(xr[:, j], x[rows, :].rearrange("(t p) d -> p t d", p=P)).then_inc(x_loaded[j], 16)
                if b >= 1:
                    sp.wait_ge(o_ready, b * T)
                    sp.dma_start(out[(b - 1) * S:b * S, :].rearrange("(t p) d -> p t d", p=P),
                                 ob[:, 1 - j]).then_inc(o_stored[1 - j], 16)
            sp.wait_ge(o_ready, B * T)
            sp.dma_start(out[(B - 1) * S:B * S, :].rearrange("(t p) d -> p t d", p=P),
                         ob[:, (B - 1) % 2]).then_inc(o_stored[(B - 1) % 2], 16)
            for n in range(2):
                sp.wait_ge(o_stored[n], 16 * (B // 2))

        @block.gpsimd
        def _(pool):
            pool.wait_ge(yi_ready, 1)
            for b in range(B):
                if b >= 2:
                    pool.wait_ge(fb_ready, (b - 1) * T)
                for t in range(T):
                    for c, y in ((0, y1), (1, y2)):
                        nc.gpsimd.indirect_dma_start(
                            y[:, b % 2, t, :], None, ys[:, :],
                            bass.IndirectOffsetOnAxis(ap=yi[:, b, c * T + t:c * T + t + 1], axis=0)
                        ).then_inc(y_loaded[b % 2], 16)

        @block.tensor
        def _(pe):
            M = nc.tensor
            pe.wait_ge(cst_loaded, 64)

            def tile(i, b, t):
                pass

            for b in range(B):
                pe.wait_ge(c_loaded[b % 2], 16 * (b // 2 + 1))
                for t in range(T):
                    i = b * T + t
                    if i >= 2:
                        pe.wait_ge(cT_ready, i - 1)
                    for k in range(KD):
                        ins = M.transpose(ps[:, i % 2, k * P:(k + 1) * P], cx[:, b % 2, t, k * P:(k + 1) * P], ident[:])
                    ins.then_inc(cT_psum, 1)
                    pe.wait_ge(cT_ready, i + 1)
                    if i >= 2:
                        pe.wait_ge(fd_ready, i - 1)
                    for k in range(KD):
                        ins = M.matmul(ps[:, 2 + i % 2, 0:D], cT[:, i % 2, k * P:(k + 1) * P], wo[:, k, :],
                                       start=(k == 0), stop=(k == KD - 1))
                    ins.then_inc(s_psum, 1)

        @block.scalar
        def _(act):
            act.wait_ge(cst_loaded, 64)
            nc.scalar.activation(ex[:], dl[:], ACT.Exp).then_inc(w_step, 1)
            for i in range(NT):
                act.wait_ge(cT_psum, i + 1)
                if i >= 2:
                    act.wait_ge(s_psum, i - 1)
                nc.scalar.copy(cT[:, i % 2, :], ps[:, i % 2, 0:D]).then_inc(cT_ready, 1)
                act.wait_ge(fb_ready, i + 1)
                if i >= 2:
                    act.wait_ge(fc_ready, i - 1)
                nc.scalar.activation(th[:, i % 2, :], fb[:, i % 2, :], ACT.Tanh, scale=0.5).then_inc(th_ready, 1)

        @block.vector
        def _(v):
            V = nc.vector
            v.wait_ge(cst_loaded, 64)
            V.tensor_copy(yf[:], slot[:]).then_inc(y_step, 1)
            v.wait_ge(y_step, 1)
            for e in range(1, E):
                V.tensor_scalar(yg[:], slot[:], float(e * QCAP), None, ALU.is_ge).then_inc(y_step, 1)
                v.wait_ge(y_step, 2 * e)
                V.scalar_tensor_tensor(out=yf[:], in0=yg[:], scalar=unused[:, e - 1:e], in1=yf[:],
                                       op0=ALU.mult, op1=ALU.subtract, reverse1=True).then_inc(y_step, 1)
                v.wait_ge(y_step, 2 * e + 1)
            V.tensor_copy(yi[:], yf[:]).then_inc(yi_ready, 1)
            v.wait_ge(w_step, 1)
            V.tensor_scalar(den[:], ex[:], 1.0, None, ALU.add).then_inc(w_step, 1)
            v.wait_ge(w_step, 2)
            V.reciprocal(den[:], den[:]).then_inc(w_step, 1)
            v.wait_ge(w_step, 3)
            V.tensor_scalar(w1[:], den[:], 0.5, None, ALU.mult).then_inc(w_step, 1)
            v.wait_ge(w_step, 4)
            V.tensor_tensor(w2[:], w1[:], ex[:], ALU.mult).then_inc(w_step, 1)
            v.wait_ge(w_step, 5)

            def mix(i):
                b, t = i // T, i % T
                if t == 0:
                    v.wait_ge(y_loaded[b % 2], 32 * T * (b // 2 + 1))
                    v.wait_ge(x_loaded[b % 2], 16 * (b // 2 + 1))
                V.tensor_scalar(fa[:, i % 2, :], y1[:, b % 2, t, :], w1[:, b, t:t + 1], None,
                                ALU.mult).then_inc(fa_ready, 1)
                v.wait_ge(fa_ready, i + 1)
                V.scalar_tensor_tensor(out=fb[:, i % 2, :], in0=y2[:, b % 2, t, :], scalar=w2[:, b, t:t + 1],
                                       in1=fa[:, i % 2, :], op0=ALU.mult, op1=ALU.add).then_inc(fb_ready, 1)

            def gate(i):
                b, t = i // T, i % T
                v.wait_ge(th_ready, i + 1)
                V.scalar_tensor_tensor(out=fc[:, i % 2, :], in0=th[:, i % 2, :], scalar=1.0,
                                       in1=fb[:, i % 2, :], op0=ALU.add, op1=ALU.mult).then_inc(fc_ready, 1)
                v.wait_ge(fc_ready, i + 1)
                v.wait_ge(s_psum, i + 1)
                V.tensor_tensor(fd[:, i % 2, :], ps[:, 2 + i % 2, 0:D], fc[:, i % 2, :],
                                ALU.mult).then_inc(fd_ready, 1)
                v.wait_ge(fd_ready, i + 1)
                if t == 0 and b >= 2:
                    v.wait_ge(o_stored[b % 2], 16 * (b // 2))
                V.scalar_tensor_tensor(out=ob[:, b % 2, t, :], in0=fd[:, i % 2, :], scalar=0.5,
                                       in1=xr[:, b % 2, t, :], op0=ALU.mult, op1=ALU.add).then_inc(o_ready, 1)

            for i in range(NT + 1):
                if i < NT:
                    mix(i)
                if i:
                    gate(i - 1)


def build(nc, x, cst, out):
    xs = nc.dram_tensor("queue_x", [NROW, D], F32, kind="Internal").ap()
    ys = nc.dram_tensor("tiles_y", [NX * P, D], F32, kind="Internal").ap()
    xT_dram = nc.dram_tensor("xT", [B, P, KD, S], F32, kind="Internal").ap()
    slots_dram = nc.dram_tensor("slots", [B, P, 2 * T], U32, kind="Internal").ap()
    dl_dram = nc.dram_tensor("logit_diff", [B, P, T], F32, kind="Internal").ap()
    fvec_dram = nc.dram_tensor("bias_by_distance", [H, 2, NREL], F32, kind="Internal").ap()
    frow_dram = nc.dram_tensor("bias_rows", [H, P, 2, NREL], F32, kind="Internal").ap()
    part_dram = nc.dram_tensor("parts", [3, P, S], BF16, kind="Internal").ap()
    ctx_dram = nc.dram_tensor("context", [B * S, D], F32, kind="Internal").ap()
    with nc.sbuf_tensor("tile_table", [1, 2, NX], I32) as tab, nc.sbuf_tensor("unused", [P, E], F32) as unused:
        phase_a(nc, x, cst, xs, xT_dram, slots_dram, dl_dram, fvec_dram, frow_dram, tab, unused)
        phase_b(nc, cst, xs, ys, tab)
        phase_c(nc, cst, xT_dram, frow_dram, part_dram, ctx_dram)
        phase_d(nc, x, cst, ctx_dram, ys, slots_dram, dl_dram, unused, out)


def shape_constants():
    import math

    import numpy as np

    f32 = np.float32
    inv = (f32(1.0) / np.power(f32(10000.0), np.arange(0, HD, 2, dtype=f32) / f32(HD))).astype(f32)
    ang = np.outer(np.arange(S, dtype=f32), inv).astype(f32)
    cos, sin = np.cos(ang), np.sin(ang)
    c16 = np.concatenate([cos, cos], 1)
    s16 = np.concatenate([-sin, sin], 1)
    scale = f32(1.0 / math.sqrt(HD))

    def rope_table(t):
        q = np.repeat(t * scale, G, axis=1)
        k = np.repeat(t, G, axis=1)
        return np.ascontiguousarray(np.concatenate([q, k], 1).reshape(T, P, 2 * G * HD).transpose(1, 0, 2)).astype(f32)

    dist = np.arange(NREL) - (P - 1)
    rp = np.maximum(dist, 0)
    exact = NBUCKET // 2
    large = exact + (np.log(np.maximum(rp.astype(f32), f32(1.0)) / f32(exact)) / f32(math.log(128 / exact))
                     * f32(NBUCKET - exact)).astype(np.int32)
    bucket = np.where(rp < exact, rp, np.minimum(large, NBUCKET - 1))
    fone = np.zeros((NBUCKET + 1, NREL), f32)
    seen = dist >= 0
    fone[bucket[seen], np.nonzero(seen)[0]] += 1.0
    fone[NBUCKET - 1, seen] -= 1.0
    fone[NBUCKET, ~seen] = -BIG
    back = 2 * P - 1 - np.arange(NREL) + (P - 1)
    fone = np.stack([fone, fone[:, np.maximum(back, 0)]], 1)
    e = np.arange(E, dtype=f32)
    return {
        "ident": np.eye(P, dtype=f32),
        "lower": np.triu(np.ones((P, P), f32), 1),
        "rev": np.ascontiguousarray(np.broadcast_to(E - e, (P, T, E))).astype(f32),
        "eoff": np.ascontiguousarray(np.broadcast_to(e * QCAP, (P, T, E))).astype(f32),
        "fone": fone,
        "cos": rope_table(c16),
        "sin": rope_table(s16),
    }


def kernel(L0_attn_x, L0_attn_Wq, L0_attn_Wk, L0_attn_Wv, L0_attn_Wo, L0_attn_rel_emb,
           L0_ffn_router_weight, L0_ffn_gate_up_proj, L0_ffn_down_proj):
    import numpy as np
    import concourse.bacc as bacc
    from concourse.bass_utils import run_bass_kernel_spmd

    def rows(w):
        return np.ascontiguousarray(np.asarray(w).reshape(KD, P, -1).transpose(1, 0, 2))

    wq, wk = (np.asarray(w).reshape(D, NG, G, HD).transpose(0, 1, 3, 2).reshape(D, NG, G * HD)
              for w in (L0_attn_Wq, L0_attn_Wk))
    wv = np.asarray(L0_attn_Wv).reshape(D, NG, G * HD)
    qkv = np.concatenate([wq, wk, wv], 2)
    gu = np.asarray(L0_ffn_gate_up_proj).transpose(2, 0, 1).reshape(KD, P, E, 2 * F).transpose(1, 2, 0, 3)
    dn = np.asarray(L0_ffn_down_proj).transpose(2, 0, 1).reshape(KD, P, E, D).transpose(1, 2, 0, 3)
    data = {
        "x": np.ascontiguousarray(np.asarray(L0_attn_x).reshape(B * S, D)),
        "wqkv": np.ascontiguousarray(qkv.reshape(KD, P, NG, 3 * G * HD).transpose(1, 0, 2, 3)),
        "wo": rows(L0_attn_Wo),
        "wr": rows(np.asarray(L0_ffn_router_weight).T),
        "rel": np.ascontiguousarray(np.asarray(L0_attn_rel_emb)),
        "wgu": np.ascontiguousarray(gu),
        "wd": np.ascontiguousarray(dn),
    }
    data.update(shape_constants())

    nc = bacc.Bacc("TRN2", target_bir_lowering=False, num_devices=1)
    aps = {n: nc.dram_tensor("in_" + n, a.shape, mybir.dt.from_np(a.dtype), kind="ExternalInput").ap()
           for n, a in data.items()}
    out = nc.dram_tensor("out", [B * S, D], F32, kind="ExternalOutput").ap()
    build(nc, aps["x"], aps, out)
    res = run_bass_kernel_spmd(nc, [{"in_" + n: a for n, a in data.items()}], core_ids=[0])
    return res.results[0]["out"].reshape(B, S, D)
```

```python
from contextlib import ExitStack

import concourse.bass as bass
from concourse import mybir

F32 = mybir.dt.float32
BF16 = mybir.dt.bfloat16
I32 = mybir.dt.int32
U32 = mybir.dt.uint32
ALU = mybir.AluOpType
ACT = mybir.ActivationFunctionType
AX = mybir.AxisListType

P = 128
B, S, D = 8, 1024, 256
H, HD = 16, 16
G = 4
NG = H // G
T = S // P
NT = B * T
KD = D // P
E, F = 8, 256
NU = B * NG
EPS = 1e-5
BIG = 1.0e30
LOWEST = -3.0e38
NBUCKET = 32
NREL = 2 * P + P

QCAP = B * S
NX = 2 * B * S // P + E
DUMMY = E * QCAP
NROW = DUMMY + E * P

QTERM = (0, 0, 0, 1, 1, 2)
KTERM = (0, 1, 2, 0, 1, 0)
NTERM = len(QTERM)
KROWS = NTERM * HD
MROWS = 3


def phase_a(nc, x, cst, xs, xT_dram, slots_dram, dl_dram, fvec_dram, frow_dram, tab, unused):
    with ExitStack() as ctx:
        def sb(name, shape, dt=F32):
            return ctx.enter_context(nc.sbuf_tensor("a_" + name, shape, dt))

        def sem(name):
            return ctx.enter_context(nc.semaphore("a_" + name))

        ps = ctx.enter_context(nc.psum_tensor("a_ps", [P, 8, 512], F32))
        xb = sb("xb", [P, 2, T, D])
        xn = sb("xn", [P, 2, T, D])
        xT = sb("xT", [P, 2, KD, S])
        wr = sb("wr", [P, KD, E])
        ident = sb("ident", [P, P])
        lowerf = sb("lowerf", [P, P])
        lower = sb("lower", [P, P], BF16)
        ones = sb("ones", [P, P], BF16)
        rev = sb("rev", [P, T, E])
        eoff = sb("eoff", [P, T, E])
        rel = sb("rel", [NBUCKET + 1, H])
        fone = sb("fone", [NBUCKET + 1, 2, NREL])
        fsb = sb("fsb", [H, 2, NREL])
        stats = sb("stats", [P, T, 6])
        mv = sb("mv", [P, T, 2])
        var = sb("var", [P, T])
        sd = sb("sd", [P, T])
        r0 = sb("r0", [P, T])
        r1 = sb("r1", [P, T])
        r2 = sb("r2", [P, T])
        r3 = sb("r3", [P, T])
        rstd = sb("rstd", [P, T])
        lg = sb("lg", [P, T, E])
        lg2 = sb("lg2", [P, T, E])
        top = sb("top", [P, 2, T])
        eq = sb("eq", [P, T, E])
        code = sb("code", [P, T])
        hot = sb("hot", [P, 2, T, E])
        both = sb("both", [P, T, E], BF16)
        acum = sb("acum", [P, T + 1, E], BF16)
        pos = sb("pos", [P, T, E])
        slotf = sb("slotf", [P, 2, T])
        slot = sb("slot", [P, 2, 2 * T], U32)
        dl = sb("dl", [P, 2, T])
        zero = sb("zero", [P, D])
        cnt = sb("cnt", [P, E])
        cnti = sb("cnti", [P, E], I32)
        pcol = sb("pcol", [P, 1])
        padend = sb("padend", [P, E])
        padf = sb("padf", [P, E])
        padg = sb("padg", [P, E])
        padi = sb("padi", [P, E], U32)
        tiles = sb("tiles", [1, E])
        tend = sb("tend", [1, E + 1])
        tnum = sb("tnum", [1, NX])
        tge = sb("tge", [1, NX])
        trow = sb("trow", [1, NX])
        texp = sb("texp", [1, NX])

        x_loaded = [sem(f"x_loaded{n}") for n in range(2)]
        cst_loaded = sem("cst_loaded")
        dve = sem("dve")
        passed = sem("passed")
        ppassed = sem("ppassed")
        var_ready = sem("var_ready")
        sd_ready = sem("sd_ready")
        xn_ready = sem("xn_ready")
        xnT_psum = sem("xnT_psum")
        xT_ready = sem("xT_ready")
        xT_stored = [sem(f"xT_stored{n}") for n in range(2)]
        lg_psum = sem("lg_psum")
        lg_read = sem("lg_read")
        acum_ready = sem("acum_ready")
        pos_psum = sem("pos_psum")
        pos_read = sem("pos_read")
        slot_ready = sem("slot_ready")
        slot_stored = [sem(f"slot_stored{n}") for n in range(2)]
        scattered = [sem(f"scattered{n}") for n in range(2)]
        zero_ready = sem("zero_ready")
        iota_ready = sem("iota_ready")
        cnt_psum = sem("cnt_psum")
        pad_ready = sem("pad_ready")
        pad_done = sem("pad_done")
        f_psum = sem("f_psum")
        f_ready = sem("f_ready")
        f_stored = sem("f_stored")
        dummy_done = sem("dummy_done")

        CST = 16 * 7
        block = ctx.enter_context(nc.Block())

        @block.sync
        def _(sp):
            for dst, name in ((wr, "wr"), (ident, "ident"), (lowerf, "lower"),
                              (rev, "rev"), (eoff, "eoff"), (fone, "fone")):
                sp.dma_start(dst[:], cst[name]).then_inc(cst_loaded, 16)
            sp.dma_start(rel[0:NBUCKET, :], cst["rel"]).then_inc(cst_loaded, 16)

            def load(blk, j):
                sp.dma_start(xb[:, j], x[bass.ds(blk * S, S), :].rearrange("(t p) d -> p t d", p=P)
                             ).then_inc(x_loaded[j], 16)

            def store(blk, j):
                sp.wait_ge(xT_ready, blk * 4 + 4)
                sp.dma_start(xT_dram[bass.ds(blk, 1)].rearrange("o p k s -> (o p) k s"),
                             xT[:, j]).then_inc(xT_stored[j], 16)
                sp.wait_ge(slot_ready, blk + 1)
                sp.dma_start(slots_dram[bass.ds(blk, 1)].rearrange("o p s -> (o p) s"),
                             slot[:, j]).then_inc(slot_stored[j], 16)
                sp.dma_start(dl_dram[bass.ds(blk, 1)].rearrange("o p s -> (o p) s"),
                             dl[:, j]).then_inc(slot_stored[j], 16)

            load(0, 0)
            load(1, 1)
            sp.wait_ge(f_ready, 1)
            sp.dma_start(fvec_dram, fsb[:]).then_inc(f_stored, 16)
            sp.wait_ge(f_stored, 16)
            sp.dma_start(frow_dram, fvec_dram.unsqueeze(1).to_broadcast([H, P, 2, NREL])).then_inc(f_stored, 16)
            sp.wait_ge(zero_ready, 1)
            for e in range(E):
                sp.dma_start(xs[DUMMY + e * P:DUMMY + (e + 1) * P, :], zero[:]).then_inc(dummy_done, 16)
            with sp.Fori(0, B // 2 - 1) as i:
                for j in range(2):
                    blk = i * 2 + j
                    store(blk, j)
                    sp.wait_ge(xn_ready, blk * T + T)
                    load(blk + 2, j)
            for j in range(2):
                store(B - 2 + j, j)
            for j in range(2):
                sp.wait_ge(xT_stored[j], 16 * (B // 2))
                sp.wait_ge(slot_stored[j], 32 * (B // 2))
            sp.wait_ge(f_stored, 32)
            sp.wait_ge(dummy_done, 16 * E)

        @block.gpsimd
        def _(pool):
            nc.gpsimd.memset(zero[:], 0.0).then_inc(zero_ready, 1)
            nc.gpsimd.iota(pcol[:], [[0, 1]], channel_multiplier=1,
                           allow_small_or_imprecise_dtypes=True).then_inc(iota_ready, 1)
            nc.gpsimd.iota(tnum[:], [[1, NX]], channel_multiplier=0,
                           allow_small_or_imprecise_dtypes=True).then_inc(iota_ready, 1)

            def scatter(blk, j):
                pool.wait_ge(xn_ready, blk * T + T)
                pool.wait_ge(slot_ready, blk + 1)
                pool.sem_inc(ppassed, 1)
                for c in range(2):
                    for t in range(T):
                        nc.gpsimd.indirect_dma_start(
                            xs[:, :], bass.IndirectOffsetOnAxis(ap=slot[:, j, c * T + t:c * T + t + 1], axis=0),
                            xn[:, j, t, :], None).then_inc(scattered[j], 16)

            with pool.Fori(0, B // 2) as i:
                for j in range(2):
                    scatter(i * 2 + j, j)
            pool.wait_ge(zero_ready, 1)
            pool.wait_ge(pad_ready, 1)
            for e in range(E):
                nc.gpsimd.indirect_dma_start(
                    xs[:, :], bass.IndirectOffsetOnAxis(ap=padi[:, e:e + 1], axis=0),
                    zero[:], None, bounds_check=NROW - 1, oob_is_err=False).then_inc(pad_done, 16)
            for j in range(2):
                pool.wait_ge(scattered[j], 16 * NT)
            pool.wait_ge(pad_done, 16 * E)

        @block.scalar
        def _(act):
            def block_(i, j):
                blk = i * 2 + j
                act.wait_ge(var_ready, blk + 1)
                nc.scalar.activation(sd[:], var[:], ACT.Sqrt).then_inc(sd_ready, 1)
                if not isinstance(i, int):
                    act.wait_ge(xT_stored[j], i * 16)
                for c in range(4):
                    act.wait_ge(xnT_psum, blk * 4 + c + 1)
                    nc.scalar.copy(xT[:, j, :, c * 256:(c + 1) * 256],
                                   ps[:, c % 2, :].rearrange("p (k s) -> p k s", k=KD)
                                   ).then_inc(xT_ready, 1)

            for j in range(2):
                block_(0, j)
            with act.Fori(1, B // 2) as i:
                for j in range(2):
                    block_(i, j)

        @block.vector
        def _(v):
            n = [0]
            V = nc.vector

            def seq(ins):
                ins.then_inc(dve, 1)
                n[0] += 1
                v.wait_ge(dve, base[0] + n[0])
                return ins

            base = [0]
            seq(V.memset(acum[:], 0.0))
            seq(V.memset(rel[NBUCKET:NBUCKET + 1, :], 1.0))
            v.wait_ge(cst_loaded, CST)
            seq(V.tensor_copy(lower[:], lowerf[:]))
            seq(V.memset(ones[:], 1.0))
            v.wait_ge(f_psum, 1)
            V.tensor_copy(fsb[:], ps[0:H, 4:6, 0:NREL]).then_inc(f_ready, 1)

            def block_(i, j):
                blk = i * 2 + j
                v.wait_ge(x_loaded[j], i * 16 + 16)
                for t in range(T):
                    V.bn_stats(stats[:, t, :], xb[:, j, t, :]).then_inc(dve, 1)
                    n[0] += 1
                v.wait_ge(dve, base[0] + n[0])
                v.sem_inc(passed, 1)
                for t in range(T):
                    V.bn_aggr(mv[:, t, :], stats[:, t, :]).then_inc(dve, 1)
                    n[0] += 1
                v.wait_ge(dve, base[0] + n[0])
                V.tensor_scalar(var[:], mv[:, :, 1], EPS, None, ALU.add).then_inc(var_ready, 1)
                v.wait_ge(var_ready, blk + 1)
                v.wait_ge(sd_ready, blk + 1)
                seq(V.reciprocal(r0[:], sd[:]))
                seq(V.tensor_tensor(r1[:], r0[:], r0[:], ALU.mult))
                seq(V.tensor_tensor(r2[:], r1[:], var[:], ALU.mult))
                seq(V.tensor_scalar(r3[:], r2[:], -0.5, 1.5, ALU.mult, ALU.add))
                seq(V.tensor_tensor(rstd[:], r0[:], r3[:], ALU.mult))
                if not isinstance(i, int):
                    v.wait_ge(scattered[j], i * (16 * 2 * T))
                    v.wait_ge(xnT_psum, blk * 4 - 4)
                for t in range(T):
                    V.tensor_scalar(xn[:, j, t, :], xb[:, j, t, :], mv[:, t, 0:1], rstd[:, t:t + 1],
                                    ALU.subtract, ALU.mult).then_inc(xn_ready, 1)
                v.wait_ge(lg_psum, blk + 1)
                seq(V.tensor_copy(lg[:], ps[:, 2, 0:T * E].rearrange("p (t e) -> p t e", t=T)))
                V.tensor_copy(lg2[:], lg[:]).then_inc(lg_read, 1)
                v.wait_ge(lg_read, blk + 1)
                for c, src in ((0, lg), (1, lg2)):
                    if c == 1:
                        seq(V.scalar_tensor_tensor(out=lg2[:], in0=hot[:, 0], scalar=LOWEST,
                                                   in1=lg[:], op0=ALU.mult, op1=ALU.add))
                    seq(V.tensor_reduce(top[:, c, :], src[:], AX.X, ALU.max))
                    seq(V.tensor_tensor(eq[:], src[:], top[:, c, :].unsqueeze(2).to_broadcast([P, T, E]),
                                        ALU.is_equal))
                    seq(V.tensor_tensor(eq[:], eq[:], rev[:], ALU.mult))
                    seq(V.tensor_reduce(code[:], eq[:], AX.X, ALU.max))
                    seq(V.tensor_tensor(hot[:, c], rev[:], code[:].unsqueeze(2).to_broadcast([P, T, E]),
                                        ALU.is_equal))
                seq(V.tensor_tensor(both[:], hot[:, 0], hot[:, 1], ALU.add))
                for t in range(T):
                    ins = V.tensor_tensor(acum[:, t + 1, :], acum[:, t, :], both[:, t, :], ALU.add)
                    if t < T - 1:
                        seq(ins)
                    else:
                        ins.then_inc(acum_ready, 1)
                v.wait_ge(pos_psum, blk + 1)
                V.tensor_tensor(pos[:], ps[:, 3, 0:T * E].rearrange("p (t e) -> p t e", t=T), eoff[:],
                                ALU.add).then_inc(pos_read, 1)
                v.wait_ge(pos_read, blk + 1)
                v.wait_ge(acum_ready, blk + 1)
                seq(V.tensor_copy(acum[:, 0, :], acum[:, T, :]))
                if not isinstance(i, int):
                    v.wait_ge(slot_stored[j], i * 32)
                for c in range(2):
                    seq(V.tensor_tensor(eq[:], hot[:, c], pos[:], ALU.mult))
                    seq(V.tensor_reduce(slotf[:, c, :], eq[:], AX.X, ALU.add))
                seq(V.tensor_tensor(dl[:, j, :], top[:, 1, :], top[:, 0, :], ALU.subtract))
                V.tensor_copy(slot[:, j, :], slotf[:].rearrange("p c t -> p (c t)")).then_inc(slot_ready, 1)

            for j in range(2):
                block_(0, j)
            first = n[0]
            start = 4
            per = first - start
            with v.Fori(1, B // 2) as i:
                n[0] = 0
                base[0] = i * per + start
                for j in range(2):
                    block_(i, j)
            assert n[0] == per
            n[0] = 0
            base[0] = start + per * (B // 2)

            v.wait_ge(cnt_psum, 1)
            v.wait_ge(iota_ready, 2)
            seq(V.tensor_copy(cnt[:], ps[:, 3, 0:E]))
            seq(V.tensor_scalar(padf[:], cnt[:], float(P - 1), None, ALU.add))
            seq(V.tensor_copy(cnti[:], padf[:]))
            seq(V.tensor_scalar(cnti[:], cnti[:], 7, 7, ALU.logical_shift_right, ALU.logical_shift_left))
            seq(V.tensor_copy(padend[:], cnti[:]))
            seq(V.tensor_scalar(padf[:], cnt[:], pcol[:, 0:1], None, ALU.add))
            seq(V.tensor_tensor(padg[:], padf[:], padend[:], ALU.is_ge))
            seq(V.tensor_tensor(padf[:], padf[:], eoff[:, 0, :], ALU.add))
            seq(V.scalar_tensor_tensor(out=padf[:], in0=padg[:], scalar=float(1 << 20), in1=padf[:],
                                       op0=ALU.mult, op1=ALU.add))
            V.tensor_copy(padi[:], padf[:]).then_inc(pad_ready, 1)
            seq(V.tensor_scalar(tiles[:], padend[0:1, :], 1.0 / P, None, ALU.mult))
            seq(V.tensor_scalar(unused[:], padend[:], -1.0, float(QCAP), ALU.mult, ALU.add))
            seq(V.memset(tend[:], 0.0))
            for e in range(E):
                seq(V.tensor_tensor(tend[:, e + 1:e + 2], tend[:, e:e + 1], tiles[:, e:e + 1], ALU.add))
            seq(V.tensor_scalar(trow[:], tnum[:], float(P), None, ALU.mult))
            seq(V.memset(texp[:], 0.0))
            for e in range(1, E + 1):
                seq(V.tensor_scalar(tge[:], tnum[:], tend[:, e:e + 1], None, ALU.is_ge))
                seq(V.scalar_tensor_tensor(out=trow[:], in0=tge[:], scalar=unused[0:1, e - 1:e], in1=trow[:],
                                           op0=ALU.mult, op1=ALU.add))
                if e < E:
                    seq(V.tensor_tensor(texp[:], texp[:], tge[:], ALU.add))
            seq(V.tensor_copy(tab[:, 0, :], trow[:]))
            seq(V.tensor_copy(tab[:, 1, :], texp[:]))

        @block.tensor
        def _(pe):
            M = nc.tensor
            pe.wait_ge(cst_loaded, CST)
            pe.wait_ge(dve, 4)
            M.matmul(ps[0:H, 4, 0:NREL], rel[:], fone[:, 0, :], start=True, stop=True)
            M.matmul(ps[0:H, 5, 0:NREL], rel[:], fone[:, 1, :], start=True, stop=True).then_inc(f_psum, 1)

            def block_(i, j):
                blk = i * 2 + j
                past = not isinstance(blk, int) or blk >= 1
                for c in range(4):
                    pe.wait_ge(xn_ready, blk * T + 2 * c + 2)
                    if past or c >= 2:
                        pe.wait_ge(xT_ready, blk * 4 + c - 1)
                    for k in range(KD):
                        for h in range(2):
                            ins = M.transpose(ps[:, c % 2, k * 256 + h * P:k * 256 + (h + 1) * P],
                                              xn[:, j, 2 * c + h, k * P:(k + 1) * P], ident[:])
                    ins.then_inc(xnT_psum, 1)
                if past:
                    pe.wait_ge(lg_read, blk)
                for t in range(T):
                    if t % 2 == 0:
                        pe.wait_ge(xT_ready, blk * 4 + t // 2 + 1)
                    for k in range(KD):
                        ins = M.matmul(ps[:, 2, t * E:(t + 1) * E], xT[:, j, k, t * P:(t + 1) * P],
                                       wr[:, k, :], start=(k == 0), stop=(k == KD - 1))
                ins.then_inc(lg_psum, 1)
                pe.wait_ge(acum_ready, blk + 1)
                if past:
                    pe.wait_ge(pos_read, blk)
                M.matmul(ps[:, 3, 0:T * E], lower[:], both[:].rearrange("p t e -> p (t e)"),
                         start=True, stop=False)
                M.matmul(ps[:, 3, 0:T * E], ones[:], acum[:, 0:T, :].rearrange("p t e -> p (t e)"),
                         start=False, stop=True).then_inc(pos_psum, 1)

            for j in range(2):
                block_(0, j)
            with pe.Fori(1, B // 2) as i:
                for j in range(2):
                    block_(i, j)
            pe.wait_ge(pos_read, B)
            M.matmul(ps[:, 3, 0:E], ones[:], acum[:, T, :], start=True, stop=True).then_inc(cnt_psum, 1)


def phase_b(nc, cst, xs, ys, tab):
    U = 4
    with ExitStack() as ctx:
        def sb(name, shape, dt=F32):
            return ctx.enter_context(nc.sbuf_tensor("b_" + name, shape, dt))

        def sem(name):
            return ctx.enter_context(nc.semaphore("b_" + name))

        ps = ctx.enter_context(nc.psum_tensor("b_ps", [P, 8, 512], F32))
        xt_ps, gu_ps, ht_ps, y_ps = (ps[:, 2 * n:2 * n + 2] for n in range(4))
        wgu = sb("wgu", [P, E, KD, 2 * F])
        wd = sb("wd", [P, E, KD, D])
        ident = sb("ident", [P, P])
        xt = sb("xt", [P, U, D])
        xT = sb("xT", [P, 2, KD, P])
        th = sb("th", [P, 2, F])
        ga = sb("ga", [P, 2, F])
        h = sb("h", [P, 2, F])
        hT = sb("hT", [P, 2, KD, P])
        y = sb("y", [P, 2, D])

        w_loaded = sem("w_loaded")
        x_loaded = [sem(f"x_loaded{n}") for n in range(U)]
        xT_psum = sem("xT_psum")
        xT_ready = sem("xT_ready")
        gu_psum = sem("gu_psum")
        th_ready = sem("th_ready")
        ga_ready = sem("ga_ready")
        h_ready = sem("h_ready")
        hT_psum = sem("hT_psum")
        hT_ready = sem("hT_ready")
        y_psum = sem("y_psum")
        y_ready = sem("y_ready")
        y_stored = [sem(f"y_stored{n}") for n in range(2)]

        def fixed(t):
            return isinstance(t, int)

        def loop(eng, body):
            for j in range(U):
                body(0, j)
            with eng.Fori(1, NX // U - 1) as i:
                for j in range(U):
                    body(i, j)
            for j in range(U):
                body(NX // U - 1, j)

        block = ctx.enter_context(nc.Block())

        @block.sync
        def _(sp):
            sp.dma_start(ident[:], cst["ident"]).then_inc(w_loaded, 16)
            sp.dma_start(wgu[:], cst["wgu"]).then_inc(w_loaded, 16)
            sp.dma_start(wd[:], cst["wd"]).then_inc(w_loaded, 16)

            def body(i, j):
                t = i * U + j
                if not fixed(t) or t >= U:
                    sp.wait_ge(xT_psum, t - U + 1)
                row = nc.sync.value_load(tab[0:1, 0, bass.ds(t, 1)], min_val=0, max_val=NROW - P)
                sp.dma_start(xt[:, j, :], xs[bass.ds(row, P), :]).then_inc(x_loaded[j], 16)

            loop(sp, body)

        @block.gpsimd
        def _(pool):
            def body(i, j):
                t = i * U + j
                pool.wait_ge(y_ready, t + 1)
                pool.dma_start(ys[bass.ds(t * P, P), :], y[:, j % 2, :]).then_inc(y_stored[j % 2], 16)

            loop(pool, body)
            for n in range(2):
                pool.wait_ge(y_stored[n], 16 * (NX // 2))

        @block.tensor
        def _(pe):
            M = nc.tensor
            pe.wait_ge(w_loaded, 48)

            def transpose_x(i, jj):
                t, j = i * U + jj, jj % U
                pe.wait_ge(x_loaded[j], (i + jj // U) * 16 + 16)
                if not fixed(t) or t >= 2:
                    pe.wait_ge(xT_ready, t - 1)
                for k in range(KD):
                    ins = M.transpose(xt_ps[:, j % 2, k * P:(k + 1) * P], xt[:, j, k * P:(k + 1) * P], ident[:])
                ins.then_inc(xT_psum, 1)

            def gate_up(t, j, e):
                pe.wait_ge(xT_ready, t + 1)
                if not fixed(t) or t >= 2:
                    pe.wait_ge(h_ready, t - 1)
                for k in range(KD):
                    ins = M.matmul(gu_ps[:, j % 2, :], xT[:, j % 2, k, :],
                                   wgu[:, bass.ds(e, 1), k, :].rearrange("p o n -> p (o n)"),
                                   start=(k == 0), stop=(k == KD - 1))
                ins.then_inc(gu_psum, 1)

            def transpose_h(t, j):
                pe.wait_ge(h_ready, t + 1)
                if not fixed(t) or t >= 2:
                    pe.wait_ge(hT_ready, t - 1)
                for k in range(KD):
                    ins = M.transpose(ht_ps[:, j % 2, k * P:(k + 1) * P], h[:, j % 2, k * P:(k + 1) * P], ident[:])
                ins.then_inc(hT_psum, 1)

            def down(t, j, e):
                pe.wait_ge(hT_ready, t + 1)
                if not fixed(t) or t >= 2:
                    pe.wait_ge(y_ready, t - 1)
                for k in range(KD):
                    ins = M.matmul(y_ps[:, j % 2, 0:D], hT[:, j % 2, k, :],
                                   wd[:, bass.ds(e, 1), k, :].rearrange("p o n -> p (o n)"),
                                   start=(k == 0), stop=(k == KD - 1))
                ins.then_inc(y_psum, 1)

            def expert(t):
                return nc.tensor.value_load(tab[0:1, 1, bass.ds(t, 1)], min_val=0, max_val=E - 1)

            def body(i, j):
                t = i * U + j
                if not fixed(t) or t < NX - 1:
                    transpose_x(i, j + 1)
                gate_up(t, j, expert(t))
                if not fixed(t) or t >= 1:
                    transpose_h(t - 1, (j - 1) % U)
                if not fixed(t) or t >= 2:
                    down(t - 2, (j - 2) % U, expert(t - 2))

            transpose_x(0, 0)
            loop(pe, body)
            down(NX - 2, (NX - 2) % U, expert(NX - 2))
            transpose_h(NX - 1, (NX - 1) % U)
            down(NX - 1, (NX - 1) % U, expert(NX - 1))

        @block.scalar
        def _(act):
            def copy_x(t, j):
                act.wait_ge(xT_psum, t + 1)
                if not fixed(t) or t >= 2:
                    act.wait_ge(gu_psum, t - 1)
                nc.scalar.copy(xT[:, j % 2].rearrange("p k s -> p (k s)"),
                               xt_ps[:, j % 2, 0:D]).then_inc(xT_ready, 1)

            def tanh(t, j):
                act.wait_ge(gu_psum, t + 1)
                if not fixed(t) or t >= 2:
                    act.wait_ge(ga_ready, t - 1)
                nc.scalar.activation(th[:, j % 2, :], gu_ps[:, j % 2, 0:F], ACT.Tanh,
                                     scale=0.5).then_inc(th_ready, 1)

            def copy_h(t, j):
                act.wait_ge(hT_psum, t + 1)
                if not fixed(t) or t >= 2:
                    act.wait_ge(y_psum, t - 1)
                nc.scalar.copy(hT[:, j % 2].rearrange("p k s -> p (k s)"),
                               ht_ps[:, j % 2, 0:F]).then_inc(hT_ready, 1)

            def body(i, j):
                t = i * U + j
                if not fixed(t) or t < NX - 1:
                    copy_x(t + 1, (j + 1) % U)
                tanh(t, j)
                if not fixed(t) or t >= 1:
                    copy_h(t - 1, (j - 1) % U)

            copy_x(0, 0)
            loop(act, body)
            copy_h(NX - 1, (NX - 1) % U)

        @block.vector
        def _(v):
            V = nc.vector

            def swiglu(t, j):
                v.wait_ge(th_ready, t + 1)
                V.scalar_tensor_tensor(out=ga[:, j % 2, :], in0=th[:, j % 2, :], scalar=1.0,
                                       in1=gu_ps[:, j % 2, 0:F], op0=ALU.add, op1=ALU.mult).then_inc(ga_ready, 1)
                v.wait_ge(ga_ready, t + 1)
                if not fixed(t) or t >= 2:
                    v.wait_ge(hT_psum, t - 1)
                V.tensor_tensor(h[:, j % 2, :], gu_ps[:, j % 2, F:2 * F], ga[:, j % 2, :],
                                ALU.mult).then_inc(h_ready, 1)

            def copy_y(i, jj):
                t, j = i * U + jj, jj % U
                v.wait_ge(y_psum, t + 1)
                if not fixed(t) or t >= 2:
                    v.wait_ge(y_stored[j % 2], (i * (U // 2) + jj // 2) * 16)
                V.tensor_copy(y[:, j % 2, :], y_ps[:, j % 2, 0:D]).then_inc(y_ready, 1)

            def body(i, j):
                t = i * U + j
                swiglu(t, j)
                if not fixed(t) or t >= 2:
                    copy_y(i, j - 2)

            loop(v, body)
            copy_y(NX // U, -2)
            copy_y(NX // U, -1)


def phase_c(nc, cst, xT_dram, frow_dram, part_dram, ctx_dram):
    with ExitStack() as ctx:
        def sb(name, shape, dt=F32):
            return ctx.enter_context(nc.sbuf_tensor("c_" + name, shape, dt))

        def sem(name):
            return ctx.enter_context(nc.semaphore("c_" + name))

        ps = ctx.enter_context(nc.psum_tensor("c_ps", [P, 8, 512], F32))
        NS = 3
        st_ps = [ps[:, n, :] for n in range(NS)]
        o_ps = ps[:, 3:5].rearrange("p b n -> p (b n)")
        NR = 3
        ring = [ps[:, 5 + n, :] for n in range(NR)]
        PS = 2 * G

        ident = sb("ident", [P, P])
        wqkv = sb("wqkv", [P, KD, NG, 3 * G * HD])
        cos = sb("cos", [P, T, 2 * G * HD])
        sin = sb("sin", [P, T, 2 * G * HD])
        bias = sb("bias", [P, H, 2 * P])
        biasT = sb("biasT", [P, H, 2 * P])
        xT = sb("xT", [P, KD, S])
        qst = sb("qst", [P, NG, G, S], BF16)
        kst = sb("kst", [P, NG, G, S], BF16)
        vst = sb("vst", [P, NG, T, G, 2 * HD])
        qkf = sb("qkf", [P, T, 2 * G * HD])
        ra = sb("ra", [P, T // 2, 2 * G * HD])
        rb = sb("rb", [P, T // 2, 2 * G * HD])
        qk = sb("qk", [P, T, 2 * G * HD])
        part = [sb(f"part{n}", [P, S], BF16) for n in range(3)]
        rest = sb("rest", [P, S])
        mp = sb("mp", [P, G * T, 3])
        mx = sb("mx", [P, G * T])
        mpart = [sb(f"mpart{n}", [G * T, P], BF16) for n in range(3)]
        mr = sb("mr", [G * T, P])
        prob = sb("prob", [P, PS, S])
        oT = sb("oT", [P, S])
        rs = sb("rs", [P, T * G])
        cn = sb("cn", [P, 2, T, G * HD])

        w_loaded = sem("w_loaded")
        bias_loaded = sem("bias_loaded")
        kones = sem("kones")
        vones = sem("vones")
        mp_set = sem("mp_set")
        passed = sem("passed")
        x_loaded = sem("x_loaded")
        ring_full = sem("ring_full")
        qkf_ready = sem("qkf_ready")
        v_ready = sem("v_ready")
        rope_step = sem("rope_step")
        qk_ready = sem("qk_ready")
        p0_ready = sem("p0_ready")
        flat_ready = sem("flat_ready")
        rest_ready = sem("rest_ready")
        p1_ready = sem("p1_ready")
        p2_ready = sem("p2_ready")
        part_stored = sem("part_stored")
        stack_loaded = [sem(f"stack_loaded{n}") for n in range(2)]
        max_done = sem("max_done")
        mx_ready = sem("mx_ready")
        mr_ready = sem("mr_ready")
        m_ready = sem("m_ready")
        m_loaded = sem("m_loaded")
        st_full = sem("st_full")
        biased = sem("biased")
        exped = sem("exped")
        pv_done = sem("pv_done")
        oT_ready = sem("oT_ready")
        o_ready = sem("o_ready")
        rs_ready = sem("rs_ready")
        cn_ready = sem("cn_ready")
        cn_stored = [sem(f"cn_stored{n}") for n in range(2)]

        NW = 4
        NSTACK = 6

        def max_items():
            out = []
            for qt in range(T):
                last = (qt + 1) * P
                near = min(last, 512)
                per = 512 // near
                for h0 in range(0, G, per):
                    out.append(("near", qt, h0, per, last - near, near))
                far = last - near
                if far:
                    per = 512 // far if far <= 256 else 1
                    for h0 in range(0, G, per):
                        out.append(("far", qt, h0, per, 0, far))
            return out

        MAXI = max_items()
        NMAX = len(MAXI)
        PROJ = [("proj", p) for p in range(T // 2)]
        QKT = [("qkT", c) for c in range(2)]
        FULL = MAXI[:6] + PROJ + MAXI[6:22] + QKT + MAXI[22:] + [("mT",)]
        NI = len(FULL)
        assert NI % NR == 0 and len(PROJ + QKT) % NR == 0

        PIECES = [(kt, h, c, min(S - kt * P, c + 512))
                  for kt in range(T) for h in range(G) for c in range(0, S - kt * P, 512)]
        NP = len(PIECES)
        UPTO = [sum(1 for p in PIECES if p[0] <= kt) for kt in range(T)]
        assert NP % NS == 0

        def ring_items(with_max, with_proj):
            if with_max and with_proj:
                return FULL
            return MAXI + [("mT",)] if with_max else PROJ + QKT if with_proj else []

        LEAD = 7
        WEIGHT = 400

        def plan(u, with_max, with_proj):
            todo = ring_items(with_max, with_proj)
            early, filling = isinstance(u, int) and u <= 0, isinstance(u, int) and u < 0
            out, n, q = [], 0, 0

            def ring_item():
                nonlocal n
                it = todo[n]
                if it[0] == "mT" and not filling:
                    return
                out.append(("ring", n, it))
                n += 1

            while n < len(todo) and (filling or n < LEAD):
                ring_item()
                if n == 2 and not early:
                    out.append(("last",))
                if n == 5 and not early:
                    out.append(("back",))
                if n == LEAD and not early:
                    out.append(("norm",))
            if filling:
                return out + ([("p1", 0), ("p1", 1)] if with_proj else [])
            if not todo and not early:
                out += [("last",), ("back",), ("norm",)]
            total = sum(S - kt * P + WEIGHT for kt in range(T) for h in range(G))
            done = 0
            second = []
            for kt in range(T):
                for h in range(G):
                    for c in (p for p in PIECES if p[:2] == (kt, h)):
                        out.append(("piece", q, c))
                        q += 1
                    if h == 1 and kt:
                        out.append(("pv", kt - 1))
                    done += S - kt * P + WEIGHT
                    if second and kt * G + h >= second[0]:
                        out += [("p1", 0), ("p1", 1)]
                        second = []
                    at = n
                    while n < len(todo) - 1 and (n - LEAD + 1) * total * MAX_BY <= (len(todo) - 1 - LEAD) * done:
                        if todo[n] == QKT[1]:
                            second = [kt * G + h + 3]
                        ring_item()
                    if todo and at == n == len(todo) - 1 and kt * G + h >= MT_AT:
                        out.append(("ring", n, todo[n]))
                        n += 1
            assert n == len(todo) and q == NP and not second
            return out

        MAX_BY = 0.9
        MT_AT = 0

        def ring_no(u, r):
            return r if isinstance(u, int) and u == -2 else u * NI + (NI + len(PROJ + QKT) + r)

        def run(eng, body):
            body(-2, -1, NG - 2, False, True)
            body(-1, -1, NG - 1, True, True)
            for j in range(NG):
                body(j, 0, j, True, True)
            with eng.Fori(1, B - 1) as i:
                for j in range(NG):
                    body(i * NG + j, i, j, True, True)
            for j in range(NG):
                u = NU - NG + j
                body(u, B - 1, j, u < NU - 1, u < NU - 2)

        LAG = 1

        def vector_order(plan):
            queue, at = [], 0
            for st in plan:
                if st[0] != "ring":
                    yield st
                    continue
                if st[2][0] not in ("proj", "qkT"):
                    queue.append((at, st))
                lag = 0 if st[2] in (MAXI[-1], ("mT",)) else LAG
                while queue and queue[0][0] <= at - lag:
                    yield queue.pop(0)[1]
                at += 1
            assert not queue

        def later(u, n):
            return not isinstance(u, int) or u >= n

        block = ctx.enter_context(nc.Block())

        @block.sync
        def _(sp):
            def load_x(b):
                if later(b, 1):
                    sp.wait_ge(v_ready, b * NG * (T // 2))
                sp.dma_start(xT[:], xT_dram[bass.ds(b, 1)].rearrange("o p k s -> (o p) k s")
                             ).then_inc(x_loaded, 16)

            def load_stacks(u, j):
                for n, ready in enumerate((p0_ready, p1_ready, p2_ready)):
                    sp.wait_ge(ready, u * 2 + 2)
                    sp.dma_start(part_dram[n], part[n][:]).then_inc(part_stored, 16)
                sp.wait_ge(part_stored, u * 48 + 48)
                half = G * HD * S
                for stack, terms, at in ((qst, QTERM, 0), (kst, KTERM, half)):
                    t = 0
                    while t < NTERM:
                        step = terms[t + 1] - terms[t] if t + 1 < NTERM else 0
                        n = 1
                        while step >= 0 and t + n < NTERM and terms[t + n] - terms[t + n - 1] == step:
                            n += 1
                        src = bass.AP(tensor=part_dram.tensor, offset=terms[t] * 2 * half + at,
                                      ap=[[step * 2 * half, n], [G * S, HD], [1, G * S]])
                        sp.dma_start(stack[t * HD:(t + n) * HD, j % NG].rearrange("p h s -> p (h s)"),
                                     src).then_inc(stack_loaded[j % 2], 16)
                        t += n

            def load_m(u, j):
                sp.wait_ge(m_ready, u * 3 + 3)
                for n in range(3):
                    sp.dma_start(qst[KROWS + n:KROWS + n + 1, j % NG, :, :].rearrange("o h (q i) -> o (h q) i", i=P),
                                 mpart[n][:]).then_inc(m_loaded, 16)

            def store(u, j, b):
                sp.wait_ge(cn_ready, u + 1)
                sp.dma_start(ctx_dram[bass.ds(b * S, S), j * G * HD:(j + 1) * G * HD]
                             .rearrange("(t p) d -> p t d", p=P), cn[:, j % 2]).then_inc(cn_stored[j % 2], 16)

            load_x(0)
            for dst, name in ((wqkv, "wqkv"), (ident, "ident"), (cos, "cos"), (sin, "sin")):
                sp.dma_start(dst[:], cst[name]).then_inc(w_loaded, 16)

            def body(u, i, j, with_max, with_proj):
                if later(u, 1):
                    store(u - 1, (j - 1) % NG, i if j else i - 1)
                if with_proj:
                    if later(u, -1):
                        sp.wait_ge(stack_loaded[(j + 1) % 2], (i * 2 + (j + 1) // 2 + 1) * 16 * NSTACK)
                    load_stacks(u + 2, (j + 2) % NG)
                    if j == 1 and not (isinstance(i, int) and i == B - 1):
                        load_x(i + 1)
                if with_max:
                    load_m(u + 1, (j + 1) % NG)

            run(sp, body)
            store(NU - 1, NG - 1, B - 1)
            for n in range(2):
                sp.wait_ge(cn_stored[n], 16 * (NU // 2))

        @block.tensor
        def _(pe):
            M = nc.tensor

            def take(u, todo, r):
                k = 0
                if r < NR:
                    if isinstance(u, int) and u == -2:
                        return
                    todo = PROJ + QKT if isinstance(u, int) and u == -1 else FULL
                    r += len(todo)
                    k = -1
                it = todo[r - NR]
                if it[0] == "proj":
                    pe.wait_ge(v_ready, (u + (2 + k)) * (T // 2) + (it[1] + 1))
                elif it[0] == "qkT":
                    pe.wait_ge(flat_ready, (u + (2 + k)) * 2 + (it[1] + 1))
                elif it[0] == "mT":
                    pe.wait_ge(mr_ready, (u + (1 + k)) + 1)
                else:
                    pe.wait_ge(max_done, (u + (1 + k)) * NMAX + (MAXI.index(it) + 1))

            def proj(i, j, p, bank):
                if p == 0 and j % NG == 0:
                    pe.wait_ge(x_loaded, (i + j // NG) * 16 + 16)
                for t in range(2):
                    for k in range(KD):
                        ins = M.matmul(bank[:, t * 256:t * 256 + 3 * G * HD],
                                       xT[:, k, (2 * p + t) * P:(2 * p + t + 1) * P],
                                       wqkv[:, k, j % NG, :], start=(k == 0), stop=(k == KD - 1))
                ins.then_inc(ring_full, 1)

            def qkT(u, c, bank):
                pe.wait_ge(qk_ready, u * 2 + c + 1)
                for t in range(4):
                    ins = M.transpose(bank[:, t * P:(t + 1) * P], qk[:, 4 * c + t, :], ident[:])
                ins.then_inc(ring_full, 1)

            def maxi(u, i, j, it, bank):
                if it == MAXI[0]:
                    pe.wait_ge(stack_loaded[j % 2], (i * 2 + (j // 2 + 1)) * (16 * NSTACK))
                kind, qt, h0, per, k0, keys = it
                for h in range(h0, h0 + per):
                    c = (h - h0) * keys
                    ins = M.matmul(bank[:, c:c + keys], qst[0:KROWS, j % NG, h, qt * P:(qt + 1) * P],
                                   kst[0:KROWS, j % NG, h, k0:k0 + keys], start=True, stop=True)
                ins.then_inc(ring_full, 1)

            def mT(u, bank):
                pe.wait_ge(mx_ready, u + 1)
                M.transpose(bank[0:G * T, 0:P], mx[:], ident[:]).then_inc(ring_full, 1)

            def piece(u, j, q, kt, h, c, e):
                if q == 0:
                    pe.wait_ge(m_loaded, u * 48 + 48)
                if later(u, 1) or q >= NS:
                    pe.wait_ge(exped, u * NP + q - NS + 1)
                M.matmul(st_ps[q % NS][:, 0:e - c], kst[0:KROWS + MROWS, j, h, kt * P:(kt + 1) * P],
                         qst[0:KROWS + MROWS, j, h, kt * P + c:kt * P + e],
                         start=True, stop=True).then_inc(st_full, 1)

            def pv(u, g, kt):
                pe.wait_ge(exped, u * NP + UPTO[kt])
                if kt == 0 and later(u, 1):
                    pe.wait_ge(cn_ready, u)
                q0 = kt * P
                for c0, c1 in ((q0, 512), (max(q0, 512), S)):
                    if c0 >= c1:
                        continue
                    for h in range(G):
                        ins = M.matmul(o_ps[32 * h:32 * h + 32, c0:c1], vst[:, g, kt, h, :],
                                       prob[:, (kt * G + h) % PS, c0 - q0:c1 - q0],
                                       start=(kt == 0), stop=(kt == (3 if c1 == 512 else T - 1)))
                ins.then_inc(pv_done, 1)

            def back(u):
                pe.wait_ge(oT_ready, u + 1)
                for t in range(T):
                    ins = M.transpose(o_ps[:, t * P:(t + 1) * P], oT[:, t * P:(t + 1) * P], ident[:])
                ins.then_inc(o_ready, 1)

            def body(u, i, j, with_max, with_proj):
                todo = ring_items(with_max, with_proj)
                for st in plan(u, with_max, with_proj):
                    if st[0] == "piece":
                        piece(u, j, st[1], *st[2])
                    elif st[0] == "pv":
                        pv(u, j, st[1])
                    elif st[0] == "last":
                        pv(u - 1, (j - 1) % NG, T - 1)
                    elif st[0] == "back":
                        back(u - 1)
                    elif st[0] == "ring":
                        r, it = st[1:]
                        bank = ring[r % NR]
                        take(u, todo, r)
                        if it[0] == "proj":
                            proj(i, j + 2, it[1], bank)
                        elif it[0] == "qkT":
                            qkT(u + 2, it[1], bank)
                        elif it[0] == "mT":
                            mT(u + 1, bank)
                        else:
                            maxi(u + 1, i, j + 1, it, bank)

            pe.wait_ge(w_loaded, 16 * NW)
            pe.wait_ge(kones, 1)
            pe.wait_ge(vones, 2)
            run(pe, body)
            pv(NU - 1, NG - 1, T - 1)
            back(NU - 1)

        @block.vector
        def _(v):
            V = nc.vector
            V.memset(mp[:], LOWEST).then_inc(mp_set, 1)
            v.wait_ge(mp_set, 1)
            V.memset(kst[KROWS:KROWS + MROWS].rearrange("p a h s -> p (a h s)"), 1.0).then_inc(kones, 1)
            v.wait_ge(bias_loaded, 16 * 2 * H)

            def maxi(u, j, it, bank):
                kind, qt, h0, per, k0, keys = it
                bank = bank[:, 0:per * keys].rearrange("p (h k) -> p h k", h=per)
                out = mp[:].rearrange("p (h q) n -> p h q n", h=G)[:, h0:h0 + per, qt, :]
                if kind == "near":
                    wn = min(2 * P, keys)
                    if keys > wn:
                        V.tensor_reduce(out[:, :, 1], bank[:, :, 0:keys - wn], AX.X, ALU.max)
                    else:
                        v.sem_inc(passed, 1)
                    for h in range(per):
                        ins = V.tensor_tensor_reduce(
                            out=bank[:, h, keys - wn:keys], in0=bank[:, h, keys - wn:keys],
                            in1=biasT[:, (j % NG) * G + h0 + h, 2 * P - wn:2 * P],
                            scale=1.0, scalar=LOWEST, op0=ALU.add, op1=ALU.max,
                            accum_out=out[:, h, 0:1])
                else:
                    ins = V.tensor_reduce(out[:, :, 2], bank, AX.X, ALU.max)
                ins.then_inc(max_done, 1)
                if it == MAXI[-1]:
                    v.wait_ge(max_done, u * NMAX + NMAX)
                    V.tensor_reduce(mx[:], mp[:], AX.X, ALU.max).then_inc(mx_ready, 1)

            def mT(u, bank):
                if later(u, 1):
                    v.wait_ge(m_loaded, u * 48)
                src = bank[0:G * T, 0:P]
                V.tensor_scalar(mpart[0][:], src, -1.0, None, ALU.mult).then_inc(m_ready, 1)
                v.wait_ge(m_ready, u * 3 + 1)
                V.scalar_tensor_tensor(out=mr[:], in0=src, scalar=-1.0, in1=mpart[0][:], op0=ALU.mult,
                                       op1=ALU.subtract).then_inc(mr_ready, 1)
                v.wait_ge(mr_ready, u + 1)
                V.tensor_copy(mpart[1][:], mr[:]).then_inc(m_ready, 1)
                v.wait_ge(m_ready, u * 3 + 2)
                V.tensor_tensor(mpart[2][:], mr[:], mpart[1][:], ALU.subtract).then_inc(m_ready, 1)

            def add_bias(u, j, q, kt, h):
                v.wait_ge(st_full, u * NP + q + 1)
                w = min(2 * P, S - kt * P)
                V.tensor_tensor(st_ps[q % NS][:, 0:w], st_ps[q % NS][:, 0:w],
                                bias[:, j * G + h, 0:w], ALU.add).then_inc(biased, 1)

            def norm(u, i, jj):
                j = jj % NG
                v.wait_ge(o_ready, u + 1)
                heads = o_ps.rearrange("p (h z) -> p h z", z=2 * HD)
                V.reciprocal(rs[:], heads[:, :, HD]).then_inc(rs_ready, 1)
                v.wait_ge(rs_ready, u + 1)
                if later(u, 2):
                    v.wait_ge(cn_stored[j % 2], (i * 2 + jj // 2) * 16)
                V.tensor_tensor(cn[:, j % 2].rearrange("p t (h z) -> p (t h) z", z=HD), heads[:, :, 0:HD],
                                rs[:].unsqueeze(2).to_broadcast([P, T * G, HD]), ALU.mult).then_inc(cn_ready, 1)

            def body(u, i, j, with_max, with_proj):
                for st in vector_order(plan(u, with_max, with_proj)):
                    if st[0] == "piece" and st[2][2] == 0:
                        add_bias(u, j, st[1], *st[2][:2])
                    elif st[0] == "norm":
                        norm(u - 1, i, j - 1)
                    elif st[0] == "ring" and st[2][0] not in ("proj", "qkT"):
                        r, it = st[1:]
                        v.wait_ge(ring_full, ring_no(u, r) + 1)
                        if it[0] == "mT":
                            mT(u + 1, ring[r % NR])
                        else:
                            maxi(u + 1, j + 1, it, ring[r % NR])

            run(v, body)
            norm(NU - 1, B - 1, NG - 1)

        @block.scalar
        def _(act):
            for h in range(H):
                act.dma_start(biasT[:, h, :], bass.AP(tensor=frow_dram.tensor, offset=(h * P * 2 + 1) * NREL + P - 1,
                                                      ap=[[2 * NREL - 1, P], [1, 2 * P]])).then_inc(bias_loaded, 16)
            for h in range(H):
                act.dma_start(bias[:, h, :], bass.AP(tensor=frow_dram.tensor, offset=h * P * 2 * NREL + P - 1,
                                                     ap=[[2 * NREL - 1, P], [1, 2 * P]])).then_inc(bias_loaded, 16)
            act.wait_ge(vones, 2)

            def proj(u, j, p, bank):
                src = bank.rearrange("p (t c) -> p t c", t=2)
                w = 2 * G * HD
                at = slice(2 * p, 2 * p + 2)
                nc.scalar.copy(qkf[:, at, :], src[:, :, 0:w]).then_inc(qkf_ready, 1)
                nc.scalar.copy(vst[:, j % NG, at, :, 0:HD],
                               src[:, :, w:w + G * HD].rearrange("p t (h z) -> p t h z", z=HD)).then_inc(v_ready, 1)

            def qkT(u, c, bank):
                at = slice(c * 512, (c + 1) * 512)
                if later(u, 1) and c == 0:
                    act.wait_ge(part_stored, u * 48)
                nc.scalar.copy(part[0][:, at], bank).then_inc(p0_ready, 1)
                nc.scalar.copy(rest[:, at], bank).then_inc(flat_ready, 1)

            def second(u, c):
                act.wait_ge(rest_ready, u * 2 + c + 1)
                nc.scalar.copy(part[1][:, c * 512:(c + 1) * 512],
                               rest[:, c * 512:(c + 1) * 512]).then_inc(p1_ready, 1)

            def piece(u, q, kt, h, c, e):
                if h == 0 and c == 0 and (later(u, 1) or kt >= 2):
                    act.wait_ge(pv_done, u * T + (kt - 1))
                if c == 0:
                    act.wait_ge(biased, u * (T * G) + (kt * G + h + 1))
                else:
                    act.wait_ge(st_full, u * NP + q + 1)
                nc.scalar.activation(prob[:, (kt * G + h) % PS, c:e], st_ps[q % NS][:, 0:e - c],
                                     ACT.Exp).then_inc(exped, 1)

            def copy_o(u):
                act.wait_ge(pv_done, u * T + T)
                nc.scalar.copy(oT[:], o_ps).then_inc(oT_ready, 1)

            def body(u, i, j, with_max, with_proj):
                for st in plan(u, with_max, with_proj):
                    if st[0] == "piece":
                        piece(u, st[1], *st[2])
                    elif st[0] == "last":
                        copy_o(u - 1)
                    elif st[0] == "p1":
                        second(u + 2, st[1])
                    elif st[0] == "ring" and st[2][0] in ("proj", "qkT"):
                        r, it = st[1:]
                        act.wait_ge(ring_full, ring_no(u, r) + 1)
                        if it[0] == "proj":
                            proj(u + 2, j + 2, it[1], ring[r % NR])
                        else:
                            qkT(u + 2, it[1], ring[r % NR])

            run(act, body)
            copy_o(NU - 1)

        @block.gpsimd
        def _(pool):
            nc.gpsimd.memset(vst[:], 0.0).then_inc(vones, 1)
            pool.wait_ge(vones, 1)
            nc.gpsimd.memset(vst[:, :, :, :, HD:HD + 1], 1.0).then_inc(vones, 1)
            pool.wait_ge(w_loaded, 16 * NW)

            def unit(u):
                wh = G * HD // 2

                def halves(a):
                    return a.rearrange("p t (a z) -> p t a z", a=2)

                for c in range(2):
                    at = slice(4 * c, 4 * c + 4)
                    pool.wait_ge(qkf_ready, u * 4 + (2 * c + 2))
                    if later(u, 1) or c:
                        pool.wait_ge(qk_ready, u * 2 + c)
                    nc.gpsimd.tensor_tensor(ra[:], qkf[:, at, :], cos[:, at, :], ALU.mult).then_inc(rope_step, 1)
                    for o in range(2):
                        to, of = slice(o * wh, (o + 1) * wh), slice((1 - o) * wh, (2 - o) * wh)
                        nc.gpsimd.tensor_tensor(halves(rb[:])[:, :, :, to], halves(qkf[:, at, :])[:, :, :, of],
                                                halves(sin[:, at, :])[:, :, :, to], ALU.mult).then_inc(rope_step, 1)
                    pool.wait_ge(rope_step, u * 6 + (3 * c + 3))
                    nc.gpsimd.tensor_tensor(qk[:, at, :], ra[:], rb[:], ALU.add).then_inc(qk_ready, 1)
                for c in range(2):
                    at = slice(c * 512, (c + 1) * 512)
                    pool.wait_ge(flat_ready, u * 2 + (c + 1))
                    nc.gpsimd.tensor_tensor(rest[:, at], rest[:, at], part[0][:, at],
                                            ALU.subtract).then_inc(rest_ready, 1)
                for c in range(2):
                    at = slice(c * 512, (c + 1) * 512)
                    pool.wait_ge(p1_ready, u * 2 + (c + 1))
                    nc.gpsimd.tensor_tensor(part[2][:, at], rest[:, at], part[1][:, at],
                                            ALU.subtract).then_inc(p2_ready, 1)

            unit(0)
            with pool.Fori(1, NU) as u:
                unit(u)


def phase_d(nc, x, cst, ctx_dram, ys, slots_dram, dl_dram, unused, out):
    with ExitStack() as ctx:
        def sb(name, shape, dt=F32):
            return ctx.enter_context(nc.sbuf_tensor("d_" + name, shape, dt))

        def sem(name):
            return ctx.enter_context(nc.semaphore("d_" + name))

        ps = ctx.enter_context(nc.psum_tensor("d_ps", [P, 8, 512], F32))
        ident = sb("ident", [P, P])
        wo = sb("wo", [P, KD, D])
        slot = sb("slot", [P, B, 2 * T], U32)
        yf = sb("yf", [P, B, 2 * T])
        yg = sb("yg", [P, B, 2 * T])
        yi = sb("yi", [P, B, 2 * T], U32)
        dl = sb("dl", [P, B, T])
        ex = sb("ex", [P, B, T])
        den = sb("den", [P, B, T])
        w1 = sb("w1", [P, B, T])
        w2 = sb("w2", [P, B, T])
        cx = sb("cx", [P, 2, T, D])
        xr = sb("xr", [P, 2, T, D])
        y1 = sb("y1", [P, 2, T, D])
        y2 = sb("y2", [P, 2, T, D])
        cT = sb("cT", [P, 2, D])
        fa = sb("fa", [P, 2, D])
        fb = sb("fb", [P, 2, D])
        th = sb("th", [P, 2, D])
        fc = sb("fc", [P, 2, D])
        fd = sb("fd", [P, 2, D])
        ob = sb("ob", [P, 2, T, D])

        cst_loaded = sem("cst_loaded")
        w_ready = sem("w_ready")
        w_step = sem("w_step")
        y_step = sem("y_step")
        yi_ready = sem("yi_ready")
        c_loaded = [sem(f"c_loaded{n}") for n in range(2)]
        x_loaded = [sem(f"x_loaded{n}") for n in range(2)]
        y_loaded = [sem(f"y_loaded{n}") for n in range(2)]
        cT_psum = sem("cT_psum")
        cT_ready = sem("cT_ready")
        s_psum = sem("s_psum")
        fa_ready = sem("fa_ready")
        fb_ready = sem("fb_ready")
        th_ready = sem("th_ready")
        fc_ready = sem("fc_ready")
        fd_ready = sem("fd_ready")
        o_ready = sem("o_ready")
        o_stored = [sem(f"o_stored{n}") for n in range(2)]
        block = ctx.enter_context(nc.Block())

        def old(b, n):
            return not isinstance(b, int) or b >= n

        @block.sync
        def _(sp):
            sp.dma_start(ident[:], cst["ident"]).then_inc(cst_loaded, 16)
            sp.dma_start(wo[:], cst["wo"]).then_inc(cst_loaded, 16)
            sp.dma_start(slot[:], slots_dram.rearrange("b p s -> p b s")).then_inc(cst_loaded, 16)
            sp.dma_start(dl[:], dl_dram.rearrange("b p s -> p b s")).then_inc(cst_loaded, 16)
            for b in range(B):
                j = b % 2
                if b >= 2:
                    sp.wait_ge(cT_psum, (b - 1) * T)
                    sp.wait_ge(o_ready, (b - 1) * T)
                rows = slice(b * S, (b + 1) * S)
                sp.dma_start(cx[:, j], ctx_dram[rows, :].rearrange("(t p) d -> p t d", p=P)).then_inc(c_loaded[j], 16)
                sp.dma_start(xr[:, j], x[rows, :].rearrange("(t p) d -> p t d", p=P)).then_inc(x_loaded[j], 16)
                if b >= 1:
                    sp.wait_ge(o_ready, b * T)
                    sp.dma_start(out[(b - 1) * S:b * S, :].rearrange("(t p) d -> p t d", p=P),
                                 ob[:, 1 - j]).then_inc(o_stored[1 - j], 16)
            sp.wait_ge(o_ready, B * T)
            sp.dma_start(out[(B - 1) * S:B * S, :].rearrange("(t p) d -> p t d", p=P),
                         ob[:, (B - 1) % 2]).then_inc(o_stored[(B - 1) % 2], 16)
            for n in range(2):
                sp.wait_ge(o_stored[n], 16 * (B // 2))

        @block.gpsimd
        def _(pool):
            pool.wait_ge(yi_ready, 1)
            for b in range(B):
                if b >= 2:
                    pool.wait_ge(fb_ready, (b - 1) * T)
                for t in range(T):
                    for c, y in ((0, y1), (1, y2)):
                        nc.gpsimd.indirect_dma_start(
                            y[:, b % 2, t, :], None, ys[:, :],
                            bass.IndirectOffsetOnAxis(ap=yi[:, b, c * T + t:c * T + t + 1], axis=0)
                        ).then_inc(y_loaded[b % 2], 16)

        @block.tensor
        def _(pe):
            M = nc.tensor
            pe.wait_ge(cst_loaded, 64)

            def tile(i, b, t):
                pass

            for b in range(B):
                pe.wait_ge(c_loaded[b % 2], 16 * (b // 2 + 1))
                for t in range(T):
                    i = b * T + t
                    if i >= 2:
                        pe.wait_ge(cT_ready, i - 1)
                    for k in range(KD):
                        ins = M.transpose(ps[:, i % 2, k * P:(k + 1) * P], cx[:, b % 2, t, k * P:(k + 1) * P], ident[:])
                    ins.then_inc(cT_psum, 1)
                    pe.wait_ge(cT_ready, i + 1)
                    if i >= 2:
                        pe.wait_ge(fd_ready, i - 1)
                    for k in range(KD):
                        ins = M.matmul(ps[:, 2 + i % 2, 0:D], cT[:, i % 2, k * P:(k + 1) * P], wo[:, k, :],
                                       start=(k == 0), stop=(k == KD - 1))
                    ins.then_inc(s_psum, 1)

        @block.scalar
        def _(act):
            act.wait_ge(cst_loaded, 64)
            nc.scalar.activation(ex[:], dl[:], ACT.Exp).then_inc(w_step, 1)
            for i in range(NT):
                act.wait_ge(cT_psum, i + 1)
                if i >= 2:
                    act.wait_ge(s_psum, i - 1)
                nc.scalar.copy(cT[:, i % 2, :], ps[:, i % 2, 0:D]).then_inc(cT_ready, 1)
                act.wait_ge(fb_ready, i + 1)
                if i >= 2:
                    act.wait_ge(fc_ready, i - 1)
                nc.scalar.activation(th[:, i % 2, :], fb[:, i % 2, :], ACT.Tanh, scale=0.5).then_inc(th_ready, 1)

        @block.vector
        def _(v):
            V = nc.vector
            v.wait_ge(cst_loaded, 64)
            V.tensor_copy(yf[:], slot[:]).then_inc(y_step, 1)
            v.wait_ge(y_step, 1)
            for e in range(1, E):
                V.tensor_scalar(yg[:], slot[:], float(e * QCAP), None, ALU.is_ge).then_inc(y_step, 1)
                v.wait_ge(y_step, 2 * e)
                V.scalar_tensor_tensor(out=yf[:], in0=yg[:], scalar=unused[:, e - 1:e], in1=yf[:],
                                       op0=ALU.mult, op1=ALU.subtract, reverse1=True).then_inc(y_step, 1)
                v.wait_ge(y_step, 2 * e + 1)
            V.tensor_copy(yi[:], yf[:]).then_inc(yi_ready, 1)
            v.wait_ge(w_step, 1)
            V.tensor_scalar(den[:], ex[:], 1.0, None, ALU.add).then_inc(w_step, 1)
            v.wait_ge(w_step, 2)
            V.reciprocal(den[:], den[:]).then_inc(w_step, 1)
            v.wait_ge(w_step, 3)
            V.tensor_scalar(w1[:], den[:], 0.5, None, ALU.mult).then_inc(w_step, 1)
            v.wait_ge(w_step, 4)
            V.tensor_tensor(w2[:], w1[:], ex[:], ALU.mult).then_inc(w_step, 1)
            v.wait_ge(w_step, 5)

            def mix(i):
                b, t = i // T, i % T
                if t == 0:
                    v.wait_ge(y_loaded[b % 2], 32 * T * (b // 2 + 1))
                    v.wait_ge(x_loaded[b % 2], 16 * (b // 2 + 1))
                V.tensor_scalar(fa[:, i % 2, :], y1[:, b % 2, t, :], w1[:, b, t:t + 1], None,
                                ALU.mult).then_inc(fa_ready, 1)
                v.wait_ge(fa_ready, i + 1)
                V.scalar_tensor_tensor(out=fb[:, i % 2, :], in0=y2[:, b % 2, t, :], scalar=w2[:, b, t:t + 1],
                                       in1=fa[:, i % 2, :], op0=ALU.mult, op1=ALU.add).then_inc(fb_ready, 1)

            def gate(i):
                b, t = i // T, i % T
                v.wait_ge(th_ready, i + 1)
                V.scalar_tensor_tensor(out=fc[:, i % 2, :], in0=th[:, i % 2, :], scalar=1.0,
                                       in1=fb[:, i % 2, :], op0=ALU.add, op1=ALU.mult).then_inc(fc_ready, 1)
                v.wait_ge(fc_ready, i + 1)
                v.wait_ge(s_psum, i + 1)
                V.tensor_tensor(fd[:, i % 2, :], ps[:, 2 + i % 2, 0:D], fc[:, i % 2, :],
                                ALU.mult).then_inc(fd_ready, 1)
                v.wait_ge(fd_ready, i + 1)
                if t == 0 and b >= 2:
                    v.wait_ge(o_stored[b % 2], 16 * (b // 2))
                V.scalar_tensor_tensor(out=ob[:, b % 2, t, :], in0=fd[:, i % 2, :], scalar=0.5,
                                       in1=xr[:, b % 2, t, :], op0=ALU.mult, op1=ALU.add).then_inc(o_ready, 1)

            for i in range(NT + 1):
                if i < NT:
                    mix(i)
                if i:
                    gate(i - 1)


def build(nc, x, cst, out):
    xs = nc.dram_tensor("queue_x", [NROW, D], F32, kind="Internal").ap()
    ys = nc.dram_tensor("tiles_y", [NX * P, D], F32, kind="Internal").ap()
    xT_dram = nc.dram_tensor("xT", [B, P, KD, S], F32, kind="Internal").ap()
    slots_dram = nc.dram_tensor("slots", [B, P, 2 * T], U32, kind="Internal").ap()
    dl_dram = nc.dram_tensor("logit_diff", [B, P, T], F32, kind="Internal").ap()
    fvec_dram = nc.dram_tensor("bias_by_distance", [H, 2, NREL], F32, kind="Internal").ap()
    frow_dram = nc.dram_tensor("bias_rows", [H, P, 2, NREL], F32, kind="Internal").ap()
    part_dram = nc.dram_tensor("parts", [3, P, S], BF16, kind="Internal").ap()
    ctx_dram = nc.dram_tensor("context", [B * S, D], F32, kind="Internal").ap()
    with nc.sbuf_tensor("tile_table", [1, 2, NX], I32) as tab, nc.sbuf_tensor("unused", [P, E], F32) as unused:
        phase_a(nc, x, cst, xs, xT_dram, slots_dram, dl_dram, fvec_dram, frow_dram, tab, unused)
        phase_b(nc, cst, xs, ys, tab)
        phase_c(nc, cst, xT_dram, frow_dram, part_dram, ctx_dram)
        phase_d(nc, x, cst, ctx_dram, ys, slots_dram, dl_dram, unused, out)


def shape_constants():
    import math

    import numpy as np

    f32 = np.float32
    inv = (f32(1.0) / np.power(f32(10000.0), np.arange(0, HD, 2, dtype=f32) / f32(HD))).astype(f32)
    ang = np.outer(np.arange(S, dtype=f32), inv).astype(f32)
    cos, sin = np.cos(ang), np.sin(ang)
    c16 = np.concatenate([cos, cos], 1)
    s16 = np.concatenate([-sin, sin], 1)
    scale = f32(1.0 / math.sqrt(HD))

    def rope_table(t):
        q = np.repeat(t * scale, G, axis=1)
        k = np.repeat(t, G, axis=1)
        return np.ascontiguousarray(np.concatenate([q, k], 1).reshape(T, P, 2 * G * HD).transpose(1, 0, 2)).astype(f32)

    dist = np.arange(NREL) - (P - 1)
    rp = np.maximum(dist, 0)
    exact = NBUCKET // 2
    large = exact + (np.log(np.maximum(rp.astype(f32), f32(1.0)) / f32(exact)) / f32(math.log(128 / exact))
                     * f32(NBUCKET - exact)).astype(np.int32)
    bucket = np.where(rp < exact, rp, np.minimum(large, NBUCKET - 1))
    fone = np.zeros((NBUCKET + 1, NREL), f32)
    seen = dist >= 0
    fone[bucket[seen], np.nonzero(seen)[0]] += 1.0
    fone[NBUCKET - 1, seen] -= 1.0
    fone[NBUCKET, ~seen] = -BIG
    back = 2 * P - 1 - np.arange(NREL) + (P - 1)
    fone = np.stack([fone, fone[:, np.maximum(back, 0)]], 1)
    e = np.arange(E, dtype=f32)
    return {
        "ident": np.eye(P, dtype=f32),
        "lower": np.triu(np.ones((P, P), f32), 1),
        "rev": np.ascontiguousarray(np.broadcast_to(E - e, (P, T, E))).astype(f32),
        "eoff": np.ascontiguousarray(np.broadcast_to(e * QCAP, (P, T, E))).astype(f32),
        "fone": fone,
        "cos": rope_table(c16),
        "sin": rope_table(s16),
    }


def kernel(L0_attn_x, L0_attn_Wq, L0_attn_Wk, L0_attn_Wv, L0_attn_Wo, L0_attn_rel_emb,
           L0_ffn_router_weight, L0_ffn_gate_up_proj, L0_ffn_down_proj):
    import numpy as np
    import concourse.bacc as bacc
    from concourse.bass_utils import run_bass_kernel_spmd

    def rows(w):
        return np.ascontiguousarray(np.asarray(w).reshape(KD, P, -1).transpose(1, 0, 2))

    wq, wk = (np.asarray(w).reshape(D, NG, G, HD).transpose(0, 1, 3, 2).reshape(D, NG, G * HD)
              for w in (L0_attn_Wq, L0_attn_Wk))
    wv = np.asarray(L0_attn_Wv).reshape(D, NG, G * HD)
    qkv = np.concatenate([wq, wk, wv], 2)
    gu = np.asarray(L0_ffn_gate_up_proj).transpose(2, 0, 1).reshape(KD, P, E, 2 * F).transpose(1, 2, 0, 3)
    dn = np.asarray(L0_ffn_down_proj).transpose(2, 0, 1).reshape(KD, P, E, D).transpose(1, 2, 0, 3)
    data = {
        "x": np.ascontiguousarray(np.asarray(L0_attn_x).reshape(B * S, D)),
        "wqkv": np.ascontiguousarray(qkv.reshape(KD, P, NG, 3 * G * HD).transpose(1, 0, 2, 3)),
        "wo": rows(L0_attn_Wo),
        "wr": rows(np.asarray(L0_ffn_router_weight).T),
        "rel": np.ascontiguousarray(np.asarray(L0_attn_rel_emb)),
        "wgu": np.ascontiguousarray(gu),
        "wd": np.ascontiguousarray(dn),
    }
    data.update(shape_constants())

    nc = bacc.Bacc("TRN2", target_bir_lowering=False, num_devices=1)
    aps = {n: nc.dram_tensor("in_" + n, a.shape, mybir.dt.from_np(a.dtype), kind="ExternalInput").ap()
           for n, a in data.items()}
    out = nc.dram_tensor("out", [B * S, D], F32, kind="ExternalOutput").ap()
    build(nc, aps["x"], aps, out)
    res = run_bass_kernel_spmd(nc, [{"in_" + n: a for n, a in data.items()}], core_ids=[0])
    return res.results[0]["out"].reshape(B, S, D)
```

```python
from contextlib import ExitStack

import concourse.bass as bass
from concourse import mybir

F32 = mybir.dt.float32
BF16 = mybir.dt.bfloat16
I32 = mybir.dt.int32
U32 = mybir.dt.uint32
ALU = mybir.AluOpType
ACT = mybir.ActivationFunctionType
AX = mybir.AxisListType

P = 128
B, S, D = 8, 1024, 256
H, HD = 16, 16
G = 4
NG = H // G
T = S // P
NT = B * T
KD = D // P
E, F = 8, 256
NU = B * NG
EPS = 1e-5
BIG = 1.0e30
LOWEST = -3.0e38
NBUCKET = 32
NREL = 2 * P + P

QCAP = B * S
NX = 2 * B * S // P + E
DUMMY = E * QCAP
NROW = DUMMY + E * P

QTERM = (0, 0, 0, 1, 1, 2)
KTERM = (0, 1, 2, 0, 1, 0)
NTERM = len(QTERM)
KROWS = NTERM * HD
MROWS = 3


def ahead(nc, ctx, prefix, shapes):
    tensors = {name: ctx.enter_context(nc.sbuf_tensor(prefix + name, shape, F32))
               for name, shape in shapes.items()}
    return {"loaded": ctx.enter_context(nc.semaphore(prefix + "loaded")), **tensors}


def phase_a(nc, x, cst, ffn, att, xs, xT_dram, slots_dram, dl_dram, fvec_dram, frow_dram, tab, unused):
    with ExitStack() as ctx:
        def sb(name, shape, dt=F32):
            return ctx.enter_context(nc.sbuf_tensor("a_" + name, shape, dt))

        def sem(name):
            return ctx.enter_context(nc.semaphore("a_" + name))

        ps = ctx.enter_context(nc.psum_tensor("a_ps", [P, 8, 512], F32))
        xb = sb("xb", [P, 2, T, D])
        xn = sb("xn", [P, 2, T, D])
        xT = sb("xT", [P, 2, KD, S])
        wr = sb("wr", [P, KD, E])
        ident = att["ident"]
        lowerf = sb("lowerf", [P, P])
        lower = sb("lower", [P, P], BF16)
        ones = sb("ones", [P, P], BF16)
        rev = sb("rev", [P, T, E])
        eoff = sb("eoff", [P, T, E])
        rel = sb("rel", [NBUCKET + 1, H])
        fone = sb("fone", [NBUCKET + 1, 2, NREL])
        fsb = sb("fsb", [H, 2, NREL])
        stats = sb("stats", [P, T, 6])
        mv = sb("mv", [P, 2, T, 2])
        var = sb("var", [P, T])
        sd = sb("sd", [P, T])
        r0 = sb("r0", [P, T])
        r1 = sb("r1", [P, T])
        r2 = sb("r2", [P, T])
        r3 = sb("r3", [P, T])
        rstd = sb("rstd", [P, 2, T])
        lg = sb("lg", [P, T, E])
        lg2 = sb("lg2", [P, T, E])
        top = sb("top", [P, 2, T])
        eq = sb("eq", [P, T, E])
        code = sb("code", [P, T])
        hot = sb("hot", [P, 2, T, E])
        both = sb("both", [P, T, E], BF16)
        acum = sb("acum", [P, T + 1, E], BF16)
        pos = sb("pos", [P, T, E])
        slotf = sb("slotf", [P, 2, T])
        slot = sb("slot", [P, 2, 2 * T], U32)
        dl = sb("dl", [P, 2, T])
        zero = sb("zero", [P, D])
        cnt = sb("cnt", [P, E])
        cnti = sb("cnti", [P, E], I32)
        pcol = sb("pcol", [P, 1])
        padend = sb("padend", [P, E])
        padf = sb("padf", [P, E])
        padg = sb("padg", [P, E])
        padi = sb("padi", [P, E], U32)
        tiles = sb("tiles", [1, E])
        tend = sb("tend", [1, E + 1])
        tnum = sb("tnum", [1, NX])
        tge = sb("tge", [1, NX])
        trow = sb("trow", [1, NX])
        texp = sb("texp", [1, NX])

        x_loaded = [sem(f"x_loaded{n}") for n in range(2)]
        cst_loaded = sem("cst_loaded")
        dve = sem("dve")
        passed = sem("passed")
        ppassed = sem("ppassed")
        var_ready = sem("var_ready")
        sd_ready = sem("sd_ready")
        xn_ready = sem("xn_ready")
        xnT_psum = sem("xnT_psum")
        xT_ready = sem("xT_ready")
        xT_stored = [sem(f"xT_stored{n}") for n in range(2)]
        lg_psum = sem("lg_psum")
        lg_read = sem("lg_read")
        acum_ready = sem("acum_ready")
        pos_psum = sem("pos_psum")
        pos_read = sem("pos_read")
        slot_ready = sem("slot_ready")
        slot_stored = [sem(f"slot_stored{n}") for n in range(2)]
        scattered = [sem(f"scattered{n}") for n in range(2)]
        zero_ready = sem("zero_ready")
        iota_ready = sem("iota_ready")
        cnt_psum = sem("cnt_psum")
        pad_ready = sem("pad_ready")
        pad_done = sem("pad_done")
        f_psum = sem("f_psum")
        f_ready = sem("f_ready")
        f_stored = sem("f_stored")
        dummy_done = sem("dummy_done")

        CST = 16 * 7

        def pairs(eng, body):
            for j in range(2):
                body(0, j, False)
            with eng.Fori(1, B // 2 - 1) as i:
                for j in range(2):
                    body(i, j, False)
            for j in range(2):
                body(B // 2 - 1, j, j == 1)

        block = ctx.enter_context(nc.Block())

        @block.sync
        def _(sp):
            for dst, name in ((wr, "wr"), (ident, "ident"), (lowerf, "lower"),
                              (rev, "rev"), (eoff, "eoff"), (fone, "fone")):
                sp.dma_start(dst[:], cst[name]).then_inc(cst_loaded, 16)
            sp.dma_start(rel[0:NBUCKET, :], cst["rel"]).then_inc(cst_loaded, 16)

            def load(blk, j):
                sp.dma_start(xb[:, j], x[bass.ds(blk * S, S), :].rearrange("(t p) d -> p t d", p=P)
                             ).then_inc(x_loaded[j], 16)

            def store(blk, j):
                sp.wait_ge(xT_ready, blk * 4 + 4)
                sp.dma_start(xT_dram[bass.ds(blk, 1)].rearrange("o p k s -> (o p) k s"),
                             xT[:, j]).then_inc(xT_stored[j], 16)
                sp.wait_ge(slot_ready, blk + 1)
                sp.dma_start(slots_dram[bass.ds(blk, 1)].rearrange("o p s -> (o p) s"),
                             slot[:, j]).then_inc(slot_stored[j], 16)
                sp.dma_start(dl_dram[bass.ds(blk, 1)].rearrange("o p s -> (o p) s"),
                             dl[:, j]).then_inc(slot_stored[j], 16)

            load(0, 0)
            load(1, 1)
            sp.wait_ge(f_ready, 1)
            sp.dma_start(fvec_dram.rearrange("(h c) r -> h c r", c=2), fsb[:]).then_inc(f_stored, 16)
            sp.wait_ge(zero_ready, 1)
            for e in range(E):
                sp.dma_start(xs[DUMMY + e * P:DUMMY + (e + 1) * P, :], zero[:]).then_inc(dummy_done, 16)

            def for_later(blk):
                sp.dma_start(ffn["wgu"][:, bass.ds(blk, 1)], cst["wgu"][:, bass.ds(blk, 1)]).then_inc(ffn["loaded"], 16)
                sp.dma_start(ffn["wd"][:, bass.ds(blk, 1)], cst["wd"][:, bass.ds(blk, 1)]).then_inc(ffn["loaded"], 16)
                share = 2 * H // B
                sp.dma_start(frow_dram[bass.ds(blk * share, share)],
                             fvec_dram[bass.ds(blk * share, share), :].unsqueeze(1).to_broadcast([share, P, NREL])
                             ).then_inc(f_stored, 16)

            sp.wait_ge(f_stored, 16)
            with sp.Fori(0, B // 2 - 1) as i:
                for j in range(2):
                    blk = i * 2 + j
                    store(blk, j)
                    sp.wait_ge(xn_ready, blk * T + T)
                    load(blk + 2, j)
                    for_later(blk)
            for j in range(2):
                store(B - 2 + j, j)
                for_later(B - 2 + j)
            for j in range(2):
                sp.wait_ge(xT_stored[j], 16 * (B // 2))
                sp.wait_ge(slot_stored[j], 32 * (B // 2))
            sp.wait_ge(f_stored, 16 + 16 * B)
            sp.wait_ge(dummy_done, 16 * E)

        @block.gpsimd
        def _(pool):
            nc.gpsimd.memset(zero[:], 0.0).then_inc(zero_ready, 1)
            nc.gpsimd.iota(pcol[:], [[0, 1]], channel_multiplier=1,
                           allow_small_or_imprecise_dtypes=True).then_inc(iota_ready, 1)
            nc.gpsimd.iota(tnum[:], [[1, NX]], channel_multiplier=0,
                           allow_small_or_imprecise_dtypes=True).then_inc(iota_ready, 1)

            def scatter(blk, j):
                pool.wait_ge(xn_ready, blk * T + T)
                pool.wait_ge(slot_ready, blk + 1)
                pool.sem_inc(ppassed, 1)
                for c in range(2):
                    for t in range(T):
                        nc.gpsimd.indirect_dma_start(
                            xs[:, :], bass.IndirectOffsetOnAxis(ap=slot[:, j, c * T + t:c * T + t + 1], axis=0),
                            xn[:, j, t, :], None).then_inc(scattered[j], 16)

            with pool.Fori(0, B // 2) as i:
                for j in range(2):
                    scatter(i * 2 + j, j)
            pool.wait_ge(zero_ready, 1)
            pool.wait_ge(pad_ready, 1)
            for e in range(E):
                nc.gpsimd.indirect_dma_start(
                    xs[:, :], bass.IndirectOffsetOnAxis(ap=padi[:, e:e + 1], axis=0),
                    zero[:], None, bounds_check=NROW - 1, oob_is_err=False).then_inc(pad_done, 16)
            for j in range(2):
                pool.wait_ge(scattered[j], 16 * NT)
            pool.wait_ge(pad_done, 16 * E)

        @block.scalar
        def _(act):
            def root(blk):
                act.wait_ge(var_ready, blk + 1)
                nc.scalar.activation(sd[:], var[:], ACT.Sqrt).then_inc(sd_ready, 1)

            root(0)

            def block_(i, j, last):
                blk = i * 2 + j
                if not isinstance(i, int) or i:
                    act.wait_ge(xT_stored[j], i * 16)
                for c in range(4):
                    act.wait_ge(xnT_psum, blk * 4 + c + 1)
                    nc.scalar.copy(xT[:, j, :, c * 256:(c + 1) * 256],
                                   ps[:, c % 2, :].rearrange("p (k s) -> p k s", k=KD)
                                   ).then_inc(xT_ready, 1)
                    if c == 2 and not last:
                        root(blk + 1)

            pairs(act, block_)

        @block.vector
        def _(v):
            n = [0]
            V = nc.vector

            def seq(ins):
                ins.then_inc(dve, 1)
                n[0] += 1
                v.wait_ge(dve, base[0] + n[0])
                return ins

            base = [0]
            seq(V.memset(acum[:], 0.0))
            seq(V.memset(rel[NBUCKET:NBUCKET + 1, :], 1.0))
            v.wait_ge(cst_loaded, CST)
            seq(V.tensor_copy(lower[:], lowerf[:]))
            seq(V.memset(ones[:], 1.0))
            v.wait_ge(f_psum, 1)
            V.tensor_copy(fsb[:], ps[0:H, 4:6, 0:NREL]).then_inc(f_ready, 1)

            def norms(i, j):
                v.wait_ge(x_loaded[j % 2], i * 16 + (j // 2 + 1) * 16)
                blk, j = i * 2 + j, j % 2
                for t in range(T):
                    V.bn_stats(stats[:, t, :], xb[:, j, t, :]).then_inc(dve, 1)
                    n[0] += 1
                v.wait_ge(dve, base[0] + n[0])
                v.sem_inc(passed, 1)
                for t in range(T):
                    V.bn_aggr(mv[:, j, t, :], stats[:, t, :]).then_inc(dve, 1)
                    n[0] += 1
                v.wait_ge(dve, base[0] + n[0])
                V.tensor_scalar(var[:], mv[:, j, :, 1], EPS, None, ALU.add).then_inc(var_ready, 1)
                v.wait_ge(var_ready, blk + 1)
                v.wait_ge(sd_ready, blk + 1)
                seq(V.reciprocal(r0[:], sd[:]))
                seq(V.tensor_tensor(r1[:], r0[:], r0[:], ALU.mult))
                seq(V.tensor_tensor(r2[:], r1[:], var[:], ALU.mult))
                seq(V.tensor_scalar(r3[:], r2[:], -0.5, 1.5, ALU.mult, ALU.add))
                seq(V.tensor_tensor(rstd[:, j, :], r0[:], r3[:], ALU.mult))

            def block_(i, j, last):
                blk = i * 2 + j
                if not isinstance(i, int) or i:
                    v.wait_ge(scattered[j], i * (16 * 2 * T))
                    v.wait_ge(xnT_psum, blk * 4 - 4)
                for t in range(T):
                    V.tensor_scalar(xn[:, j, t, :], xb[:, j, t, :], mv[:, j, t, 0:1], rstd[:, j, t:t + 1],
                                    ALU.subtract, ALU.mult).then_inc(xn_ready, 1)
                if not last:
                    norms(i, j + 1)
                v.wait_ge(lg_psum, blk + 1)
                seq(V.tensor_copy(lg[:], ps[:, 2, 0:T * E].rearrange("p (t e) -> p t e", t=T)))
                V.tensor_copy(lg2[:], lg[:]).then_inc(lg_read, 1)
                v.wait_ge(lg_read, blk + 1)
                for c, src in ((0, lg), (1, lg2)):
                    if c == 1:
                        seq(V.scalar_tensor_tensor(out=lg2[:], in0=hot[:, 0], scalar=LOWEST,
                                                   in1=lg[:], op0=ALU.mult, op1=ALU.add))
                    seq(V.tensor_reduce(top[:, c, :], src[:], AX.X, ALU.max))
                    seq(V.tensor_tensor(eq[:], src[:], top[:, c, :].unsqueeze(2).to_broadcast([P, T, E]),
                                        ALU.is_equal))
                    seq(V.tensor_tensor(eq[:], eq[:], rev[:], ALU.mult))
                    seq(V.tensor_reduce(code[:], eq[:], AX.X, ALU.max))
                    seq(V.tensor_tensor(hot[:, c], rev[:], code[:].unsqueeze(2).to_broadcast([P, T, E]),
                                        ALU.is_equal))
                seq(V.tensor_tensor(both[:], hot[:, 0], hot[:, 1], ALU.add))
                for t in range(T):
                    ins = V.tensor_tensor(acum[:, t + 1, :], acum[:, t, :], both[:, t, :], ALU.add)
                    if t < T - 1:
                        seq(ins)
                    else:
                        ins.then_inc(acum_ready, 1)
                v.wait_ge(pos_psum, blk + 1)
                V.tensor_tensor(pos[:], ps[:, 3, 0:T * E].rearrange("p (t e) -> p t e", t=T), eoff[:],
                                ALU.add).then_inc(pos_read, 1)
                v.wait_ge(pos_read, blk + 1)
                v.wait_ge(acum_ready, blk + 1)
                seq(V.tensor_copy(acum[:, 0, :], acum[:, T, :]))
                if not isinstance(i, int) or i:
                    v.wait_ge(slot_stored[j], i * 32)
                for c in range(2):
                    seq(V.tensor_tensor(eq[:], hot[:, c], pos[:], ALU.mult))
                    seq(V.tensor_reduce(slotf[:, c, :], eq[:], AX.X, ALU.add))
                seq(V.tensor_tensor(dl[:, j, :], top[:, 1, :], top[:, 0, :], ALU.subtract))
                V.tensor_copy(slot[:, j, :], slotf[:].rearrange("p c t -> p (c t)")).then_inc(slot_ready, 1)

            norms(0, 0)
            start = n[0]
            for j in range(2):
                block_(0, j, False)
            per = n[0] - start
            with v.Fori(1, B // 2 - 1) as i:
                n[0] = 0
                base[0] = i * per + start
                for j in range(2):
                    block_(i, j, False)
            assert n[0] == per
            n[0] = 0
            base[0] = start + per * (B // 2 - 1)
            for j in range(2):
                block_(B // 2 - 1, j, j == 1)

            v.wait_ge(cnt_psum, 1)
            v.wait_ge(iota_ready, 2)
            seq(V.tensor_copy(cnt[:], ps[:, 3, 0:E]))
            seq(V.tensor_scalar(padf[:], cnt[:], float(P - 1), None, ALU.add))
            seq(V.tensor_copy(cnti[:], padf[:]))
            seq(V.tensor_scalar(cnti[:], cnti[:], 7, 7, ALU.logical_shift_right, ALU.logical_shift_left))
            seq(V.tensor_copy(padend[:], cnti[:]))
            seq(V.tensor_scalar(padf[:], cnt[:], pcol[:, 0:1], None, ALU.add))
            seq(V.tensor_tensor(padg[:], padf[:], padend[:], ALU.is_ge))
            seq(V.tensor_tensor(padf[:], padf[:], eoff[:, 0, :], ALU.add))
            seq(V.scalar_tensor_tensor(out=padf[:], in0=padg[:], scalar=float(1 << 20), in1=padf[:],
                                       op0=ALU.mult, op1=ALU.add))
            V.tensor_copy(padi[:], padf[:]).then_inc(pad_ready, 1)
            seq(V.tensor_scalar(tiles[:], padend[0:1, :], 1.0 / P, None, ALU.mult))
            seq(V.tensor_scalar(unused[:], padend[:], -1.0, float(QCAP), ALU.mult, ALU.add))
            seq(V.memset(tend[:], 0.0))
            for e in range(E):
                seq(V.tensor_tensor(tend[:, e + 1:e + 2], tend[:, e:e + 1], tiles[:, e:e + 1], ALU.add))
            seq(V.tensor_scalar(trow[:], tnum[:], float(P), None, ALU.mult))
            seq(V.memset(texp[:], 0.0))
            for e in range(1, E + 1):
                seq(V.tensor_scalar(tge[:], tnum[:], tend[:, e:e + 1], None, ALU.is_ge))
                seq(V.scalar_tensor_tensor(out=trow[:], in0=tge[:], scalar=unused[0:1, e - 1:e], in1=trow[:],
                                           op0=ALU.mult, op1=ALU.add))
                if e < E:
                    seq(V.tensor_tensor(texp[:], texp[:], tge[:], ALU.add))
            seq(V.tensor_copy(tab[:, 0, :], trow[:]))
            seq(V.tensor_copy(tab[:, 1, :], texp[:]))

        @block.tensor
        def _(pe):
            M = nc.tensor
            pe.wait_ge(cst_loaded, CST)
            pe.wait_ge(dve, 4)
            M.matmul(ps[0:H, 4, 0:NREL], rel[:], fone[:, 0, :], start=True, stop=True)
            M.matmul(ps[0:H, 5, 0:NREL], rel[:], fone[:, 1, :], start=True, stop=True).then_inc(f_psum, 1)

            def block_(i, j):
                blk = i * 2 + j
                past = not isinstance(blk, int) or blk >= 1
                for c in range(4):
                    pe.wait_ge(xn_ready, blk * T + 2 * c + 2)
                    if past or c >= 2:
                        pe.wait_ge(xT_ready, blk * 4 + c - 1)
                    for k in range(KD):
                        for h in range(2):
                            ins = M.transpose(ps[:, c % 2, k * 256 + h * P:k * 256 + (h + 1) * P],
                                              xn[:, j, 2 * c + h, k * P:(k + 1) * P], ident[:])
                    ins.then_inc(xnT_psum, 1)
                if past:
                    pe.wait_ge(lg_read, blk)
                for t in range(T):
                    if t % 2 == 0:
                        pe.wait_ge(xT_ready, blk * 4 + t // 2 + 1)
                    for k in range(KD):
                        ins = M.matmul(ps[:, 2, t * E:(t + 1) * E], xT[:, j, k, t * P:(t + 1) * P],
                                       wr[:, k, :], start=(k == 0), stop=(k == KD - 1))
                ins.then_inc(lg_psum, 1)
                pe.wait_ge(acum_ready, blk + 1)
                if past:
                    pe.wait_ge(pos_read, blk)
                M.matmul(ps[:, 3, 0:T * E], lower[:], both[:].rearrange("p t e -> p (t e)"),
                         start=True, stop=False)
                M.matmul(ps[:, 3, 0:T * E], ones[:], acum[:, 0:T, :].rearrange("p t e -> p (t e)"),
                         start=False, stop=True).then_inc(pos_psum, 1)

            for j in range(2):
                block_(0, j)
            with pe.Fori(1, B // 2) as i:
                for j in range(2):
                    block_(i, j)
            pe.wait_ge(pos_read, B)
            M.matmul(ps[:, 3, 0:E], ones[:], acum[:, T, :], start=True, stop=True).then_inc(cnt_psum, 1)


def phase_b(nc, cst, ffn, att, frow_dram, xT_dram, xs, ys, tab):
    U = 4
    with ExitStack() as ctx:
        def sb(name, shape, dt=F32):
            return ctx.enter_context(nc.sbuf_tensor("b_" + name, shape, dt))

        def sem(name):
            return ctx.enter_context(nc.semaphore("b_" + name))

        ps = ctx.enter_context(nc.psum_tensor("b_ps", [P, 8, 512], F32))
        xt_ps, gu_ps, ht_ps, y_ps = (ps[:, 2 * n:2 * n + 2] for n in range(4))
        wgu, wd, ident = ffn["wgu"], ffn["wd"], att["ident"]
        xt = sb("xt", [P, U, D])
        xT = sb("xT", [P, 2, KD, P])
        th = sb("th", [P, 2, F])
        ga = sb("ga", [P, 2, F])
        h = sb("h", [P, 2, F])
        hT = sb("hT", [P, 2, KD, P])
        y = sb("y", [P, 2, D])

        x_loaded = [sem(f"x_loaded{n}") for n in range(U)]
        xT_psum = sem("xT_psum")
        xT_ready = sem("xT_ready")
        gu_psum = sem("gu_psum")
        th_ready = sem("th_ready")
        ga_ready = sem("ga_ready")
        h_ready = sem("h_ready")
        hT_psum = sem("hT_psum")
        hT_ready = sem("hT_ready")
        y_psum = sem("y_psum")
        y_ready = sem("y_ready")
        y_stored = [sem(f"y_stored{n}") for n in range(2)]

        def fixed(t):
            return isinstance(t, int)

        def loop(eng, body):
            for j in range(U):
                body(0, j)
            with eng.Fori(1, NX // U - 1) as i:
                for j in range(U):
                    body(i, j)
            for j in range(U):
                body(NX // U - 1, j)

        block = ctx.enter_context(nc.Block())

        @block.sync
        def _(sp):
            def body(i, j):
                t = i * U + j
                if not fixed(t) or t >= U:
                    sp.wait_ge(xT_psum, t - U + 1)
                row = nc.sync.value_load(tab[0:1, 0, bass.ds(t, 1)], min_val=0, max_val=NROW - P)
                sp.dma_start(xt[:, j, :], xs[bass.ds(row, P), :]).then_inc(x_loaded[j], 16)

            skewed = (frow_dram.rearrange("n p r -> n (p r)")[:, P - 1:P - 1 + P * (NREL - 1)]
                      .rearrange("n (p r) -> n p r", p=P))
            assert NX // U - 2 == 2 * H

            for j in range(U):
                body(0, j)
            for dst, name in ((att["wqkv"], "wqkv"), (att["cos"], "cos"), (att["sin"], "sin")):
                sp.dma_start(dst[:], cst[name]).then_inc(att["loaded"], 16)
            sp.dma_start(att["xT"][:], xT_dram[0]).then_inc(att["loaded"], 16)
            with sp.Fori(1, NX // U - 1) as i:
                for j in range(U):
                    body(i, j)
                sp.dma_start(att["bias"][:, bass.ds(i - 1, 1), :].rearrange("p o r -> p (o r)"),
                             skewed[bass.ds(i - 1, 1), :, 0:2 * P].rearrange("o p r -> (o p) r")
                             ).then_inc(att["loaded"], 16)
            for j in range(U):
                body(NX // U - 1, j)

        @block.gpsimd
        def _(pool):
            def body(i, j):
                t = i * U + j
                pool.wait_ge(y_ready, t + 1)
                pool.dma_start(ys[bass.ds(t * P, P), :], y[:, j % 2, :]).then_inc(y_stored[j % 2], 16)

            loop(pool, body)
            for n in range(2):
                pool.wait_ge(y_stored[n], 16 * (NX // 2))

        @block.tensor
        def _(pe):
            M = nc.tensor
            pe.wait_ge(ffn["loaded"], 16 * 2 * E)

            def transpose_x(i, jj):
                t, j = i * U + jj, jj % U
                pe.wait_ge(x_loaded[j], (i + jj // U) * 16 + 16)
                if not fixed(t) or t >= 2:
                    pe.wait_ge(xT_ready, t - 1)
                for k in range(KD):
                    ins = M.transpose(xt_ps[:, j % 2, k * P:(k + 1) * P], xt[:, j, k * P:(k + 1) * P], ident[:])
                ins.then_inc(xT_psum, 1)

            def gate_up(t, j, e):
                pe.wait_ge(xT_ready, t + 1)
                if not fixed(t) or t >= 2:
                    pe.wait_ge(h_ready, t - 1)
                for k in range(KD):
                    ins = M.matmul(gu_ps[:, j % 2, :], xT[:, j % 2, k, :],
                                   wgu[:, bass.ds(e, 1), k, :].rearrange("p o n -> p (o n)"),
                                   start=(k == 0), stop=(k == KD - 1))
                ins.then_inc(gu_psum, 1)

            def transpose_h(t, j):
                pe.wait_ge(h_ready, t + 1)
                if not fixed(t) or t >= 2:
                    pe.wait_ge(hT_ready, t - 1)
                for k in range(KD):
                    ins = M.transpose(ht_ps[:, j % 2, k * P:(k + 1) * P], h[:, j % 2, k * P:(k + 1) * P], ident[:])
                ins.then_inc(hT_psum, 1)

            def down(t, j, e):
                pe.wait_ge(hT_ready, t + 1)
                if not fixed(t) or t >= 2:
                    pe.wait_ge(y_ready, t - 1)
                for k in range(KD):
                    ins = M.matmul(y_ps[:, j % 2, 0:D], hT[:, j % 2, k, :],
                                   wd[:, bass.ds(e, 1), k, :].rearrange("p o n -> p (o n)"),
                                   start=(k == 0), stop=(k == KD - 1))
                ins.then_inc(y_psum, 1)

            def expert(t):
                return nc.tensor.value_load(tab[0:1, 1, bass.ds(t, 1)], min_val=0, max_val=E - 1)

            def body(i, j):
                t = i * U + j
                if not fixed(t) or t < NX - 1:
                    transpose_x(i, j + 1)
                gate_up(t, j, expert(t))
                if not fixed(t) or t >= 1:
                    transpose_h(t - 1, (j - 1) % U)
                if not fixed(t) or t >= 2:
                    down(t - 2, (j - 2) % U, expert(t - 2))

            transpose_x(0, 0)
            loop(pe, body)
            down(NX - 2, (NX - 2) % U, expert(NX - 2))
            transpose_h(NX - 1, (NX - 1) % U)
            down(NX - 1, (NX - 1) % U, expert(NX - 1))

        @block.scalar
        def _(act):
            def copy_x(t, j):
                act.wait_ge(xT_psum, t + 1)
                if not fixed(t) or t >= 2:
                    act.wait_ge(gu_psum, t - 1)
                nc.scalar.copy(xT[:, j % 2].rearrange("p k s -> p (k s)"),
                               xt_ps[:, j % 2, 0:D]).then_inc(xT_ready, 1)

            def tanh(t, j):
                act.wait_ge(gu_psum, t + 1)
                if not fixed(t) or t >= 2:
                    act.wait_ge(ga_ready, t - 1)
                nc.scalar.activation(th[:, j % 2, :], gu_ps[:, j % 2, 0:F], ACT.Tanh,
                                     scale=0.5).then_inc(th_ready, 1)

            def copy_h(t, j):
                act.wait_ge(hT_psum, t + 1)
                if not fixed(t) or t >= 2:
                    act.wait_ge(y_psum, t - 1)
                nc.scalar.copy(hT[:, j % 2].rearrange("p k s -> p (k s)"),
                               ht_ps[:, j % 2, 0:F]).then_inc(hT_ready, 1)

            def body(i, j):
                t = i * U + j
                if not fixed(t) or t < NX - 1:
                    copy_x(t + 1, (j + 1) % U)
                tanh(t, j)
                if not fixed(t) or t >= 1:
                    copy_h(t - 1, (j - 1) % U)

            copy_x(0, 0)
            loop(act, body)
            copy_h(NX - 1, (NX - 1) % U)

        @block.vector
        def _(v):
            V = nc.vector

            def swiglu(t, j):
                v.wait_ge(th_ready, t + 1)
                V.scalar_tensor_tensor(out=ga[:, j % 2, :], in0=th[:, j % 2, :], scalar=1.0,
                                       in1=gu_ps[:, j % 2, 0:F], op0=ALU.add, op1=ALU.mult).then_inc(ga_ready, 1)
                v.wait_ge(ga_ready, t + 1)
                if not fixed(t) or t >= 2:
                    v.wait_ge(hT_psum, t - 1)
                V.tensor_tensor(h[:, j % 2, :], gu_ps[:, j % 2, F:2 * F], ga[:, j % 2, :],
                                ALU.mult).then_inc(h_ready, 1)

            def copy_y(i, jj):
                t, j = i * U + jj, jj % U
                v.wait_ge(y_psum, t + 1)
                if not fixed(t) or t >= 2:
                    v.wait_ge(y_stored[j % 2], (i * (U // 2) + jj // 2) * 16)
                V.tensor_copy(y[:, j % 2, :], y_ps[:, j % 2, 0:D]).then_inc(y_ready, 1)

            def body(i, j):
                t = i * U + j
                swiglu(t, j)
                if not fixed(t) or t >= 2:
                    copy_y(i, j - 2)

            loop(v, body)
            copy_y(NX // U, -2)
            copy_y(NX // U, -1)


def phase_c(nc, att, xT_dram, part_dram, ctx_dram, slots_dram, dl_dram, unused, ys, gate_dram):
    with ExitStack() as ctx:
        def sb(name, shape, dt=F32):
            return ctx.enter_context(nc.sbuf_tensor("c_" + name, shape, dt))

        def sem(name):
            return ctx.enter_context(nc.semaphore("c_" + name))

        ps = ctx.enter_context(nc.psum_tensor("c_ps", [P, 8, 512], F32))
        NS = 3
        st_ps = [ps[:, n, :] for n in range(NS)]
        o_ps = ps[:, 3:5].rearrange("p b n -> p (b n)")
        NR = 3
        ring = [ps[:, 5 + n, :] for n in range(NR)]
        PS = 2 * G

        ident, wqkv, cos, sin = att["ident"], att["wqkv"], att["cos"], att["sin"]
        tables = att["bias"][:].rearrange("p (h c) r -> p h c r", c=2)
        bias, biasT = tables[:, :, 0], tables[:, :, 1]
        xT = att["xT"]
        qst = sb("qst", [P, NG, G, S], BF16)
        kst = sb("kst", [P, NG, G, S], BF16)
        vst = sb("vst", [P, NG, T, G, 2 * HD])
        qkf = sb("qkf", [P, T, 2 * G * HD])
        ra = sb("ra", [P, T // 2, 2 * G * HD])
        rb = sb("rb", [P, T // 2, 2 * G * HD])
        qk = qkf
        part = [sb(f"part{n}", [P, S], BF16) for n in range(3)]
        rest = sb("rest", [P, S])
        mp = sb("mp", [P, G * T, 3])
        mx = sb("mx", [P, G * T])
        mpart = [sb(f"mpart{n}", [G * T, P], BF16) for n in range(3)]
        mr = sb("mr", [G * T, P])
        prob = sb("prob", [P, PS, S])
        oT = sb("oT", [P, S])
        rs = sb("rs", [P, T * G])
        cn = sb("cn", [P, 2, T, G * HD])
        TU = NT // NU
        slot = sb("slot", [P, B, 2 * T], U32)
        yf = sb("yf", [P, B, 2 * T])
        yg = sb("yg", [P, B, 2 * T])
        dl = sb("dl", [P, B, T])
        ex = sb("ex", [P, B, T])
        w1 = sb("w1", [P, B, T])
        w2 = sb("w2", [P, B, T])
        yrow = sb("yrow", [P, NU, 2, TU])
        yw = sb("yw", [P, NU, 2, TU])
        row_now = sb("row_now", [P, 2, TU], U32)
        w_now = sb("w_now", [P, 2, TU])
        y = sb("y", [P, 2, TU, D])
        z = sb("z", [P, TU, D])

        kones = sem("kones")
        vones = sem("vones")
        mp_set = sem("mp_set")
        passed = sem("passed")
        x_loaded = sem("x_loaded")
        ring_full = sem("ring_full")
        qkf_ready = sem("qkf_ready")
        v_ready = sem("v_ready")
        rope_step = sem("rope_step")
        qk_ready = sem("qk_ready")
        p0_ready = sem("p0_ready")
        flat_ready = sem("flat_ready")
        rest_ready = sem("rest_ready")
        p1_ready = sem("p1_ready")
        p2_ready = sem("p2_ready")
        part_stored = sem("part_stored")
        stack_loaded = [sem(f"stack_loaded{n}") for n in range(2)]
        max_done = sem("max_done")
        mx_ready = sem("mx_ready")
        mr_ready = sem("mr_ready")
        m_ready = sem("m_ready")
        m_loaded = sem("m_loaded")
        st_full = sem("st_full")
        biased = sem("biased")
        exped = sem("exped")
        pv_done = sem("pv_done")
        oT_ready = sem("oT_ready")
        o_ready = sem("o_ready")
        rs_ready = sem("rs_ready")
        cn_ready = sem("cn_ready")
        cn_stored = [sem(f"cn_stored{n}") for n in range(2)]

        NW = 4 + 2 * H
        tab_loaded = sem("tab_loaded")
        w_step = sem("w_step")
        y_step = sem("y_step")
        yrow_ready = sem("yrow_ready")
        now_ready = sem("now_ready")
        y_loaded = sem("y_loaded")
        z_step = sem("z_step")
        z_ready = sem("z_ready")
        th_ready = sem("th_ready")
        g_ready = sem("g_ready")
        g_stored = sem("g_stored")

        NSTACK = 6

        def max_items():
            out = []
            for qt in range(T):
                last = (qt + 1) * P
                near = min(last, 512)
                per = 512 // near
                for h0 in range(0, G, per):
                    out.append(("near", qt, h0, per, last - near, near))
                far = last - near
                if far:
                    per = 512 // far if far <= 256 else 1
                    for h0 in range(0, G, per):
                        out.append(("far", qt, h0, per, 0, far))
            return out

        MAXI = max_items()
        NMAX = len(MAXI)
        PROJ = [("proj", p) for p in range(T // 2)]
        QKT = [("qkT", c) for c in range(2)]
        PIECES = [(kt, h, c, min(S - kt * P, c + 512))
                  for kt in range(T) for h in range(G) for c in range(0, S - kt * P, 512)]
        NP = len(PIECES)
        UPTO = [sum(1 for p in PIECES if p[0] <= kt) for kt in range(T)]
        assert NP % NS == 0
        PV = [(kt, max(kt * P, c), c + 512) for kt in range(T) for c in (0, 512) if kt * P < c + 512]
        NPV = len(PV)
        PV_UPTO = [sum(1 for p in PV if p[0] <= kt) for kt in range(T)]

        OWN = []
        for kt in range(T):
            for h in range(G):
                OWN += [("piece", q, p) for q, p in enumerate(PIECES) if p[:2] == (kt, h)]
                if kt and h in (1, 2):
                    OWN += [("pv", *p) for p in [p for p in PV if p[0] == kt - 1][h - 1:h]]
        MAX_AT = (0, 0, 0, 0, 0, 2, 3, 3, 5, 7, 9, 10, 11, 14, 14, 16, 19, 19, 21, 24, 24, 25, 27, 29,
                  31, 32, 34, 34, 37, 38, 39, 39, 44, 44, 46, 48, 50, 51)
        QKT_AT = (10, 15)
        PROJ_AT = (19, 29, 44, 50)
        MT_AT = 55
        P1_AT = 20
        GATE_AT = 36
        END_AT = (2, 5, 7)
        START = -3
        assert len(MAX_AT) == NMAX

        def plan(u):
            fixed = isinstance(u, int)
            todo = []
            if not fixed or -1 <= u < NU - 1:
                todo += [*zip(MAX_AT, MAXI), (MT_AT, ("mT",))]
            if not fixed or -2 <= u < NU - 2:
                todo += [*zip(QKT_AT, QKT)]
            if not fixed or u < NU - 3:
                todo += [*zip(PROJ_AT, PROJ)]
            if fixed and u < 0:
                split = [("ring", it) for _, it in todo if it in QKT]
                if split:
                    split += [("p1", c) for c in range(2)]
                late = [("ring", it) for _, it in todo if it in MAXI or it == ("mT",)]
                proj = [("ring", it) for _, it in todo if it in PROJ]
                return split + late[:12] + proj + late[12:]
            out = []
            for n in range(len(OWN) + 1):
                here = [("ring", it) for at, it in todo if at == n]
                if n == 0 and (not fixed or u >= 1):
                    ring_here = len(here)
                    for at, step in reversed([*zip(END_AT, ("last", "back", "norm"))]):
                        here.insert(min(at, ring_here), (step,))
                out += here
                if n == P1_AT and any(it in QKT for _, it in todo):
                    out += [("p1", 0), ("p1", 1)]
                if n == GATE_AT:
                    out.append(("gate",))
                out += [("step", *st) for st in OWN[n:n + 1]]
            return [st[1:] if st[0] == "step" else st for st in out]

        plans = {u: plan(u) for u in [*range(START, 1), 1, NU - 3, NU - 2, NU - 1]}

        def plan_of(u):
            return plans[u if isinstance(u, int) and u in plans else 1]

        def ring_of(u):
            return [st[1] for st in plan_of(u) if st[0] == "ring"]

        NI = len(ring_of(1))
        assert NI % NR == 0 and all(len(ring_of(u)) == NI for u in (-1, 0, 1))
        NFILL = sum(len(ring_of(u)) for u in range(START, -1))

        def ring_no(u, r):
            if isinstance(u, int) and u < -1:
                return sum(len(ring_of(w)) for w in range(START, u)) + r
            short = NI - len(ring_of(NU - 3)) if isinstance(u, int) and u == NU - 2 else 0
            return u * NI + (NI + NFILL - short + r)

        def bank_no(u, r):
            return ring_no(u if isinstance(u, int) else 1, r) % NR

        def run(eng, body):
            for u in range(START, NG):
                body(u, u // NG, u % NG)
            with eng.Fori(1, B - 1) as i:
                for j in range(NG):
                    body(i * NG + j, i, j)
            for j in range(NG):
                body(NU - NG + j, B - 1, j)

        def steps(u):
            r = 0
            for st in plan_of(u):
                if st[0] == "ring":
                    st = (*st, r)
                    r += 1
                yield st

        def later(u, n):
            return not isinstance(u, int) or u >= n

        block = ctx.enter_context(nc.Block())

        @block.sync
        def _(sp):
            def load_x(b):
                sp.wait_ge(v_ready, b * NG * (T // 2))
                sp.dma_start(xT[:], xT_dram[bass.ds(b, 1)].rearrange("o p k s -> (o p) k s")
                             ).then_inc(x_loaded, 16)

            def load_stacks(u, j):
                for n, ready in enumerate((p0_ready, p1_ready, p2_ready)):
                    sp.wait_ge(ready, u * 2 + 2)
                    sp.dma_start(part_dram[n], part[n][:]).then_inc(part_stored, 16)
                sp.wait_ge(part_stored, u * 48 + 48)
                half = G * HD * S
                for stack, terms, at in ((qst, QTERM, 0), (kst, KTERM, half)):
                    t = 0
                    while t < NTERM:
                        step = terms[t + 1] - terms[t] if t + 1 < NTERM else 0
                        n = 1
                        while step >= 0 and t + n < NTERM and terms[t + n] - terms[t + n - 1] == step:
                            n += 1
                        src = bass.AP(tensor=part_dram.tensor, offset=terms[t] * 2 * half + at,
                                      ap=[[step * 2 * half, n], [G * S, HD], [1, G * S]])
                        sp.dma_start(stack[t * HD:(t + n) * HD, j % NG].rearrange("p h s -> p (h s)"),
                                     src).then_inc(stack_loaded[j % 2], 16)
                        t += n

            def load_m(u, j):
                sp.wait_ge(m_ready, u * 3 + 3)
                for n in range(3):
                    sp.dma_start(qst[KROWS + n:KROWS + n + 1, j % NG, :, :].rearrange("o h (q i) -> o (h q) i", i=P),
                                 mpart[n][:]).then_inc(m_loaded, 16)

            def store(u, j, b):
                sp.wait_ge(cn_ready, u + 1)
                sp.dma_start(ctx_dram[bass.ds(b * S, S), j * G * HD:(j + 1) * G * HD]
                             .rearrange("(t p) d -> p t d", p=P), cn[:, j % 2]).then_inc(cn_stored[j % 2], 16)

            sp.dma_start(slot[:], slots_dram.rearrange("b p s -> p b s")).then_inc(tab_loaded, 16)
            sp.dma_start(dl[:], dl_dram.rearrange("b p s -> p b s")).then_inc(tab_loaded, 16)

            def body(u, i, j):
                items = ring_of(u)
                if later(u, 1):
                    store(u - 1, (j - 1) % NG, i if j else i - 1)
                if QKT[0] in items:
                    if later(u, -1):
                        sp.wait_ge(stack_loaded[(j + 1) % 2], (i * 2 + (j + 1) // 2 + 1) * 16 * NSTACK)
                    load_stacks(u + 2, (j + 2) % NG)
                if MAXI[0] in items:
                    load_m(u + 1, (j + 1) % NG)
                if j == 0 and not (isinstance(i, int) and i == B - 1):
                    load_x(i + 1)
                if later(u, 0):
                    store_gate(u)

            def store_gate(u):
                sp.wait_ge(g_ready, u + 1)
                sp.dma_start(gate_dram[bass.ds(u * TU * P, TU * P), :].rearrange("(t p) d -> p t d", p=P),
                             z[:]).then_inc(g_stored, 16)

            run(sp, body)
            sp.wait_ge(g_stored, 16 * NU)
            store(NU - 1, NG - 1, B - 1)
            for n in range(2):
                sp.wait_ge(cn_stored[n], 16 * (NU // 2))

        @block.tensor
        def _(pe):
            M = nc.tensor

            def take(u, r):
                k = 0
                if r >= NR:
                    it = ring_of(u)[r - NR]
                elif isinstance(u, int) and u == START:
                    return
                else:
                    prev = ring_of(u - 1) if isinstance(u, int) else ring_of(1)
                    it, k = prev[len(prev) - NR + r], -1
                if it[0] == "proj":
                    pe.wait_ge(v_ready, (u + (3 + k)) * (T // 2) + (it[1] + 1))
                elif it[0] == "qkT":
                    pe.wait_ge(flat_ready, (u + (2 + k)) * 2 + (it[1] + 1))
                elif it[0] == "mT":
                    pe.wait_ge(mr_ready, (u + (1 + k)) + 1)
                else:
                    pe.wait_ge(max_done, (u + (1 + k)) * NMAX + (MAXI.index(it) + 1))

            def proj(i, j, p, bank):
                if p == 0 and j % NG == 0 and later(i + j // NG, 1):
                    pe.wait_ge(x_loaded, (i + j // NG) * 16)
                for t in range(2):
                    for k in range(KD):
                        ins = M.matmul(bank[:, t * 256:t * 256 + 3 * G * HD],
                                       xT[:, k, (2 * p + t) * P:(2 * p + t + 1) * P],
                                       wqkv[:, k, j % NG, :], start=(k == 0), stop=(k == KD - 1))
                ins.then_inc(ring_full, 1)

            def qkT(u, c, bank):
                pe.wait_ge(qk_ready, u * 2 + c + 1)
                for t in range(4):
                    ins = M.transpose(bank[:, t * P:(t + 1) * P], qk[:, 4 * c + t, :], ident[:])
                ins.then_inc(ring_full, 1)

            def maxi(u, i, j, it, bank):
                if it == MAXI[0]:
                    pe.wait_ge(stack_loaded[j % 2], (i * 2 + (j // 2 + 1)) * (16 * NSTACK))
                kind, qt, h0, per, k0, keys = it
                for h in range(h0, h0 + per):
                    c = (h - h0) * keys
                    ins = M.matmul(bank[:, c:c + keys], qst[0:KROWS, j % NG, h, qt * P:(qt + 1) * P],
                                   kst[0:KROWS, j % NG, h, k0:k0 + keys], start=True, stop=True)
                ins.then_inc(ring_full, 1)

            def mT(u, bank):
                pe.wait_ge(mx_ready, u + 1)
                M.transpose(bank[0:G * T, 0:P], mx[:], ident[:]).then_inc(ring_full, 1)

            def piece(u, j, q, kt, h, c, e):
                if isinstance(u, int) and u == 0 and q == 0:
                    pe.wait_ge(kones, 1)
                    pe.wait_ge(vones, 2)
                if q == 0:
                    pe.wait_ge(m_loaded, u * 48 + 48)
                if later(u, 1) or q >= NS:
                    pe.wait_ge(exped, u * NP + q - NS + 1)
                M.matmul(st_ps[q % NS][:, 0:e - c], kst[0:KROWS + MROWS, j, h, kt * P:(kt + 1) * P],
                         qst[0:KROWS + MROWS, j, h, kt * P + c:kt * P + e],
                         start=True, stop=True).then_inc(st_full, 1)

            def pv(u, g, kt, c0, c1):
                pe.wait_ge(exped, u * NP + UPTO[kt])
                if kt == 0 and c0 == 0 and later(u, 1):
                    pe.wait_ge(cn_ready, u)
                for h in range(G):
                    ins = M.matmul(o_ps[32 * h:32 * h + 32, c0:c1], vst[:, g, kt, h, :],
                                   prob[:, (kt * G + h) % PS, c0 - kt * P:c1 - kt * P],
                                   start=(kt == 0), stop=(kt == (3 if c1 == 512 else T - 1)))
                ins.then_inc(pv_done, 1)

            def back(u):
                pe.wait_ge(oT_ready, u + 1)
                for t in range(T):
                    ins = M.transpose(o_ps[:, t * P:(t + 1) * P], oT[:, t * P:(t + 1) * P], ident[:])
                ins.then_inc(o_ready, 1)

            def body(u, i, j):
                for st in steps(u):
                    if st[0] == "piece":
                        piece(u, j, st[1], *st[2])
                    elif st[0] == "pv":
                        pv(u, j, *st[1:])
                    elif st[0] == "last":
                        pv(u - 1, (j - 1) % NG, *PV[-1])
                    elif st[0] == "back":
                        back(u - 1)
                    elif st[0] == "ring":
                        it, r = st[1:]
                        bank = ring[bank_no(u, r)]
                        take(u, r)
                        if it[0] == "proj":
                            proj(i, j + 3, it[1], bank)
                        elif it[0] == "qkT":
                            qkT(u + 2, it[1], bank)
                        elif it[0] == "mT":
                            mT(u + 1, bank)
                        else:
                            maxi(u + 1, i, j + 1, it, bank)

            pe.wait_ge(att["loaded"], 16 * NW)
            run(pe, body)
            pv(NU - 1, NG - 1, *PV[-1])
            back(NU - 1)

        @block.vector
        def _(v):
            V = nc.vector
            V.memset(mp[:], LOWEST).then_inc(mp_set, 1)
            v.wait_ge(mp_set, 1)
            V.memset(kst[KROWS:KROWS + MROWS].rearrange("p a h s -> p (a h s)"), 1.0).then_inc(kones, 1)
            v.wait_ge(tab_loaded, 32)
            V.tensor_copy(yf[:], slot[:]).then_inc(y_step, 1)
            v.wait_ge(y_step, 1)
            for e in range(1, E):
                V.tensor_scalar(yg[:], slot[:], float(e * QCAP), None, ALU.is_ge).then_inc(y_step, 1)
                v.wait_ge(y_step, 2 * e)
                V.scalar_tensor_tensor(out=yf[:], in0=yg[:], scalar=unused[:, e - 1:e], in1=yf[:],
                                       op0=ALU.mult, op1=ALU.subtract, reverse1=True).then_inc(y_step, 1)
                v.wait_ge(y_step, 2 * e + 1)
            for c in range(2):
                V.tensor_copy(yrow[:, :, c, :].rearrange("p (b j) t -> p b j t", b=B),
                              yf[:, :, c * T:(c + 1) * T].rearrange("p b (j t) -> p b j t", t=TU)
                              ).then_inc(yrow_ready, 1)
            v.wait_ge(w_step, 1)
            V.tensor_scalar(w2[:], ex[:], 1.0, None, ALU.add).then_inc(w_step, 1)
            v.wait_ge(w_step, 2)
            V.reciprocal(w2[:], w2[:]).then_inc(w_step, 1)
            v.wait_ge(w_step, 3)
            V.tensor_scalar(w1[:], w2[:], 0.5, None, ALU.mult).then_inc(w_step, 1)
            v.wait_ge(w_step, 4)
            V.tensor_tensor(w2[:], w1[:], ex[:], ALU.mult).then_inc(w_step, 1)
            v.wait_ge(w_step, 5)
            for c, w in enumerate((w1, w2)):
                V.tensor_copy(yw[:, :, c, :].rearrange("p (b j) t -> p b j t", b=B),
                              w[:].rearrange("p b (j t) -> p b j t", t=TU)).then_inc(yrow_ready, 1)
            v.wait_ge(att["loaded"], 16 * NW)

            def maxi(u, j, it, bank):
                kind, qt, h0, per, k0, keys = it
                bank = bank[:, 0:per * keys].rearrange("p (h k) -> p h k", h=per)
                out = mp[:].rearrange("p (h q) n -> p h q n", h=G)[:, h0:h0 + per, qt, :]
                if kind == "near":
                    wn = min(2 * P, keys)
                    if keys > wn:
                        V.tensor_reduce(out[:, :, 1], bank[:, :, 0:keys - wn], AX.X, ALU.max)
                    else:
                        v.sem_inc(passed, 1)
                    for h in range(per):
                        ins = V.tensor_tensor_reduce(
                            out=bank[:, h, keys - wn:keys], in0=bank[:, h, keys - wn:keys],
                            in1=biasT[:, (j % NG) * G + h0 + h, 2 * P - wn:2 * P],
                            scale=1.0, scalar=LOWEST, op0=ALU.add, op1=ALU.max,
                            accum_out=out[:, h, 0:1])
                else:
                    ins = V.tensor_reduce(out[:, :, 2], bank, AX.X, ALU.max)
                ins.then_inc(max_done, 1)
                if it == MAXI[-1]:
                    v.wait_ge(max_done, u * NMAX + NMAX)
                    V.tensor_reduce(mx[:], mp[:], AX.X, ALU.max).then_inc(mx_ready, 1)

            def mT(u, bank):
                if later(u, 1):
                    v.wait_ge(m_loaded, u * 48)
                src = bank[0:G * T, 0:P]
                V.tensor_scalar(mpart[0][:], src, -1.0, None, ALU.mult).then_inc(m_ready, 1)
                v.wait_ge(m_ready, u * 3 + 1)
                V.scalar_tensor_tensor(out=mr[:], in0=src, scalar=-1.0, in1=mpart[0][:], op0=ALU.mult,
                                       op1=ALU.subtract).then_inc(mr_ready, 1)
                v.wait_ge(mr_ready, u + 1)
                V.tensor_copy(mpart[1][:], mr[:]).then_inc(m_ready, 1)
                v.wait_ge(m_ready, u * 3 + 2)
                V.tensor_tensor(mpart[2][:], mr[:], mpart[1][:], ALU.subtract).then_inc(m_ready, 1)

            def add_bias(u, j, q, kt, h):
                v.wait_ge(st_full, u * NP + q + 1)
                w = min(2 * P, S - kt * P)
                V.tensor_tensor(st_ps[q % NS][:, 0:w], st_ps[q % NS][:, 0:w],
                                bias[:, j * G + h, 0:w], ALU.add).then_inc(biased, 1)

            def norm(u, i, jj):
                j = jj % NG
                v.wait_ge(o_ready, u + 1)
                heads = o_ps.rearrange("p (h z) -> p h z", z=2 * HD)
                V.reciprocal(rs[:], heads[:, :, HD]).then_inc(rs_ready, 1)
                v.wait_ge(rs_ready, u + 1)
                if later(u, 2):
                    v.wait_ge(cn_stored[j % 2], (i * 2 + jj // 2) * 16)
                V.tensor_tensor(cn[:, j % 2].rearrange("p t (h z) -> p (t h) z", z=HD), heads[:, :, 0:HD],
                                rs[:].unsqueeze(2).to_broadcast([P, T * G, HD]), ALU.mult).then_inc(cn_ready, 1)

            def body(u, i, j):
                for st in steps(u):
                    if st[0] == "piece" and st[2][2] == 0:
                        add_bias(u, j, st[1], *st[2][:2])
                    elif st[0] == "norm":
                        norm(u - 1, i, j - 1)
                    elif st[0] == "ring" and st[1][0] not in ("proj", "qkT"):
                        it, r = st[1:]
                        v.wait_ge(ring_full, ring_no(u, r) + 1)
                        if it[0] == "mT":
                            mT(u + 1, ring[bank_no(u, r)])
                        else:
                            maxi(u + 1, j + 1, it, ring[bank_no(u, r)])

            run(v, body)
            norm(NU - 1, B - 1, NG - 1)

        @block.scalar
        def _(act):
            def proj(u, j, p, bank):
                src = bank.rearrange("p (t c) -> p t c", t=2)
                w = 2 * G * HD
                at = slice(2 * p, 2 * p + 2)
                nc.scalar.copy(qkf[:, at, :], src[:, :, 0:w]).then_inc(qkf_ready, 1)
                nc.scalar.copy(vst[:, j % NG, at, :, 0:HD],
                               src[:, :, w:w + G * HD].rearrange("p t (h z) -> p t h z", z=HD)).then_inc(v_ready, 1)

            def qkT(u, c, bank):
                at = slice(c * 512, (c + 1) * 512)
                if later(u, 1) and c == 0:
                    act.wait_ge(part_stored, u * 48)
                nc.scalar.copy(part[0][:, at], bank).then_inc(p0_ready, 1)
                nc.scalar.copy(rest[:, at], bank).then_inc(flat_ready, 1)

            def second(u, c):
                act.wait_ge(rest_ready, u * 2 + c + 1)
                nc.scalar.copy(part[1][:, c * 512:(c + 1) * 512],
                               rest[:, c * 512:(c + 1) * 512]).then_inc(p1_ready, 1)

            def piece(u, q, kt, h, c, e):
                if h == 0 and c == 0 and (later(u, 1) or kt >= 2):
                    act.wait_ge(pv_done, u * NPV + (PV_UPTO[kt - 2] if kt >= 2 else kt - 1))
                if c == 0:
                    act.wait_ge(biased, u * (T * G) + (kt * G + h + 1))
                else:
                    act.wait_ge(st_full, u * NP + q + 1)
                nc.scalar.activation(prob[:, (kt * G + h) % PS, c:e], st_ps[q % NS][:, 0:e - c],
                                     ACT.Exp).then_inc(exped, 1)

            def tanh(u):
                act.wait_ge(z_ready, u + 1)
                nc.scalar.activation(y[:, 0], z[:], ACT.Tanh, scale=0.5).then_inc(th_ready, 1)

            def copy_o(u):
                act.wait_ge(pv_done, u * NPV + NPV)
                nc.scalar.copy(oT[:], o_ps).then_inc(oT_ready, 1)

            def body(u, i, j):
                for st in steps(u):
                    if st[0] == "piece":
                        piece(u, st[1], *st[2])
                    elif st[0] == "gate":
                        tanh(u)
                    elif st[0] == "last":
                        copy_o(u - 1)
                    elif st[0] == "p1":
                        second(u + 2, st[1])
                    elif st[0] == "ring" and st[1][0] in ("proj", "qkT"):
                        it, r = st[1:]
                        act.wait_ge(ring_full, ring_no(u, r) + 1)
                        if it[0] == "proj":
                            proj(u + 3, j + 3, it[1], ring[bank_no(u, r)])
                        else:
                            qkT(u + 2, it[1], ring[bank_no(u, r)])

            act.wait_ge(tab_loaded, 32)
            nc.scalar.activation(ex[:], dl[:], ACT.Exp).then_inc(w_step, 1)
            run(act, body)
            copy_o(NU - 1)

        @block.gpsimd
        def _(pool):
            nc.gpsimd.memset(vst[:, :, :, :, HD + 1:2 * HD], 0.0).then_inc(vones, 1)
            nc.gpsimd.memset(vst[:, :, :, :, HD:HD + 1], 1.0).then_inc(vones, 1)
            pool.wait_ge(att["loaded"], 16 * NW)

            def rope(u):
                wh = G * HD // 2

                def halves(a):
                    return a.rearrange("p t (a z) -> p t a z", a=2)

                for c in range(2):
                    at = slice(4 * c, 4 * c + 4)
                    pool.wait_ge(qkf_ready, u * 4 + (2 * c + 2))
                    if later(u, 1) or c:
                        pool.wait_ge(qk_ready, u * 2 + c)
                    nc.gpsimd.tensor_tensor(ra[:], qkf[:, at, :], cos[:, at, :], ALU.mult).then_inc(rope_step, 1)
                    for o in range(2):
                        to, of = slice(o * wh, (o + 1) * wh), slice((1 - o) * wh, (2 - o) * wh)
                        nc.gpsimd.tensor_tensor(halves(rb[:])[:, :, :, to], halves(qkf[:, at, :])[:, :, :, of],
                                                halves(sin[:, at, :])[:, :, :, to], ALU.mult).then_inc(rope_step, 1)
                    pool.wait_ge(rope_step, u * 6 + (3 * c + 3))
                    nc.gpsimd.tensor_tensor(qk[:, at, :], ra[:], rb[:], ALU.add).then_inc(qk_ready, 1)

            def split(u):
                for c in range(2):
                    at = slice(c * 512, (c + 1) * 512)
                    pool.wait_ge(flat_ready, u * 2 + (c + 1))
                    nc.gpsimd.tensor_tensor(rest[:, at], rest[:, at], part[0][:, at],
                                            ALU.subtract).then_inc(rest_ready, 1)
                for c in range(2):
                    at = slice(c * 512, (c + 1) * 512)
                    pool.wait_ge(p1_ready, u * 2 + (c + 1))
                    nc.gpsimd.tensor_tensor(part[2][:, at], rest[:, at], part[1][:, at],
                                            ALU.subtract).then_inc(p2_ready, 1)

            def gather(u):
                if later(u, 1):
                    pool.wait_ge(g_ready, u)
                nc.gpsimd.tensor_copy(row_now[:], yrow[:, bass.ds(u, 1)].rearrange("p o c t -> p (o c) t")
                                      ).then_inc(now_ready, 1)
                nc.gpsimd.tensor_copy(w_now[:], yw[:, bass.ds(u, 1)].rearrange("p o c t -> p (o c) t")
                                      ).then_inc(now_ready, 1)
                pool.wait_ge(now_ready, u * 2 + 2)
                pool.sem_inc(passed, 1)
                for c in range(2):
                    for t in range(TU):
                        nc.gpsimd.indirect_dma_start(
                            y[:, c, t, :], None, ys[:, :],
                            bass.IndirectOffsetOnAxis(ap=row_now[:, c, t:t + 1], axis=0)
                        ).then_inc(y_loaded, 16)

            def gate(u, half):
                if half == 0:
                    pool.wait_ge(y_loaded, u * (16 * 2 * TU) + 16 * 2 * TU)
                    nc.gpsimd.tensor_tensor(y[:].rearrange("p c t d -> p (c t) d"), y[:].rearrange("p c t d -> p (c t) d"),
                                            w_now[:].rearrange("p c t -> p (c t)").unsqueeze(2)
                                            .to_broadcast([P, 2 * TU, D]), ALU.mult).then_inc(z_step, 1)
                    pool.wait_ge(z_step, u * 2 + 1)
                    if later(u, 1):
                        pool.wait_ge(g_stored, u * 16)
                    nc.gpsimd.tensor_tensor(z[:], y[:, 0], y[:, 1], ALU.add).then_inc(z_ready, 1)
                else:
                    pool.wait_ge(th_ready, u + 1)
                    nc.gpsimd.tensor_tensor(y[:, 1], y[:, 0], z[:], ALU.mult).then_inc(z_step, 1)
                    pool.wait_ge(z_step, u * 2 + 2)
                    nc.gpsimd.tensor_tensor(z[:], z[:], y[:, 1], ALU.add).then_inc(g_ready, 1)

            def body(u):
                gather(u)
                if not (isinstance(u, int) and u + 2 >= NU):
                    split(u + 2)
                gate(u, 0)
                gate(u, 1)
                if not (isinstance(u, int) and u + 3 >= NU):
                    rope(u + 3)

            rope(0)
            for u in range(2):
                split(u)
                rope(u + 1)
            pool.wait_ge(yrow_ready, 4)
            body(0)
            with pool.Fori(1, NU - 3) as u:
                body(u)
            for u in range(NU - 3, NU):
                body(u)


def phase_d(nc, x, cst, ident, ctx_dram, gate_dram, out):
    NBUF, TG = 4, 4
    NQ = NT // (NBUF * TG)
    with ExitStack() as ctx:
        def sb(name, shape, dt=F32):
            return ctx.enter_context(nc.sbuf_tensor("d_" + name, shape, dt))

        def sem(name):
            return ctx.enter_context(nc.semaphore("d_" + name))

        ps = ctx.enter_context(nc.psum_tensor("d_ps", [P, 4, 512], F32))
        wo = sb("wo", [P, KD, D])
        cx = sb("cx", [P, NBUF, TG, D])
        xr = sb("xr", [P, NBUF, TG, D])
        g2 = sb("g2", [P, NBUF, TG, D])
        cT = sb("cT", [P, 2, D])
        fd = sb("fd", [P, 2, D])
        ob = sb("ob", [P, NBUF, TG, D])

        cst_loaded = sem("cst_loaded")
        c_loaded = [sem(f"c_loaded{n}") for n in range(NBUF)]
        cT_psum = sem("cT_psum")
        cT_ready = sem("cT_ready")
        s_psum = sem("s_psum")
        fd_ready = sem("fd_ready")
        o_ready = sem("o_ready")
        o_stored = [sem(f"o_stored{n}") for n in range(NBUF)]
        block = ctx.enter_context(nc.Block())

        def later(i, n):
            return not isinstance(i, int) or i >= n

        def tiles(eng, body):
            for j in range(NBUF):
                for t in range(TG):
                    body(0, j, t)
            with eng.Fori(1, NQ - 1) as i:
                for j in range(NBUF):
                    for t in range(TG):
                        body(i, j, t)
            for j in range(NBUF):
                for t in range(TG):
                    body(NQ - 1, j, t)

        @block.sync
        def _(sp):
            R = TG * P

            def load(i, j):
                rows = bass.ds((i * NBUF + j) * R, R)
                for dst, src in ((cx, ctx_dram), (g2, gate_dram), (xr, x)):
                    sp.dma_start(dst[:, j], src[rows, :].rearrange("(t p) d -> p t d", p=P)).then_inc(c_loaded[j], 16)

            def store(i, j):
                sp.wait_ge(o_ready, (i * NBUF + j) * TG + TG)
                sp.dma_start(out[bass.ds((i * NBUF + j) * R, R), :].rearrange("(t p) d -> p t d", p=P),
                             ob[:, j]).then_inc(o_stored[j], 16)

            load(0, 0)
            sp.dma_start(wo[:], cst["wo"]).then_inc(cst_loaded, 16)
            for j in range(1, NBUF):
                load(0, j)
            with sp.Fori(0, NQ - 1) as i:
                for j in range(NBUF):
                    store(i, j)
                    load(i + 1, j)
            for j in range(NBUF):
                store(NQ - 1, j)
            for j in range(NBUF):
                sp.wait_ge(o_stored[j], 16 * NQ)

        @block.tensor
        def _(pe):
            M = nc.tensor
            pe.wait_ge(cst_loaded, 16)

            def transpose(i, j, t):
                n = (i * NBUF + j) * TG + t
                if t == 0:
                    pe.wait_ge(c_loaded[j % NBUF], i * 48 + (48 if j < NBUF else 96))
                if later(i, 1) or j or t >= 2:
                    pe.wait_ge(cT_ready, n - 1)
                for k in range(KD):
                    ins = M.transpose(ps[:, t % 2, k * P:(k + 1) * P], cx[:, j % NBUF, t, k * P:(k + 1) * P], ident[:])
                ins.then_inc(cT_psum, 1)

            def project(i, j, t):
                n = (i * NBUF + j) * TG + t
                pe.wait_ge(cT_ready, n + 1)
                if later(i, 1) or j or t >= 2:
                    pe.wait_ge(fd_ready, n - 1)
                for k in range(KD):
                    ins = M.matmul(ps[:, 2 + t % 2, 0:D], cT[:, t % 2, k * P:(k + 1) * P], wo[:, k, :],
                                   start=(k == 0), stop=(k == KD - 1))
                ins.then_inc(s_psum, 1)

            def body(i, j, t):
                if not (isinstance(i, int) and i == NQ - 1 and j == NBUF - 1 and t == TG - 1):
                    transpose(i, *((j, t + 1) if t < TG - 1 else (j + 1, 0)))
                project(i, j, t)

            transpose(0, 0, 0)
            tiles(pe, body)

        @block.scalar
        def _(act):
            def body(i, j, t):
                n = (i * NBUF + j) * TG + t
                act.wait_ge(cT_psum, n + 1)
                if later(i, 1) or j or t >= 2:
                    act.wait_ge(s_psum, n - 1)
                nc.scalar.copy(cT[:, t % 2, :], ps[:, t % 2, 0:D]).then_inc(cT_ready, 1)

            tiles(act, body)

        @block.vector
        def _(v):
            V = nc.vector

            def body(i, j, t):
                n = (i * NBUF + j) * TG + t
                if t == 0:
                    v.wait_ge(c_loaded[j], i * 48 + 48)
                v.wait_ge(s_psum, n + 1)
                if later(i, 1) or j or t >= 2:
                    v.wait_ge(o_ready, n - 1)
                V.tensor_tensor(fd[:, t % 2, :], ps[:, 2 + t % 2, 0:D], g2[:, j, t, :],
                                ALU.mult).then_inc(fd_ready, 1)
                v.wait_ge(fd_ready, n + 1)
                if t == 0 and later(i, 1):
                    v.wait_ge(o_stored[j], i * 16)
                V.scalar_tensor_tensor(out=ob[:, j, t, :], in0=fd[:, t % 2, :], scalar=0.5,
                                       in1=xr[:, j, t, :], op0=ALU.mult, op1=ALU.add).then_inc(o_ready, 1)

            tiles(v, body)


def build(nc, x, cst, out):
    xs = nc.dram_tensor("queue_x", [NROW, D], F32, kind="Internal").ap()
    ys = nc.dram_tensor("tiles_y", [NX * P, D], F32, kind="Internal").ap()
    xT_dram = nc.dram_tensor("xT", [B, P, KD, S], F32, kind="Internal").ap()
    slots_dram = nc.dram_tensor("slots", [B, P, 2 * T], U32, kind="Internal").ap()
    dl_dram = nc.dram_tensor("logit_diff", [B, P, T], F32, kind="Internal").ap()
    fvec_dram = nc.dram_tensor("bias_by_distance", [2 * H, NREL], F32, kind="Internal").ap()
    frow_dram = nc.dram_tensor("bias_rows", [2 * H, P, NREL], F32, kind="Internal").ap()
    part_dram = nc.dram_tensor("parts", [3, P, S], BF16, kind="Internal").ap()
    gate_dram = nc.dram_tensor("gate", [B * S, D], F32, kind="Internal").ap()
    ctx_dram = nc.dram_tensor("context", [B * S, D], F32, kind="Internal").ap()
    with ExitStack() as ctx:
        tab = ctx.enter_context(nc.sbuf_tensor("tile_table", [1, 2, NX], I32))
        unused = ctx.enter_context(nc.sbuf_tensor("unused", [P, E], F32))
        with ExitStack() as to_c:
            att = ahead(nc, to_c, "att_", {
                "ident": [P, P],
                "wqkv": [P, KD, NG, 3 * G * HD],
                "cos": [P, T, 2 * G * HD],
                "sin": [P, T, 2 * G * HD],
                "bias": [P, 2 * H, 2 * P],
                "xT": [P, KD, S],
            })
            with ExitStack() as to_b:
                ffn = ahead(nc, to_b, "ffn_", {"wgu": [P, E, KD, 2 * F], "wd": [P, E, KD, D]})
                phase_a(nc, x, cst, ffn, att, xs, xT_dram, slots_dram, dl_dram, fvec_dram, frow_dram, tab, unused)
                phase_b(nc, cst, ffn, att, frow_dram, xT_dram, xs, ys, tab)
            phase_c(nc, att, xT_dram, part_dram, ctx_dram, slots_dram, dl_dram, unused, ys, gate_dram)
            phase_d(nc, x, cst, att["ident"], ctx_dram, gate_dram, out)


def shape_constants():
    import math

    import numpy as np

    f32 = np.float32
    inv = (f32(1.0) / np.power(f32(10000.0), np.arange(0, HD, 2, dtype=f32) / f32(HD))).astype(f32)
    ang = np.outer(np.arange(S, dtype=f32), inv).astype(f32)
    cos, sin = np.cos(ang), np.sin(ang)
    c16 = np.concatenate([cos, cos], 1)
    s16 = np.concatenate([-sin, sin], 1)
    scale = f32(1.0 / math.sqrt(HD))

    def rope_table(t):
        q = np.repeat(t * scale, G, axis=1)
        k = np.repeat(t, G, axis=1)
        return np.ascontiguousarray(np.concatenate([q, k], 1).reshape(T, P, 2 * G * HD).transpose(1, 0, 2)).astype(f32)

    dist = np.arange(NREL) - (P - 1)
    rp = np.maximum(dist, 0)
    exact = NBUCKET // 2
    large = exact + (np.log(np.maximum(rp.astype(f32), f32(1.0)) / f32(exact)) / f32(math.log(128 / exact))
                     * f32(NBUCKET - exact)).astype(np.int32)
    bucket = np.where(rp < exact, rp, np.minimum(large, NBUCKET - 1))
    fone = np.zeros((NBUCKET + 1, NREL), f32)
    seen = dist >= 0
    fone[bucket[seen], np.nonzero(seen)[0]] += 1.0
    fone[NBUCKET - 1, seen] -= 1.0
    fone[NBUCKET, ~seen] = -BIG
    back = 2 * P - 1 - np.arange(NREL) + (P - 1)
    fone = np.stack([fone, fone[:, np.maximum(back, 0)]], 1)
    e = np.arange(E, dtype=f32)
    return {
        "ident": np.eye(P, dtype=f32),
        "lower": np.triu(np.ones((P, P), f32), 1),
        "rev": np.ascontiguousarray(np.broadcast_to(E - e, (P, T, E))).astype(f32),
        "eoff": np.ascontiguousarray(np.broadcast_to(e * QCAP, (P, T, E))).astype(f32),
        "fone": fone,
        "cos": rope_table(c16),
        "sin": rope_table(s16),
    }


def kernel(L0_attn_x, L0_attn_Wq, L0_attn_Wk, L0_attn_Wv, L0_attn_Wo, L0_attn_rel_emb,
           L0_ffn_router_weight, L0_ffn_gate_up_proj, L0_ffn_down_proj):
    import numpy as np
    import concourse.bacc as bacc
    from concourse.bass_utils import run_bass_kernel_spmd

    def rows(w):
        return np.ascontiguousarray(np.asarray(w).reshape(KD, P, -1).transpose(1, 0, 2))

    wq, wk = (np.asarray(w).reshape(D, NG, G, HD).transpose(0, 1, 3, 2).reshape(D, NG, G * HD)
              for w in (L0_attn_Wq, L0_attn_Wk))
    wv = np.asarray(L0_attn_Wv).reshape(D, NG, G * HD)
    qkv = np.concatenate([wq, wk, wv], 2)
    gu = np.asarray(L0_ffn_gate_up_proj).transpose(2, 0, 1).reshape(KD, P, E, 2 * F).transpose(1, 2, 0, 3)
    dn = np.asarray(L0_ffn_down_proj).transpose(2, 0, 1).reshape(KD, P, E, D).transpose(1, 2, 0, 3)
    data = {
        "x": np.ascontiguousarray(np.asarray(L0_attn_x).reshape(B * S, D)),
        "wqkv": np.ascontiguousarray(qkv.reshape(KD, P, NG, 3 * G * HD).transpose(1, 0, 2, 3)),
        "wo": rows(L0_attn_Wo),
        "wr": rows(np.asarray(L0_ffn_router_weight).T),
        "rel": np.ascontiguousarray(np.asarray(L0_attn_rel_emb)),
        "wgu": np.ascontiguousarray(gu),
        "wd": np.ascontiguousarray(dn),
    }
    data.update(shape_constants())

    nc = bacc.Bacc("TRN2", target_bir_lowering=False, num_devices=1)
    aps = {n: nc.dram_tensor("in_" + n, a.shape, mybir.dt.from_np(a.dtype), kind="ExternalInput").ap()
           for n, a in data.items()}
    out = nc.dram_tensor("out", [B * S, D], F32, kind="ExternalOutput").ap()
    build(nc, aps["x"], aps, out)
    res = run_bass_kernel_spmd(nc, [{"in_" + n: a for n, a in data.items()}], core_ids=[0])
    return res.results[0]["out"].reshape(B, S, D)
```
